# Optimizing a Trainium2 kernel written in Bass

```python
import numpy as np
import jax
import jax.numpy as jnp

def _softmax(x, axis=-1):
    return jax.nn.softmax(x, axis=axis)

def _gelu(x):
    return jax.nn.gelu(x, approximate=True)

def _silu(x):
    return jax.nn.silu(x)

def _sigmoid(x):
    return jax.nn.sigmoid(x)

def _layernorm(x, axis=-1, eps=1e-05):
    m = jnp.mean(x, axis=axis, keepdims=True)
    v = jnp.var(x, axis=axis, keepdims=True)
    return (x - m) / jnp.sqrt(v + eps)

def _scatter_add(tgt, idx, src, axis=0):
    return tgt.at[idx].add(src)

def _segment_sum(src, seg, n):
    return jax.ops.segment_sum(src, seg, n)
kernel_name = 'mk_gnn_ffn_d1_gnn_r8_93006f'

def setup_inputs(seed: int=0):
    np.random.seed(seed)
    _w = jnp.asarray

    def _rec_inputs():
        import jax
        import jax.numpy as jnp
        _gk = jax.random.key(seed)
        x = -0.0003713 + 1 * jax.random.normal(jax.random.fold_in(_gk, 1), (6250, 256), jnp.float32)
        _s = jax.random.randint(jax.random.fold_in(_gk, 2), (100000,), 0, 6250, jnp.int32)
        _d = jax.random.randint(jax.random.fold_in(_gk, 3), (100000,), 0, 6250, jnp.int32)
        _loop = jnp.arange(6250, dtype=jnp.int32)
        src = jnp.concatenate([_s, _d, _loop])
        dst = jnp.concatenate([_d, _s, _loop])
        _o = jnp.argsort(dst, stable=True)
        src = src[_o]
        dst = dst[_o]
        return (x, src, dst)
    x, src, dst = _rec_inputs()

    def _L0_gnn_setup():
        import jax, jax.numpy as jnp
        import numpy as np
        N = 6250
        E = 100000
        IN = 256
        H = 8
        C = 32
        NEG_SLOPE = 0.2
        LN_EPS = 1e-05

        def _gat_block(x, edge_index, W, att_src, att_dst, bias, ln_scale, ln_bias):
            src, dst = (edge_index[0], edge_index[1])
            h = (x @ W).reshape(N, H, C)
            a_src = jnp.einsum('nhc,hc->nh', h, att_src)
            a_dst = jnp.einsum('nhc,hc->nh', h, att_dst)
            alpha = jax.nn.leaky_relu(a_src[src] + a_dst[dst], NEG_SLOPE)
            amax = jax.ops.segment_max(alpha, dst, num_segments=N)
            amax = jnp.where(jnp.isfinite(amax), amax, 0.0)
            ex = jnp.exp(alpha - amax[dst])
            denom = jax.ops.segment_sum(ex, dst, num_segments=N)
            attn = ex / (denom[dst] + 1e-16)
            msg = h[src] * attn[:, :, None]
            out = jax.ops.segment_sum(msg, dst, num_segments=N)
            out = out.reshape(N, H * C) + bias
            out = out + x
            out = jax.nn.elu(out)
            mu = jnp.mean(out, axis=-1, keepdims=True)
            var = jnp.var(out, axis=-1, keepdims=True)
            return (out - mu) * jax.lax.rsqrt(var + LN_EPS) * ln_scale + ln_bias
        key = jax.random.key(seed)
        ks = jax.random.split(key, 8)
        x = jax.random.normal(ks[0], (N, IN), dtype=jnp.float32)
        edge_index = jax.random.randint(ks[1], (2, E), 0, N, dtype=jnp.int64)
        W = jax.random.normal(ks[2], (IN, H * C), dtype=jnp.float32) / np.sqrt(IN)
        att_src = jax.random.normal(ks[3], (H, C), dtype=jnp.float32) / np.sqrt(C)
        att_dst = jax.random.normal(ks[4], (H, C), dtype=jnp.float32) / np.sqrt(C)
        bias = jnp.zeros((H * C,), dtype=jnp.float32)
        ln_scale = jnp.ones((H * C,), dtype=jnp.float32)
        ln_bias = jnp.zeros((H * C,), dtype=jnp.float32)
        return {'x': x, 'edge_index': edge_index, 'W': W, 'att_src': att_src, 'att_dst': att_dst, 'bias': bias, 'ln_scale': ln_scale, 'ln_bias': ln_bias}
    _L0_gnn_all = _L0_gnn_setup()
    _L0_gnn_in = {k: v for k, v in _L0_gnn_all.items() if k in ('W', 'att_src', 'att_dst', 'bias', 'ln_scale', 'ln_bias')}
    del _L0_gnn_all

    def _L0_ffn_setup():
        import jax, jax.numpy as jnp
        import numpy as np
        E, D, H, TOP_K = (6, 256, 256, 2)
        ROUTER_H = D // 2
        key = jax.random.key(seed)
        ks = jax.random.split(key, 12)
        s = 1.0 / np.sqrt(D)
        sh = 1.0 / np.sqrt(H)
        sr = 1.0 / np.sqrt(ROUTER_H)
        return {'features': jax.random.normal(ks[0], (8, 512, D), dtype=jnp.float32), 'router_w1': jax.random.uniform(ks[1], (D, ROUTER_H), jnp.float32, -s, s), 'router_b1': jnp.zeros((ROUTER_H,), jnp.float32), 'router_w2': jax.random.uniform(ks[2], (ROUTER_H, E), jnp.float32, -sr, sr), 'router_b2': jnp.zeros((E,), jnp.float32), 'expert_w1': jax.random.uniform(ks[3], (E, D, H), jnp.float32, -s, s), 'expert_b1': jnp.zeros((E, H), jnp.float32), 'expert_w2': jax.random.uniform(ks[4], (E, H, H), jnp.float32, -sh, sh), 'expert_b2': jnp.zeros((E, H), jnp.float32), 'expert_w3': jax.random.uniform(ks[5], (E, H, D), jnp.float32, -sh, sh), 'expert_b3': jnp.zeros((E, D), jnp.float32)}
    _L0_ffn_all = _L0_ffn_setup()
    _L0_ffn_in = {k: v for k, v in _L0_ffn_all.items() if k in ('router_w1', 'router_b1', 'router_w2', 'router_b2', 'expert_w1', 'expert_b1', 'expert_w2', 'expert_b2', 'expert_w3', 'expert_b3')}
    del _L0_ffn_all
    return {'x': x, 'src': src, 'dst': dst, 'L0_gnn_W': _L0_gnn_in['W'], 'L0_gnn_att_src': _L0_gnn_in['att_src'], 'L0_gnn_att_dst': _L0_gnn_in['att_dst'], 'L0_gnn_bias': _L0_gnn_in['bias'], 'L0_gnn_ln_scale': _L0_gnn_in['ln_scale'], 'L0_gnn_ln_bias': _L0_gnn_in['ln_bias'], 'L0_ffn_router_w1': _L0_ffn_in['router_w1'], 'L0_ffn_router_b1': _L0_ffn_in['router_b1'], 'L0_ffn_router_w2': _L0_ffn_in['router_w2'], 'L0_ffn_router_b2': _L0_ffn_in['router_b2'], 'L0_ffn_expert_w1': _L0_ffn_in['expert_w1'], 'L0_ffn_expert_b1': _L0_ffn_in['expert_b1'], 'L0_ffn_expert_w2': _L0_ffn_in['expert_w2'], 'L0_ffn_expert_b2': _L0_ffn_in['expert_b2'], 'L0_ffn_expert_w3': _L0_ffn_in['expert_w3'], 'L0_ffn_expert_b3': _L0_ffn_in['expert_b3']}

def reference(x, src, dst, L0_gnn_W, L0_gnn_att_src, L0_gnn_att_dst, L0_gnn_bias, L0_gnn_ln_scale, L0_gnn_ln_bias, L0_ffn_router_w1, L0_ffn_router_b1, L0_ffn_router_w2, L0_ffn_router_b2, L0_ffn_expert_w1, L0_ffn_expert_b1, L0_ffn_expert_w2, L0_ffn_expert_b2, L0_ffn_expert_w3, L0_ffn_expert_b3):
    import jax
    import jax.numpy as jnp

    def _L0_gnn_ref(x, edge_index, W, att_src, att_dst, bias, ln_scale, ln_bias):
        import jax, jax.numpy as jnp
        import numpy as np
        N = 6250
        E = 100000
        IN = 256
        H = 8
        C = 32
        NEG_SLOPE = 0.2
        LN_EPS = 1e-05

        def _gat_block(x, edge_index, W, att_src, att_dst, bias, ln_scale, ln_bias):
            src, dst = (edge_index[0], edge_index[1])
            h = (x @ W).reshape(N, H, C)
            a_src = jnp.einsum('nhc,hc->nh', h, att_src)
            a_dst = jnp.einsum('nhc,hc->nh', h, att_dst)
            alpha = jax.nn.leaky_relu(a_src[src] + a_dst[dst], NEG_SLOPE)
            amax = jax.ops.segment_max(alpha, dst, num_segments=N)
            amax = jnp.where(jnp.isfinite(amax), amax, 0.0)
            ex = jnp.exp(alpha - amax[dst])
            denom = jax.ops.segment_sum(ex, dst, num_segments=N)
            attn = ex / (denom[dst] + 1e-16)
            msg = h[src] * attn[:, :, None]
            out = jax.ops.segment_sum(msg, dst, num_segments=N)
            out = out.reshape(N, H * C) + bias
            out = out + x
            out = jax.nn.elu(out)
            mu = jnp.mean(out, axis=-1, keepdims=True)
            var = jnp.var(out, axis=-1, keepdims=True)
            return (out - mu) * jax.lax.rsqrt(var + LN_EPS) * ln_scale + ln_bias
        return _gat_block(x, edge_index, W, att_src, att_dst, bias, ln_scale, ln_bias)

    def _L0_ffn_ref(features, router_w1, router_b1, router_w2, router_b2, expert_w1, expert_b1, expert_w2, expert_b2, expert_w3, expert_b3):
        import jax, jax.numpy as jnp
        import numpy as np
        E, D, H, TOP_K = (6, 256, 256, 2)
        ROUTER_H = D // 2
        rh = jax.nn.relu(features @ router_w1 + router_b1)
        expert_logits = jax.nn.softmax(rh @ router_w2 + router_b2, axis=-1)
        top_w, top_i = jax.lax.top_k(expert_logits, TOP_K)
        routing_weights = jax.nn.softmax(top_w, axis=-1)
        h1 = jax.nn.relu(jnp.einsum('bsd,edh->bseh', features, expert_w1) + expert_b1)
        h2 = jax.nn.relu(jnp.einsum('bseh,ehf->bsef', h1, expert_w2) + expert_b2)
        expert_out = jnp.einsum('bsef,efo->bseo', h2, expert_w3) + expert_b3
        sel = jnp.take_along_axis(expert_out, top_i[:, :, :, None], axis=2)
        combined = jnp.sum(sel * routing_weights[..., None], axis=2)
        return combined
    edge_index = jnp.stack([src, dst])
    x = x + _L0_gnn_ref(_layernorm(x, axis=-1), edge_index, L0_gnn_W, L0_gnn_att_src, L0_gnn_att_dst, L0_gnn_bias, L0_gnn_ln_scale, L0_gnn_ln_bias)
    x = x + _L0_ffn_ref(_layernorm(x, axis=-1)[None], L0_ffn_router_w1, L0_ffn_router_b1, L0_ffn_router_w2, L0_ffn_router_b2, L0_ffn_expert_w1, L0_ffn_expert_b1, L0_ffn_expert_w2, L0_ffn_expert_b2, L0_ffn_expert_w3, L0_ffn_expert_b3)[0]
    return x

_drawn_inputs = setup_inputs


def setup_inputs(seed=0):
    import zlib

    import numpy as np

    out = dict(_drawn_inputs(seed))
    spreads = {'L0_gnn_bias': (0.0, 0.1),
     'L0_gnn_ln_scale': (1.0, 0.2),
     'L0_gnn_ln_bias': (0.0, 0.1),
     'L0_ffn_router_b1': (0.0, 0.426),
     'L0_ffn_router_b2': (0.0, 0.269),
     'L0_ffn_expert_b1': (0.0, 0.8),
     'L0_ffn_expert_b2': (0.0, 0.566),
     'L0_ffn_expert_b3': (0.0, 0.1)}
    factors = {}
    for name, (base, spread) in spreads.items():
        noise = np.random.default_rng([zlib.crc32(name.encode()), seed]).standard_normal(out[name].shape)
        drawn = base * np.exp(spread * noise) if base else spread * noise
        out[name] = jnp.asarray(drawn.astype(out[name].dtype))
    for name, factor in factors.items():
        out[name] = (out[name] * factor).astype(out[name].dtype)
    return out
```

```python
from contextlib import ExitStack

import concourse.bass as bass
from concourse import mybir

ALU = mybir.AluOpType
ACT = mybir.ActivationFunctionType
AX = mybir.AxisListType
F32 = mybir.dt.float32
I32 = mybir.dt.int32
U32 = mybir.dt.uint32

P = 128
N = 6250
NE = 206250
D = 256
H = 8
C = D // H
HC = C + 1
ROW = H * HC
NW = -(-N // P)
NPAD = NW * P
EPP = -(-NE // P)
IT = 4
IE = IT * P
GI = 4
GT = GI * IT
NG_MIN = -(-(NE // IE + NW) // GI)
TRIPS = -(-(NG_MIN - 3) // 3)
NG = 3 * TRIPS + 3
NI = NG * GI
LE = NI * IE
NX = 6
RH = 128
BIG = 1e30
SLOPE = 0.2
EPS = 1e-5
TG = 7
NTG = NW // TG
TOK = TG * P
HT = TOK // 2


class Links:

    def __init__(self, engine, sem):
        self.engine, self.sem, self.n, self.trip, self.per_trip = engine, sem, 0, None, 0

    def link(self, ins):
        ins.then_inc(self.sem, 1)
        self.n += 1
        value = self.n if self.trip is None else self.trip * self.per_trip + self.n
        self.engine.wait_ge(self.sem, value)

    def enter(self, trip, per_trip):
        self.n -= per_trip
        self.trip, self.per_trip, self.start = trip, per_trip, self.n

    def leave(self, trips):
        assert self.n - self.start == self.per_trip, (self.n - self.start, self.per_trip)
        self.n += self.per_trip * trips
        self.trip = None


def at_least(engine, sem, value):
    if not (isinstance(value, int) and value <= 0):
        engine.wait_ge(sem, value)


def turn(trip, k):
    return 3 * trip + k, trip + k // 3, k % 3


def build(nc, io):
    with ExitStack() as ctx:
        def sb(name, shape, dt=F32):
            return ctx.enter_context(nc.sbuf_tensor(name, shape, dt))

        def ps(name, shape):
            return ctx.enter_context(nc.psum_tensor(name, shape, F32))

        def sem(name):
            return ctx.enter_context(nc.semaphore(name))

        x_d, src_d, dst_d = io["x"], io["src"], io["dst"]
        out_d = io["out"]
        rows_d = nc.dram_tensor("rows_d", (NPAD, ROW), F32).ap()
        adst_d = nc.dram_tensor("adst_d", (NPAD, H), F32).ap()
        xn_d = nc.dram_tensor("xn_d", (NPAD, D), F32).ap()
        sums_d = nc.dram_tensor("sums_d", (NI * P, ROW), F32).ap()

        arena = sb("arena", [P, 3 * GT * ROW])
        X = arena[:, 0:NW * D].rearrange("p (t d) -> p t d", t=NW)
        G = arena[:, :].rearrange("p (b t c) -> p b t c", b=3, t=GT)
        slot = lambda i, k: GI * k + i
        S = sb("S", [P, 3, GT, P])
        ST = sb("ST", [P, GT, P])
        ident = sb("ident", [P, P])
        ones = sb("ones", [P, P])
        lane = sb("lane", [P, P])
        lane_p = sb("lane_p", [P, 1])
        item_end = sb("item_end", [P, GT])
        winb = sb("winb", [P, NI])
        reset = sb("reset", [P, NI])
        table = sb("table", [1, NI, 2], I32)
        sums_idx = sb("sums_idx", [P, NW], U32)

        eps = sb("eps", [P, 1])

        last_i = sb("last_i", [P, 1], I32)
        last = sb("last", [P, 1])
        thr = sb("thr", [P, NW + 1])
        thr_p = sb("thr_p", [NW + 1, 1])
        below = sb("below", [P, NW + 1])
        rowno = sb("rowno", [NW + 1, 1])
        rowno_u = sb("rowno_u", [NW + 1, 1], U32)
        found = S[0:NW + 1, 0, :, :].rearrange("p t e -> p (t e)")[:, 0:EPP].bitcast(I32)
        less = S[0:NW + 1, 1, :, :].rearrange("p t e -> p (t e)")[:, 0:EPP]
        cnt = sb("cnt", [NW + 1, 1])
        wst = sb("wst", [NW + 1, 1])
        diffm = sb("diffm", [NW + 1, NW])
        before = sb("before", [NW, NW])
        tailc = sb("tailc", [NW, 1])
        nit_i = sb("nit_i", [NW, 2], I32)
        nit = sb("nit", [NW, 1])
        i0 = sb("i0", [NW, 1])
        i1 = sb("i1", [NW, 1])
        i1t = sb("i1t", [NW, 1])
        dcol = sb("dcol", [NW, 1])
        diagl = sb("diagl", [NW, NW])
        iota_i = sb("iota_i", [NW, NI])
        ge = sb("ge", [NW, NI])
        oneh = sb("oneh", [NW, NI])
        w128 = sb("w128", [NW, P])

        W_s = sb("W_s", [P, 2, D])
        att = sb("att", [P, 2, D])
        prod = sb("prod", [P, D])
        Wcat = sb("Wcat", [P, 2, ROW + H])
        wa = sb("wa", [P, 2, 2, H])
        stat = sb("stat", [P, 2, 6])
        mv = sb("mv", [P, 2, 2])
        sd = sb("sd", [P, 2, 1])
        rs = sb("rs", [P, 2, 1])
        xn_s = sb("xn_s", [P, 2, D])
        xnT = sb("xnT", [P, 2, 2, P])
        hrow = sb("hrow", [P, 2, ROW + H])

        erow = sb("erow", [GT, 3, 2 * P + 1], I32)
        erowf = sb("erowf", [GT, 2 * P + 1])
        erend = sb("erend", [GT, P])
        hrep = sb("hrep", [GI * H, 3, IE + 1], I32)
        hrepf = sb("hrepf", [GI * H, 3, IE + 1])
        gap = sb("gap", [GI * H, IE])
        F = sb("F", [GI * H, IE])
        gidx = sb("gidx", [P, 3, GT], U32)
        dloc = sb("dloc", [P, GT])
        isend = sb("isend", [P, 3, GT])
        Fe = sb("Fe", [P, GT, H + 1])
        t1 = sb("t1", [P, GI])
        mi = sb("mi", [P, GI, H])
        M = sb("M", [P, GI + 1, H])
        xm = sb("xm", [P, GI, H])
        R = sb("R", [P, 3, GI + 1, 2 * H])
        da = sb("da", [P, GI, H])
        alpha = sb("alpha", [P, 3, GI, H])
        z = sb("z", [P, GT, H])
        lz = sb("lz", [P, GT, H])
        df = sb("df", [P, GT, H])
        scaled = sb("scaled", [P, ROW])
        acc = sb("acc", [P, 3, GI, ROW])

        b0 = ps("b0", [P, 512])
        b1 = ps("b1", [P, 512])
        b2 = ps("b2", [P, 512])
        b3 = ps("b3", [P, 512])
        b4 = ps("b4", [P, 512])
        b5 = ps("b5", [P, 512])
        b6 = ps("b6", [P, 512])
        b7 = ps("b7", [P, 512])

        idx_ps = b7[:, 0:3 * GT].rearrange("p (n t) -> p n t", n=3)
        mt_ps = b7[:, 64:64 + GI * (H + 1)].rearrange("p (i h) -> p i h", i=GI)
        ex_ps = b2[:, 0:GT * 2 * H].rearrange("p (t h) -> p t h", t=GT)

        s_const = sem("s_const")
        s_ld = sem("s_ld")
        s_apart = sem("s_apart")
        s_last = sem("s_last")
        s_w = sem("s_w")
        s_x = sem("s_x")
        s_v = sem("s_v")
        s_below = sem("s_below")
        s_rowcnt = sem("s_rowcnt")
        s_rowno = sem("s_rowno")
        s_row = sem("s_row")
        s_wst = sem("s_wst")
        s_wcnt = sem("s_wcnt")
        s_nit = sem("s_nit")
        s_i0 = sem("s_i0")
        s_diagl = sem("s_diagl")
        s_lists = sem("s_lists")
        s_items = sem("s_items")
        s_wcat = sem("s_wcat")
        s_var = sem("s_var")
        s_sd = sem("s_sd")
        s_xn = sem("s_xn")
        s_xtp = sem("s_xtp")
        s_xt = sem("s_xt")
        s_hp = sem("s_hp")
        s_hrow = sem("s_hrow")
        s_hst = [sem(f"s_hst{b}") for b in range(2)]
        s_eld = [sem(f"s_eld{b}") for b in range(3)]
        s_cast = sem("s_cast")
        s_rend = sem("s_rend")
        s_idxp = sem("s_idxp")
        s_gidx = sem("s_gidx")
        s_prep = sem("s_prep")
        s_gath = [sem(f"s_gath{b}") for b in range(3)]
        s_S = sem("s_S")
        s_stp = sem("s_stp")
        s_st = sem("s_st")
        s_sT = sem("s_sT")
        s_gap = sem("s_gap")
        s_scan = sem("s_scan")
        s_FP = sem("s_FP")
        s_Fe = sem("s_Fe")
        s_mt = sem("s_mt")
        s_R = sem("s_R")
        s_da = sem("s_da")
        s_alpha = sem("s_alpha")
        s_ex = sem("s_ex")
        s_df = sem("s_df")
        s_wt = sem("s_wt")
        s_msg = sem("s_msg")
        s_pm = sem("s_pm")
        s_acc = sem("s_acc")
        s_sums = [sem(f"s_sums{b}") for b in range(3)]

        def carve(space, at, *shape):
            n = 1
            for q in shape:
                n *= q
            names = " ".join("abcd"[:len(shape)])
            sizes = {"abcd"[i]: q for i, q in enumerate(shape[:-1])}
            return space[:, at:at + n].rearrange(f"p ({names}) -> p {names}", **sizes), at + n

        XT, at = carve(arena, 0, 2, 2, TOK)
        X1, at = carve(arena, at, 2, TG, D)
        XL, at = carve(arena, at, 2, TG, D)
        SM, at = carve(arena, at, TG, ROW)
        S_flat = S[:, :, :, :].rearrange("p b t e -> p (b t e)")
        h1T, at = carve(S_flat, 0, 2, TOK)
        h2T, at = carve(S_flat, at, 2, TOK)
        rhT = S_flat[:, at:at + TOK]
        EW1 = sb("EW1", [P, NX, 2, D])
        EW2 = sb("EW2", [P, NX, 2, D])
        EW3 = sb("EW3", [P, NX, 2, D])
        RW1 = sb("RW1", [P, 2, RH])
        RW2 = sb("RW2", [P, NX])
        EB3 = sb("EB3", [NX, D])
        RB1 = sb("RB1", [P, 1])
        EB = sb("EB", [P, 2, NX, 2])
        RB2 = sb("RB2", [P, NX])
        VEC = sb("VEC", [P, 3, D])
        den = sb("den", [P, TG * H])
        rden = sb("rden", [P, TG * H])
        st_s = sb("st_s", [P, TG, 6])
        st_m = sb("st_m", [P, TG, 2])
        st_d = sb("st_d", [P, TG])
        st_r = sb("st_r", [P, TG])
        lgs = sb("lgs", [P, TG, NX])
        lmx = sb("lmx", [P, TG])
        lsum = sb("lsum", [P, TG])
        lrec = sb("lrec", [P, TG])
        prob = sb("prob", [P, TG, 8])
        top = sb("top", [P, TG, 8])
        topi = sb("topi", [P, TG, 8], U32)
        topf = sb("topf", [P, TG, 2])
        tdif = sb("tdif", [P, TG])
        tex = sb("tex", [P, TG])
        ten = sb("ten", [P, TG])
        tw = sb("tw", [P, 2, TG])
        expert = sb("expert", [P, TG, NX])
        c1 = sb("c1", [P, TG, NX])
        c2 = sb("c2", [P, TG, NX])
        coef = sb("coef", [P, TG, NX])
        coefT = sb("coefT", [NX, TOK])
        s_ew = sem("s_ew")
        s_xl = sem("s_xl")
        s_sm = sem("s_sm")
        s_smfree = sem("s_smfree")
        s_neg = sem("s_neg")
        s_exp = sem("s_exp")
        s_var4 = sem("s_var4")
        s_sd4 = sem("s_sd4")
        s_xn4 = sem("s_xn4")
        s_tp4 = sem("s_tp4")
        s_xt4 = sem("s_xt4")
        s_bank = sem("s_bank")
        s_lay = sem("s_lay")
        s_lg = sem("s_lg")
        s_lsub = sem("s_lsub")
        s_lexp = sem("s_lexp")
        s_tdif = sem("s_tdif")
        s_tex = sem("s_tex")
        s_coef = sem("s_coef")
        s_cT = sem("s_cT")
        s_coefT = sem("s_coefT")
        s_eo = sem("s_eo")
        s_comb = sem("s_comb")
        s_out = [sem(f"s_out{b}") for b in range(2)]
        lg_ps = b6[:, 0:TG * NX].rearrange("p (t e) -> p t e", t=TG)
        lay_bank = lambda b, n: (b0, b1, b2, b3)[(NLAY * b + n) % 4][:, 0:HT]
        eo_bank = lambda b, n: (b4, b5)[(NCOMB * b + n) % 2][:, 0:D]
        NLAY = 2 + NX * 8
        NCOMB = TG * (NX + 1)

        def apart(engine):
            engine.sem_inc(s_apart, 1)

        x_t = x_d.rearrange("(t p) d -> p t d", p=P)
        block = ctx.enter_context(nc.Block())

        @block.sync
        def _(sp):
            dst_pp = dst_d[0:P * EPP].rearrange("(p e) -> p e", p=P)
            with nc.allow_non_contiguous_dma(reason="one number per partition"):
                sp.dma_start(last_i[:, :], dst_pp[:, EPP - 1:EPP]).then_inc(s_last, 16)
            sp.dma_start(W_s[:, :, :], io["W"].rearrange("(c p) n -> p c n", p=P)).then_inc(s_w, 16)
            for n, a in enumerate((io["att_src"], io["att_dst"])):
                sp.dma_start(att[:, n, :], a.rearrange("h c -> (h c)").partition_broadcast(P)).then_inc(s_w, 16)
            for t in range(0, NW, 7):
                sp.dma_start(X[:, t:t + 7, :], x_t[:, t:t + 7, :]).then_inc(s_x, 16)

            for tile, dram in zip((EW1, EW2, EW3), (io["ew1"], io["ew2"], io["ew3"])):
                sp.dma_start(tile[:, :, :, :], dram.rearrange("e (c p) n -> p e c n", p=P)).then_inc(s_ew, 16)
            sp.dma_start(RW1[:, :, :], io["rw1"].rearrange("(c p) n -> p c n", p=P)).then_inc(s_ew, 16)
            sp.dma_start(RW2[:, :], io["rw2"]).then_inc(s_ew, 16)
            sp.dma_start(EB3[:, :], io["eb3"]).then_inc(s_ew, 16)
            with nc.allow_non_contiguous_dma(reason="small biases, one per partition"):
                sp.dma_start(RB1[:, :], io["rb1"].rearrange("(p a) -> p a", a=1)).then_inc(s_ew, 16)
                for n, dram in enumerate((io["eb1"], io["eb2"])):
                    for e in range(NX):
                        sp.dma_start(EB[:, n, e, :], dram[e].rearrange("(c p) -> p c", p=P)).then_inc(s_ew, 16)
            sp.dma_start(RB2[:, :], io["rb2"].partition_broadcast(P)).then_inc(s_ew, 16)
            for n, dram in enumerate((io["bias"], io["ln_scale"], io["ln_bias"])):
                sp.dma_start(VEC[:, n, :], dram.partition_broadcast(P)).then_inc(s_ew, 16)

            def store_rows(n, b):
                sp.wait_ge(s_hrow, n + 1)
                rows = bass.ds(n * P, P)
                sp.dma_start(rows_d[rows, :], hrow[:, b, 0:ROW]).then_inc(s_hst[b], 16)
                sp.dma_start(adst_d[rows, :], hrow[:, b, ROW:ROW + H]).then_inc(s_hst[b], 16)
                sp.dma_start(xn_d[rows, :], xn_s[:, b, :]).then_inc(s_hst[b], 16)

            for n in range(3):
                store_rows(n, n % 2)
            with sp.Fori(1, NW // 2) as trip:
                for k in (1, 2):
                    store_rows(2 * trip + k, k % 2)
            for b, n in ((0, NW // 2 + 1), (1, NW // 2)):
                sp.wait_ge(s_hst[b], 48 * n)

            sp.wait_ge(s_items, 1)

            def load_group(j, q, b):
                at_least(sp, s_ex, j - 2)
                for i in range(GI):
                    start = sp.value_load(table[0:1, bass.ds(GI * j + i, 1), 0], min_val=0, max_val=LE - IE)
                    node = sp.value_load(table[0:1, bass.ds(GI * j + i, 1), 1], min_val=0, max_val=NPAD - P)
                    sp.dma_start(erow[IT * i:IT * i + IT, b, 0:P],
                                 src_d[bass.ds(start, IE)].rearrange("(k e) -> k e", k=IT)).then_inc(s_eld[b], 16)
                    d = dst_d[bass.ds(start + 1, IE + 1)]
                    sp.dma_start(erow[IT * i:IT * i + IT, b, P:2 * P + 1],
                                 bass.AP(d.tensor, d.offset, [[P, IT], [1, P + 1]])).then_inc(s_eld[b], 16)
                    sp.dma_start(hrep[H * i:H * i + H, b, :],
                                 dst_d[bass.ds(start, IE + 1)].partition_broadcast(H)).then_inc(s_eld[b], 16)
                    sp.dma_start(R[:, b, 1 + i, 0:H], adst_d[bass.ds(node, P), :]).then_inc(s_eld[b], 16)

            for k in range(3):
                load_group(*turn(0, k))
            with sp.Fori(1, NG // 3) as trip:
                for k in range(3):
                    load_group(*turn(trip, k))

            sp.wait_ge(s_pm, GI * NG)

            def load_nodes(g):
                at_least(sp, s_tp4, 4 * g)
                nodes = bass.ds(g * TOK, TOK)
                for n, dram in enumerate((x_d, xn_d)):
                    sp.dma_start(XL[:, n, :, :], dram[nodes, :].rearrange("(t p) d -> p t d", p=P)).then_inc(s_xl, 16)

            def store_nodes(g, b):
                sp.wait_ge(s_comb, NCOMB * (g + 1))
                sp.dma_start(out_d[bass.ds(g * TOK, TOK), :].rearrange("(t p) d -> p t d", p=P),
                             X1[:, b, :, :]).then_inc(s_out[b], 16)

            load_nodes(0)
            for g in range(2):
                load_nodes(g + 1)
                store_nodes(g, g)
            with sp.Fori(1, (NTG - 1) // 2) as trip:
                for b in range(2):
                    load_nodes(2 * trip + b + 1)
                    store_nodes(2 * trip + b, b)
            sp.wait_ge(s_comb, NCOMB * NTG)
            first, full = (NTG - 1) * TOK, N // P - (NTG - 1) * TG
            sp.dma_start(out_d[first:first + full * P, :].rearrange("(t p) d -> p t d", p=P),
                         X1[:, 0, 0:full, :]).then_inc(s_out[0], 16)
            sp.dma_start(out_d[first + full * P:N, :], X1[0:N % P, 0, full, :]).then_inc(s_out[0], 16)
            sp.wait_ge(s_out[0], 16 * ((NTG + 1) // 2 + 1))
            sp.wait_ge(s_out[1], 16 * (NTG // 2))

        @block.gpsimd
        def _(pool):
            iota = lambda o, pat, m: pool.iota(o, pattern=pat, base=0, channel_multiplier=m,
                                               allow_small_or_imprecise_dtypes=True)
            pool.memset(ident[:, :], 0.0).then_inc(s_ld, 1)
            pool.memset(diffm[:, :], 0.0).then_inc(s_ld, 1)
            pool.memset(before[:, :], 1.0).then_inc(s_ld, 1)
            pool.memset(tailc[:, :], 0.0).then_inc(s_ld, 1)
            pool.memset(item_end[:, :], 0.0).then_inc(s_ld, 1)
            pool.memset(ones[:, :], 1.0).then_inc(s_const, 1)
            pool.memset(eps[:, :], EPS).then_inc(s_const, 1)
            iota(thr[:, :], [[P, NW + 1]], 0).then_inc(s_const, 1)
            iota(thr_p[:, :], [[0, 1]], P).then_inc(s_const, 1)
            iota(lane[:, :], [[1, P]], 0).then_inc(s_const, 1)
            iota(lane_p[:, :], [[0, 1]], 1).then_inc(s_const, 1)
            iota(iota_i[:, :], [[1, NI]], 0).then_inc(s_const, 1)
            iota(w128[:, :], [[0, P]], P).then_inc(s_const, 1)
            iota(expert[:, :, :], [[0, TG], [1, NX]], 0).then_inc(s_const, 1)
            pool.memset(prob[:, :, :], -1.0).then_inc(s_const, 1)

            def select(m, pat, base, mult, op, fill):
                return pool.affine_select(out=m, in_=m, compare_op=op, fill=fill, base=base,
                                          pattern=pat, channel_multiplier=mult)

            pool.wait_ge(s_ld, 5)
            select(ident[:, :], [[-1, P]], 0, 1, ALU.not_equal, 1.0).then_inc(s_const, 1)
            select(before[:, :], [[1, NW]], 0, -1, ALU.is_gt, 0.0).then_inc(s_const, 1)
            select(tailc[:, :], [[0, 1]], -(NW - 1), 1, ALU.not_equal, 1e6).then_inc(s_const, 1)
            e = item_end[:, :].rearrange("p (i k) -> p i k", k=IT)
            select(e, [[0, GI], [1, IT]], -(IT - 1 + P - 1), 1, ALU.not_equal, 1.0).then_inc(s_const, 1)
            select(diffm[:, :], [[-1, NW]], 0, 1, ALU.not_equal, -1.0).then_inc(s_ld, 1)
            pool.wait_ge(s_ld, 6)
            select(diffm[:, :], [[-1, NW]], -1, 1, ALU.not_equal, 1.0).then_inc(s_const, 1)

            pool.wait_ge(s_rowno, 1)
            dst_pp = dst_d[0:P * EPP].rearrange("(p e) -> p e", p=P)
            pool.indirect_dma_start(found, None, dst_pp,
                                    bass.IndirectOffsetOnAxis(ap=rowno_u[:, 0:1], axis=0)).then_inc(s_row, 16)

            for b, n in ((0, NW // 2 + 1), (1, NW // 2)):
                pool.wait_ge(s_hst[b], 48 * n)

            def gather(j, q, b):
                pool.wait_ge(s_gidx, j + 1)
                at_least(pool, s_pm, GI * (j - 2))
                apart(pool)
                for t in range(GT):
                    pool.indirect_dma_start(G[:, b, slot(t // IT, t % IT), :], None, rows_d,
                                            bass.IndirectOffsetOnAxis(ap=gidx[:, b, t:t + 1], axis=0)
                                            ).then_inc(s_gath[b], 16)

            for k in range(3):
                gather(*turn(0, k))
            with pool.Fori(1, NG // 3) as trip:
                for k in range(3):
                    gather(*turn(trip, k))

            for b in range(3):
                pool.wait_ge(s_sums[b], 16 * (NG // 3))
            for g in range(NTG):
                at_least(pool, s_smfree, g)
                for t in range(TG):
                    pool.indirect_dma_start(SM[:, t, :], None, sums_d,
                                            bass.IndirectOffsetOnAxis(ap=sums_idx[:, TG * g + t:TG * g + t + 1],
                                                                      axis=0)).then_inc(s_sm, 16)

        @block.vector
        def _(dve):
            v = Links(dve, s_v)
            dve.wait_ge(s_last, 16)
            dve.wait_ge(s_const, 15)
            v.link(dve.tensor_copy(last[:, :], last_i[:, :]))
            dve.tensor_scalar(below[:, :], thr[:, :], last[:, 0:1], None, ALU.is_gt).then_inc(s_below, 1)
            dve.wait_ge(s_rowcnt, 1)
            v.link(dve.tensor_scalar(rowno[:, :], b0[0:NW + 1, 0:1], float(P - 1), None, ALU.min))
            dve.tensor_copy(rowno_u[:, :], rowno[:, :]).then_inc(s_rowno, 1)
            dve.wait_ge(s_row, 16)
            v.link(dve.tensor_scalar(less, found, thr_p[:, 0:1], None, ALU.is_lt))
            v.link(dve.tensor_reduce(cnt[:, :], less, AX.X, ALU.add))
            v.link(dve.scalar_tensor_tensor(out=wst[:, :], in0=rowno[:, :], scalar=float(EPP), in1=cnt[:, :],
                                            op0=ALU.mult, op1=ALU.add))
            dve.tensor_scalar(wst[:, :], wst[:, :], -1.0, None, ALU.add).then_inc(s_wst, 1)
            dve.wait_ge(s_wcnt, 1)
            v.link(dve.tensor_scalar(nit_i[:, 0:1], b1[0:NW, 0:1], float(IE - 1), None, ALU.add))
            v.link(dve.tensor_scalar(nit_i[:, 1:2], nit_i[:, 0:1], IE.bit_length() - 1, None,
                                     ALU.arith_shift_right))
            dve.tensor_scalar(nit[:, :], nit_i[:, 1:2], 1.0, None, ALU.max).then_inc(s_nit, 1)
            dve.wait_ge(s_i0, 1)
            v.link(dve.tensor_copy(i0[:, :], b2[0:NW, 0:1]))
            v.link(dve.tensor_tensor(i1t[:, :], i0[:, :], nit[:, :], ALU.add))
            v.link(dve.tensor_tensor(i1[:, :], i1t[:, :], tailc[:, :], ALU.add))
            v.link(dve.tensor_scalar(ge[:, :], iota_i[:, :], i0[:, 0:1], None, ALU.is_ge))
            v.link(dve.scalar_tensor_tensor(out=oneh[:, :], in0=iota_i[:, :], scalar=i1[:, 0:1], in1=ge[:, :],
                                            op0=ALU.is_lt, op1=ALU.mult))
            v.link(dve.scalar_tensor_tensor(out=dcol[:, :], in0=i0[:, :], scalar=-float(IE), in1=wst[0:NW, :],
                                            op0=ALU.mult, op1=ALU.add))
            v.link(dve.tensor_scalar(i1t[:, :], i1[:, :], float(NI), -1.0, ALU.min, ALU.add))
            dve.tensor_scalar(diagl[:, :], ident[0:NW, 0:NW], i1t[:, 0:1], None, ALU.mult).then_inc(s_diagl, 1)
            dve.wait_ge(s_lists, 1)
            v.link(dve.tensor_copy(winb[:, :], b3[:, 0:NI]))
            dve.tensor_copy(table[0:1, :, 1], winb[0:1, :])
            dve.scalar_tensor_tensor(out=table[0:1, :, 0], in0=iota_i[0:1, :], scalar=float(IE),
                                     in1=b4[0:1, 0:NI], op0=ALU.mult, op1=ALU.add).then_inc(s_items, 1)
            v.link(dve.memset(reset[:, 0:1], -BIG))
            v.link(dve.tensor_tensor(reset[:, 1:NI], winb[:, 1:NI], winb[:, 0:NI - 1], ALU.not_equal))
            v.link(dve.tensor_scalar(reset[:, 1:NI], reset[:, 1:NI], -BIG, None, ALU.mult))
            v.link(dve.tensor_scalar(sums_idx[:, :], b5[:, 0:NW], float(P), lane_p[:, 0:1], ALU.mult, ALU.add))

            dve.wait_ge(s_w, 48)
            for c in range(2):
                for n in range(2):
                    v.link(dve.tensor_tensor(prod[:, :], W_s[:, c, :], att[:, n, :], ALU.mult))
                    v.link(dve.tensor_reduce(wa[:, c, n, :], prod[:, :].rearrange("p (h c) -> p h c", h=H),
                                             AX.X, ALU.add))
                heads = Wcat[:, c, 0:ROW].rearrange("p (h c) -> p h c", h=H)
                v.link(dve.tensor_copy(heads[:, :, 0:C], W_s[:, c, :].rearrange("p (h c) -> p h c", h=H)))
                v.link(dve.tensor_copy(heads[:, :, C], wa[:, c, 0, :]))
                dve.tensor_copy(Wcat[:, c, ROW:ROW + H], wa[:, c, 1, :]).then_inc(s_wcat, 1)
            dve.wait_ge(s_x, 16 * NTG)

            def node_tile(n, b, used):
                xt = X[:, bass.ds(n, 1), :].rearrange("p t d -> p (t d)")
                v.link(dve.bn_stats(stat[:, b, :], xt))
                apart(dve)
                dve.bn_aggr(mv[:, b, :], stat[:, b, :]).then_inc(s_var, 1)
                dve.wait_ge(s_sd, n + 1)
                v.link(dve.reciprocal(rs[:, b, :], sd[:, b, :]))
                at_least(dve, s_hst[b], 48 * used)
                dve.tensor_scalar(xn_s[:, b, :], xt, mv[:, b, 0:1], rs[:, b, 0:1], ALU.subtract, ALU.mult).then_inc(s_xn, 1)
                dve.wait_ge(s_xtp, n + 1)
                at_least(dve, s_hp, n - 1)
                dve.tensor_copy(xnT[:, b, :, :], b0[:, 0:D].rearrange("p (c e) -> p c e", c=2)).then_inc(s_xt, 1)

            for n in range(3):
                node_tile(n, n % 2, n // 2)
            with dve.Fori(1, NW // 2) as trip:
                v.enter(trip, 4)
                for k in (1, 2):
                    node_tile(2 * trip + k, k % 2, trip + k // 2)
                v.leave(NW // 2 - 1)

            v.link(dve.memset(acc[:, 2, GI - 1, :], 0.0))
            v.link(dve.memset(M[:, GI, :], -BIG))
            v.link(dve.memset(R[:, 2, GI, H:2 * H], 0.0))

            def prepare(j, q, b):
                dve.wait_ge(s_cast, 2 * (j + 1) - 1)
                dve.tensor_tensor(erend[:, :], erowf[:, P:2 * P], erowf[:, P + 1:2 * P + 1],
                                  ALU.not_equal).then_inc(s_rend, 1)

            def place(j, q, b):
                dve.wait_ge(s_idxp, j + 1)
                dve.tensor_copy(gidx[:, b, :], idx_ps[:, 0, :]).then_inc(s_gidx, 1)
                items = bass.ds(GI * j, GI)
                v.link(dve.tensor_tensor(dloc[:, :].rearrange("p (i k) -> p i k", k=IT),
                                         idx_ps[:, 1, :].rearrange("p (i k) -> p i k", k=IT),
                                         winb[:, items].unsqueeze(2).to_broadcast([P, GI, IT]), ALU.subtract))
                dve.tensor_tensor(isend[:, b, :], idx_ps[:, 2, :], item_end[:, :], ALU.max).then_inc(s_prep, 1)

            def one_hot(j, q, b):
                dve.wait_ge(s_prep, j + 1)
                at_least(dve, s_pm, GI * (j - 2))
                dve.tensor_tensor(S[:, b, :, :], dloc[:, :].unsqueeze(2).to_broadcast([P, GT, P]),
                                  lane[:, :].unsqueeze(1).to_broadcast([P, GT, P]), ALU.is_equal).then_inc(s_S, 1)

            def segment_gaps(j, q, b):
                dve.wait_ge(s_cast, 2 * (j + 1))
                dve.tensor_tensor(gap[:, :], hrepf[:, b, 0:IE], hrepf[:, b, 1:IE + 1], ALU.subtract).then_inc(s_gap, 1)

            def scan(j, q, b):
                dve.wait_ge(s_gap, j + 1)
                dve.wait_ge(s_sT, j + 1)
                dve.tensor_tensor_scan(F[:, :], gap[:, :], b0[0:GI * H, :], -BIG, ALU.add, ALU.max).then_inc(s_scan, 1)

            def ends(j, q, b):
                dve.wait_ge(s_FP, j + 1)
                dve.wait_ge(s_prep, j + 1)
                dve.tensor_tensor(Fe[:, :, 0:H].rearrange("p (i k) h -> p i k h", k=IT),
                                  b1[:, 0:GT * H].rearrange("p (k i h) -> p i k h", k=IT, i=GI),
                                  isend[:, b, :].rearrange("p (i k) -> p i k", k=IT).unsqueeze(3)
                                  .to_broadcast([P, GI, IT, H]), ALU.mult).then_inc(s_Fe, 1)
                dve.tensor_copy(Fe[:, :, H], isend[:, b, :]).then_inc(s_Fe, 1)

            def shifts(j, q, b):
                dve.wait_ge(s_mt, j + 1)
                v.link(dve.tensor_scalar(t1[:, :], mt_ps[:, :, H], BIG, -BIG, ALU.mult, ALU.add))
                dve.tensor_copy(M[:, 0, :], M[:, GI, :])
                dve.tensor_copy(R[:, b, 0, H:2 * H], R[:, (b + 2) % 3, GI, H:2 * H])
                v.link(dve.tensor_tensor(mi[:, :, :], mt_ps[:, :, 0:H],
                                         t1[:, :].unsqueeze(2).to_broadcast([P, GI, H]), ALU.add))
                for i in range(GI):
                    v.link(dve.scalar_tensor_tensor(out=M[:, i + 1, :], in0=M[:, i, :],
                                                    scalar=reset[:, bass.ds(GI * j + i, 1)], in1=mi[:, i, :],
                                                    op0=ALU.add, op1=ALU.max))
                v.link(dve.tensor_tensor(xm[:, :, :], M[:, 1:GI + 1, :], R[:, b, 1:GI + 1, 0:H], ALU.add))
                dve.scalar_tensor_tensor(out=R[:, b, 1:GI + 1, H:2 * H], in0=xm[:, :, :], scalar=SLOPE,
                                         in1=xm[:, :, :], op0=ALU.mult, op1=ALU.max).then_inc(s_R, 1)
                dve.wait_ge(s_R, j + 1)
                v.link(dve.tensor_tensor(da[:, :, :], R[:, b, 0:GI, H:2 * H], R[:, b, 1:GI + 1, H:2 * H],
                                         ALU.subtract))
                dve.tensor_tensor(da[:, :, :], da[:, :, :],
                                  reset[:, bass.ds(GI * j, GI)].unsqueeze(2).to_broadcast([P, GI, H]),
                                  ALU.add).then_inc(s_da, 1)

            def logits(j, q, b):
                dve.wait_ge(s_ex, j + 1)
                a_src = G[:, b, :, :].rearrange("p t (h c) -> p t h c", h=H)[:, :, :, C]
                v.link(dve.tensor_tensor(z[:, :, :], a_src, ex_ps[:, :, 0:H], ALU.add))
                v.link(dve.scalar_tensor_tensor(out=lz[:, :, :], in0=z[:, :, :], scalar=SLOPE, in1=z[:, :, :],
                                                op0=ALU.mult, op1=ALU.max))
                v.link(dve.tensor_tensor(df[:, :, :], lz[:, :, :], ex_ps[:, :, H:2 * H], ALU.subtract))
                dve.tensor_scalar(df[:, :, :], df[:, :, :], 0.0, None, ALU.min).then_inc(s_df, 1)

            def message(j, q, b, i):
                dve.wait_ge(s_wt, j + 1)
                g = G[:, b, i:GT:GI, :].rearrange("p t (h c) -> p t h c", h=H)
                dve.tensor_tensor(g[:, :, :, 0:C], g[:, :, :, 0:C], g[:, :, :, C:HC].to_broadcast([P, IT, H, C]),
                                  ALU.mult).then_inc(s_msg, 1)

            def accumulate(j, q, b, i):
                dve.wait_ge(s_alpha, j + 1)
                if i == 0:
                    at_least(dve, s_sums[b], 16 * q)
                at_least(dve, s_acc, GI * j + i)
                old = acc[:, (b + 2) % 3, GI - 1, :] if i == 0 else acc[:, b, i - 1, :]
                v.link(dve.tensor_tensor(scaled[:, :].rearrange("p (h c) -> p h c", h=H),
                                         old.rearrange("p (h c) -> p h c", h=H),
                                         alpha[:, b, i, :].unsqueeze(2).to_broadcast([P, H, HC]), ALU.mult))
                dve.wait_ge(s_pm, GI * j + i + 1)
                dve.tensor_tensor(acc[:, b, i, :], scaled[:, :], (b3, b4)[i % 2][:, 0:ROW], ALU.add).then_inc(s_acc, 1)

            prepare(*turn(0, 0)); place(*turn(0, 0)); one_hot(*turn(0, 0))
            prepare(*turn(0, 1)); place(*turn(0, 1))

            def body(trip, k, back=True, prep=True, hot=True):
                now, ago = turn(trip, k), turn(trip, k - 1)
                segment_gaps(*now)
                if back:
                    message(*ago, 0)
                scan(*now)
                if back:
                    message(*ago, 1)
                if hot:
                    one_hot(*turn(trip, k + 1))
                ends(*now)
                if back:
                    accumulate(*ago, 0)
                    message(*ago, 2)
                shifts(*now)
                if back:
                    message(*ago, 3)
                    accumulate(*ago, 1)
                if prep:
                    prepare(*turn(trip, k + 2))
                    place(*turn(trip, k + 2))
                if back:
                    accumulate(*ago, 2)
                    accumulate(*ago, 3)
                logits(*now)

            body(0, 0, back=False)
            for k in (1, 2, 3):
                body(0, k)
            with dve.Fori(1, TRIPS) as trip:
                v.enter(trip, 3 * (8 + 1 + 3 + 4))
                for k in (1, 2, 3):
                    body(trip, k)
                v.leave(TRIPS - 1)
            body(TRIPS, 1, prep=False)
            body(TRIPS, 2, prep=False, hot=False)
            for i in range(GI):
                message(*turn(TRIPS, 2), i)
            for i in range(GI):
                accumulate(*turn(TRIPS, 2), i)

            flat = lambda o: o.rearrange("p t d -> p (t d)")
            over_tiles = lambda n: VEC[:, n, :].unsqueeze(1).to_broadcast([P, TG, D])

            def attention_out(g, b):
                dve.wait_ge(s_sm, 16 * TG * (g + 1))
                dve.wait_ge(s_xl, 32 * (g + 1))
                sm = SM[:, :, :].rearrange("p t (h c) -> p (t h) c", h=H)
                v.link(dve.tensor_scalar(den[:, :], sm[:, :, C], 1e-16, None, ALU.add))
                v.link(dve.reciprocal(rden[:, :], den[:, :]))
                at_least(dve, s_out[b], 16 * stored[b])
                dve.tensor_tensor(X1[:, b, :, :].rearrange("p t (h c) -> p (t h) c", h=H), sm[:, :, 0:C],
                                  rden[:, :].unsqueeze(2).to_broadcast([P, TG * H, C]), ALU.mult).then_inc(s_smfree, 1)
                dve.wait_ge(s_smfree, g + 1)
                v.link(dve.tensor_tensor(X1[:, b, :, :], X1[:, b, :, :], over_tiles(0), ALU.add))
                v.link(dve.tensor_tensor(X1[:, b, :, :], X1[:, b, :, :], XL[:, 1, :, :], ALU.add))
                dve.tensor_scalar(XL[:, 1, :, :], X1[:, b, :, :], 0.0, None, ALU.min).then_inc(s_neg, 1)

            def statistics(b):
                for t in range(TG):
                    one = dve.bn_stats(st_s[:, t, :], X1[:, b, t, :])
                v.link(one)
                apart(dve)
                for t in range(TG):
                    one = dve.bn_aggr(st_m[:, t, :], st_s[:, t, :])
                return one

            def elu(g, b):
                dve.wait_ge(s_exp, g + 1)
                v.link(dve.scalar_tensor_tensor(out=flat(X1[:, b, :, :]), in0=flat(XL[:, 1, :, :]), scalar=-1.0,
                                                in1=flat(X1[:, b, :, :]), op0=ALU.add, op1=ALU.max))
                statistics(b).then_inc(s_var4, 1)

            def normalize(out, g, b, done):
                dve.wait_ge(s_sd4, done)
                v.link(dve.reciprocal(st_r[:, :], st_d[:, :]))
                for t in range(TG):
                    one = dve.tensor_scalar(out[:, t, :], X1[:, b, t, :], st_m[:, t, 0:1], st_r[:, t:t + 1],
                                            ALU.subtract, ALU.mult)
                return one

            def first_norm(g, b):
                v.link(normalize(X1[:, b, :, :], g, b, 2 * g + 1))
                v.link(dve.tensor_tensor(X1[:, b, :, :], X1[:, b, :, :], over_tiles(1), ALU.mult))
                v.link(dve.tensor_tensor(X1[:, b, :, :], X1[:, b, :, :], over_tiles(2), ALU.add))
                v.link(dve.tensor_tensor(X1[:, b, :, :], X1[:, b, :, :], XL[:, 0, :, :], ALU.add))
                statistics(b).then_inc(s_var4, 1)

            def second_norm(g, b):
                normalize(XL[:, 1, :, :], g, b, 2 * g + 2).then_inc(s_xn4, 1)

            def route(g, b):
                wide = lambda o, n: o.unsqueeze(2).to_broadcast([P, TG, n])
                dve.wait_ge(s_lg, g + 1)
                v.link(dve.tensor_tensor(lgs[:, :, :], lg_ps, RB2[:, :].unsqueeze(1).to_broadcast([P, TG, NX]), ALU.add))
                v.link(dve.tensor_reduce(lmx[:, :], lgs[:, :, :], AX.X, ALU.max))
                dve.tensor_tensor(lgs[:, :, :], lgs[:, :, :], wide(lmx[:, :], NX), ALU.subtract).then_inc(s_lsub, 1)
                dve.wait_ge(s_lexp, g + 1)
                v.link(dve.tensor_reduce(lsum[:, :], lgs[:, :, :], AX.X, ALU.add))
                v.link(dve.reciprocal(lrec[:, :], lsum[:, :]))
                v.link(dve.tensor_tensor(prob[:, :, 0:NX], lgs[:, :, :], wide(lrec[:, :], NX), ALU.mult))
                apart(dve)
                for t in range(TG):
                    one = dve.max(top[:, t, :], prob[:, t, :])
                v.link(one)
                apart(dve)
                for t in range(TG):
                    one = dve.max_index(topi[:, t, :], top[:, t, :], prob[:, t, :])
                v.link(one)
                dve.tensor_tensor(tdif[:, :], top[:, :, 1], top[:, :, 0], ALU.subtract).then_inc(s_tdif, 1)
                v.link(dve.tensor_copy(topf[:, :, :], topi[:, :, 0:2]))
                v.link(dve.tensor_tensor(c1[:, :, :], expert[:, :, :], wide(topf[:, :, 0], NX), ALU.is_equal))
                v.link(dve.tensor_tensor(c2[:, :, :], expert[:, :, :], wide(topf[:, :, 1], NX), ALU.is_equal))
                dve.wait_ge(s_tex, g + 1)
                v.link(dve.tensor_scalar(ten[:, :], tex[:, :], 1.0, None, ALU.add))
                v.link(dve.reciprocal(tw[:, 0, :], ten[:, :]))
                v.link(dve.tensor_tensor(tw[:, 1, :], tex[:, :], tw[:, 0, :], ALU.mult))
                v.link(dve.tensor_tensor(c1[:, :, :], c1[:, :, :], wide(tw[:, 0, :], NX), ALU.mult))
                v.link(dve.tensor_tensor(c2[:, :, :], c2[:, :, :], wide(tw[:, 1, :], NX), ALU.mult))
                dve.tensor_tensor(coef[:, :, :], c1[:, :, :], c2[:, :, :], ALU.add).then_inc(s_coef, 1)

            def expert_bias(g, b):
                dve.wait_ge(s_cT, g + 1)
                dve.tensor_copy(coefT[:, 0:4 * P], b6[0:NX, :]).then_inc(s_coefT, 1)
                dve.tensor_copy(coefT[:, 4 * P:TOK], b7[0:NX, 0:(TG - 4) * P]).then_inc(s_coefT, 1)
                for t in range(TG):
                    dve.wait_ge(s_eo, NCOMB * g + t + 1)
                    dve.tensor_tensor(X1[:, b, t, :], X1[:, b, t, :], eo_bank(b, t), ALU.add).then_inc(s_comb, 1)

            def combine(g, b, e):
                for t in range(TG):
                    n = TG * (e + 1) + t
                    dve.wait_ge(s_eo, NCOMB * g + n + 1)
                    dve.wait_ge(s_comb, NCOMB * g + n - TG + 1)
                    dve.scalar_tensor_tensor(out=X1[:, b, t, :], in0=eo_bank(b, n), scalar=coef[:, t, e:e + 1],
                                             in1=X1[:, b, t, :], op0=ALU.mult, op1=ALU.add).then_inc(s_comb, 1)

            def node_body(g, b, ahead=True):
                parts = (attention_out, elu, first_norm, second_norm)
                route(g, b)
                for e in range(-1, NX):
                    if e < 0:
                        expert_bias(g, b)
                    else:
                        combine(g, b, e)
                    if ahead and e + 1 < len(parts):
                        parts[e + 1](g + 1, 1 - b)

            stored = [0, 0]
            dve.wait_ge(s_ew, 16 * 23)
            for part in (attention_out, elu, first_norm, second_norm):
                part(0, 0)
            for g in range(2):
                stored = [1, 0]
                node_body(g, g)
            with dve.Fori(1, (NTG - 1) // 2) as trip:
                v.enter(trip, 2 * 28)
                for b in range(2):
                    stored = [trip + 1, trip]
                    node_body(2 * trip + b, b)
                v.leave((NTG - 1) // 2 - 1)
            node_body(NTG - 1, 0, ahead=False)

        @block.scalar
        def _(act):
            def node_tile(n, b, used):
                act.wait_ge(s_var, n + 1)
                nc.scalar.activation(sd[:, b, :], mv[:, b, 1:2], ACT.Sqrt, bias=eps[:, 0:1]).then_inc(s_sd, 1)
                at_least(act, s_hst[b], 48 * used)
                act.wait_ge(s_hp, n + 1)
                nc.scalar.copy(hrow[:, b, :], (b1, b2)[b][:, 0:ROW + H]).then_inc(s_hrow, 1)

            act.wait_ge(s_const, 15)
            for n in range(3):
                node_tile(n, n % 2, n // 2)
            with act.Fori(1, NW // 2) as trip:
                for k in (1, 2):
                    node_tile(2 * trip + k, k % 2, trip + k // 2)

            def casts(j, q, b):
                act.wait_ge(s_eld[b], 4 * GI * 16 * (q + 1))
                at_least(act, s_idxp, j)
                nc.scalar.copy(erowf[:, 0:2 * P + 1], erow[:, b, :]).then_inc(s_cast, 1)
                nc.scalar.activation(hrepf[:, b, :], hrep[:, b, :], ACT.Copy, scale=BIG).then_inc(s_cast, 1)

            def st_copies(j, q, b):
                at_least(act, s_ex, j)
                for i in range(GI):
                    act.wait_ge(s_stp, GI * j + i + 1)
                    nc.scalar.copy(ST[:, IT * i:IT * i + IT, :].rearrange("p t e -> p (t e)"),
                                   (b5, b6)[i % 2][:, :]).then_inc(s_st, 1)

            def alphas(j, q, b):
                act.wait_ge(s_da, j + 1)
                nc.scalar.activation(alpha[:, b, :, :], da[:, :, :], ACT.Exp).then_inc(s_alpha, 1)

            def weights(j, q, b):
                act.wait_ge(s_df, j + 1)
                w = G[:, b, :, :].rearrange("p t (h c) -> p (t h) c", h=H)[:, :, C]
                nc.scalar.activation(w, df[:, :, :].rearrange("p t h -> p (t h)"), ACT.Exp).then_inc(s_wt, 1)

            def store_sums(j, q, b):
                act.wait_ge(s_acc, GI * (j + 1))
                act.dma_start(sums_d[bass.ds(GI * P * j, GI * P), :].rearrange("(i p) c -> p i c", p=P),
                              acc[:, b, :, :]).then_inc(s_sums[b], 16)

            casts(*turn(0, 0))
            casts(*turn(0, 1))

            def body(trip, k, back=True, prep=True):
                st_copies(*turn(trip, k))
                alphas(*turn(trip, k))
                if prep:
                    casts(*turn(trip, k + 2))
                weights(*turn(trip, k))
                if back:
                    store_sums(*turn(trip, k - 1))

            body(0, 0, back=False)
            for k in (1, 2, 3):
                body(0, k)
            with act.Fori(1, TRIPS) as trip:
                for k in (1, 2, 3):
                    body(trip, k)
            body(TRIPS, 1, prep=False)
            body(TRIPS, 2, prep=False)
            store_sums(*turn(TRIPS, 2))

            act.sem_inc(s_bank, 4)
            act.wait_ge(s_ew, 16 * 23)

            def negative_exp(g):
                act.wait_ge(s_neg, g + 1)
                nc.scalar.activation(XL[:, 1, :, :], XL[:, 1, :, :], ACT.Exp).then_inc(s_exp, 1)

            def deviation(done):
                act.wait_ge(s_var4, done)
                nc.scalar.activation(st_d[:, :], st_m[:, :, 1], ACT.Sqrt, bias=eps[:, 0:1]).then_inc(s_sd4, 1)

            def transposed(g, b):
                blocks = XT[:, b, :, :].rearrange("p c (t e) -> p (c t) e", e=P)
                for r in range(4):
                    n = min(4, 2 * TG - 4 * r)
                    act.wait_ge(s_tp4, 4 * g + r + 1)
                    nc.scalar.copy(blocks[:, 4 * r:4 * r + n, :], (b6, b7)[r % 2][:, 0:n * P]
                                   .rearrange("p (t e) -> p t e", e=P)).then_inc(s_xt4, 1)

            def layer(g, b, n, out, bias):
                act.wait_ge(s_lay, NLAY * g + n + 1)
                nc.scalar.activation(out, lay_bank(b, n), ACT.Relu, bias=bias).then_inc(s_bank, 1)

            def router(g, b):
                for hf in range(2):
                    layer(g, b, hf, rhT[:, hf * HT:(hf + 1) * HT], RB1[:, 0:1])
                act.wait_ge(s_lsub, g + 1)
                nc.scalar.activation(lgs[:, :, :], lgs[:, :, :], ACT.Exp).then_inc(s_lexp, 1)
                act.wait_ge(s_tdif, g + 1)
                nc.scalar.activation(tex[:, :], tdif[:, :], ACT.Exp).then_inc(s_tex, 1)

            def hidden(g, b, e, lay):
                out = (h1T, h2T)[lay]
                for m in range(2):
                    for hf in range(2):
                        layer(g, b, 2 + 8 * e + 4 * lay + 2 * m + hf, out[:, m, hf * HT:(hf + 1) * HT],
                              EB[:, lay, e, m:m + 1])

            def node_body(g, b, ahead=True):
                router(g, b)
                for e in range(NX):
                    hidden(g, b, e, 0)
                    hidden(g, b, e, 1)
                    if ahead and e == 0:
                        negative_exp(g + 1)
                    if ahead and e in (1, 2):
                        deviation(2 * g + 2 + e)
                    if ahead and e == 4:
                        transposed(g + 1, 1 - b)

            negative_exp(0)
            deviation(1)
            deviation(2)
            transposed(0, 0)
            for g in range(2):
                node_body(g, g)
            with act.Fori(1, (NTG - 1) // 2) as trip:
                for b in range(2):
                    node_body(2 * trip + b, b)
            node_body(NTG - 1, 0, ahead=False)

        @block.tensor
        def _(pe):
            pe.wait_ge(s_const, 15)
            pe.wait_ge(s_below, 1)
            pe.matmul(b0[0:NW + 1, 0:1], below[:, :], ones[:, 0:1], start=True, stop=True).then_inc(s_rowcnt, 1)
            pe.wait_ge(s_wst, 1)
            pe.matmul(b1[0:NW, 0:1], diffm[:, :], wst[:, :], start=True, stop=True).then_inc(s_wcnt, 1)
            pe.wait_ge(s_nit, 1)
            pe.matmul(b2[0:NW, 0:1], before[:, :], nit[:, :], start=True, stop=True).then_inc(s_i0, 1)
            pe.wait_ge(s_diagl, 1)
            pe.matmul(b3[:, 0:NI], w128[:, :], oneh[:, :], start=True, stop=True)
            pe.matmul(b4[0:1, 0:NI], dcol[:, :], oneh[:, :], start=True, stop=True)
            pe.matmul(b5[:, 0:NW], ones[0:NW, :], diagl[:, :], start=True, stop=True).then_inc(s_lists, 1)

            def node_tile(n, b):
                pe.wait_ge(s_xn, n + 1)
                at_least(pe, s_xt, n)
                for c in range(2):
                    last_ = pe.transpose(b0[:, c * P:(c + 1) * P],
                                         xn_s[:, b, c * P:(c + 1) * P], ident[:, :])
                last_.then_inc(s_xtp, 1)
                pe.wait_ge(s_xt, n + 1)
                at_least(pe, s_hrow, n - 1)
                for c in range(2):
                    last_ = pe.matmul((b1, b2)[b][:, 0:ROW + H], xnT[:, b, c, :], Wcat[:, c, :],
                                      start=(c == 0), stop=(c == 1))
                last_.then_inc(s_hp, 1)

            pe.wait_ge(s_wcat, 2)
            for n in range(3):
                node_tile(n, n % 2)
            with pe.Fori(1, NW // 2) as trip:
                for k in (1, 2):
                    node_tile(2 * trip + k, k % 2)
            pe.wait_ge(s_hrow, NW)

            def prepare(j, q, b):
                pe.wait_ge(s_cast, 2 * (j + 1) - 1)
                at_least(pe, s_prep, j)
                pe.wait_ge(s_rend, j + 1)
                apart(pe)
                for n, o in ((0, erowf[:, 0:P]), (1, erowf[:, P:2 * P]), (2, erend[:, :])):
                    last_ = pe.transpose(idx_ps[:, n, :], o, ident[0:GT, 0:GT])
                last_.then_inc(s_idxp, 1)

            def transpose_one_hot(j, q, b):
                pe.wait_ge(s_S, j + 1)
                for i in range(GI):
                    at_least(pe, s_st, GI * j + i - 1)
                    for k in range(IT):
                        last_ = pe.transpose((b5, b6)[i % 2][:, k * P:(k + 1) * P], S[:, b, IT * i + k, :], ident[:, :])
                    last_.then_inc(s_stp, 1)

            def a_src_rows(j, q, b):
                pe.wait_ge(s_gath[b], GT * 16 * (q + 1))
                at_least(pe, s_scan, j)
                a_src = G[:, b, :, :].rearrange("p t (h c) -> p (t h) c", h=H)[:, :, C]
                for k in range(IT):
                    last_ = pe.transpose(b0[0:GI * H, k * P:(k + 1) * P], 
                                         a_src[:, k * GI * H:(k + 1) * GI * H], ident[:, :])
                last_.then_inc(s_sT, 1)

            def maxima_back(j, q, b):
                pe.wait_ge(s_scan, j + 1)
                at_least(pe, s_Fe, 2 * j)
                apart(pe)
                for k in range(IT):
                    last_ = pe.transpose(b1[:, k * GI * H:(k + 1) * GI * H], F[:, k * P:(k + 1) * P],
                                         ident[0:GI * H, 0:GI * H])
                last_.then_inc(s_FP, 1)

            def node_maxima(j, q, b):
                pe.wait_ge(s_Fe, 2 * (j + 1))
                at_least(pe, s_R, j)
                for i in range(GI):
                    for k in range(IT):
                        last_ = pe.matmul(mt_ps[:, i, :], S[:, b, IT * i + k, :], Fe[:, IT * i + k, :],
                                          start=(k == 0), stop=(k == IT - 1))
                last_.then_inc(s_mt, 1)

            def expand(j, q, b):
                pe.wait_ge(s_st, GI * (j + 1))
                pe.wait_ge(s_R, j + 1)
                pe.wait_ge(s_eld[b], 4 * GI * 16 * (q + 1))
                at_least(pe, s_df, j)
                for t in range(GT):
                    last_ = pe.matmul(ex_ps[:, slot(t // IT, t % IT), :], ST[:, t, :], R[:, b, 1 + t // IT, :], start=True, stop=True)
                last_.then_inc(s_ex, 1)

            def sum_item(j, q, b, i):
                pe.wait_ge(s_msg, GI * j + i + 1)
                at_least(pe, s_acc, GI * j + max(i - 1, 0))
                for k in range(IT):
                    last_ = pe.matmul((b3, b4)[i % 2][:, 0:ROW], S[:, b, IT * i + k, :], G[:, b, slot(i, k), :],
                                      start=(k == 0), stop=(k == IT - 1))
                last_.then_inc(s_pm, 1)

            prepare(*turn(0, 0))
            prepare(*turn(0, 1))

            def body(trip, k, back=True, prep=True):
                now, ago = turn(trip, k), turn(trip, k - 1)
                transpose_one_hot(*now)
                if back:
                    sum_item(*ago, 0)
                a_src_rows(*now)
                if back:
                    sum_item(*ago, 1)
                maxima_back(*now)
                node_maxima(*now)
                if back:
                    sum_item(*ago, 2)
                    sum_item(*ago, 3)
                if prep:
                    prepare(*turn(trip, k + 2))
                expand(*now)

            body(0, 0, back=False)
            for k in (1, 2, 3):
                body(0, k)
            with pe.Fori(1, TRIPS) as trip:
                for k in (1, 2, 3):
                    body(trip, k)
            body(TRIPS, 1, prep=False)
            body(TRIPS, 2, prep=False)
            for i in range(GI):
                sum_item(*turn(TRIPS, 2), i)

            pe.wait_ge(s_ew, 16 * 23)
            pe.wait_ge(s_acc, GI * NG)

            def transposes(g, b):
                pe.wait_ge(s_xn4, g + 1)
                for r in range(4):
                    at_least(pe, s_xt4, 4 * g + r - 1)
                    for n in range(4 * r, min(4 * r + 4, 2 * TG)):
                        c, t = n // TG, n % TG
                        one = pe.transpose((b6, b7)[r % 2][:, (n % 4) * P:(n % 4 + 1) * P],
                                           XL[:, 1, t, c * P:(c + 1) * P], ident[:, :])
                    one.then_inc(s_tp4, 1)

            def layer(g, b, n, weights, x, hf):
                pe.wait_ge(s_bank, NLAY * g + n + 1)
                for c in range(2):
                    one = pe.matmul(lay_bank(b, n), weights(c), x[:, c, hf * HT:(hf + 1) * HT],
                                    start=(c == 0), stop=(c == 1))
                one.then_inc(s_lay, 1)

            def router(g, b):
                pe.wait_ge(s_xt4, 4 * (g + 1))
                for hf in range(2):
                    layer(g, b, hf, lambda c: RW1[:, c, :], XT[:, b, :, :], hf)
                pe.wait_ge(s_bank, NLAY * g + 2 + 4)
                for t in range(TG):
                    one = pe.matmul(lg_ps[:, t, :], rhT[:, t * P:(t + 1) * P], RW2[:, :], start=True, stop=True)
                one.then_inc(s_lg, 1)

            def hidden(g, b, e, lay):
                w, x = ((EW1, XT[:, b, :, :]), (EW2, h1T))[lay]
                if lay:
                    pe.wait_ge(s_bank, NLAY * g + 2 + 8 * e + 4 + 4)
                for m in range(2):
                    for hf in range(2):
                        layer(g, b, 2 + 8 * e + 4 * lay + 2 * m + hf,
                              lambda c: w[:, e, c, m * P:(m + 1) * P], x, hf)

            def to_add(g, b, n, pairs):
                at_least(pe, s_comb, NCOMB * g + max(n - 1, 0))
                for k, (l, r) in enumerate(pairs):
                    one = pe.matmul(eo_bank(b, n), l, r, start=(k == 0), stop=(k == len(pairs) - 1))
                one.then_inc(s_eo, 1)

            def expert_bias(g, b):
                pe.wait_ge(s_coef, g + 1)
                for t in range(TG):
                    one = pe.transpose((b6, b7)[t // 4][0:NX, (t % 4) * P:(t % 4 + 1) * P], coef[:, t, :], ident[:, :])
                one.then_inc(s_cT, 1)
                pe.wait_ge(s_coefT, 2 * (g + 1))
                for t in range(TG):
                    to_add(g, b, t, [(coefT[:, t * P:(t + 1) * P], EB3[:, :])])

            def expert_out(g, b, e):
                pe.wait_ge(s_bank, NLAY * g + 2 + 8 * (e + 1) + 4)
                for t in range(TG):
                    to_add(g, b, TG * (e + 1) + t,
                           [(h2T[:, c, t * P:(t + 1) * P], EW3[:, e, c, :]) for c in range(2)])

            def node_body(g, b, ahead=True):
                router(g, b)
                hidden(g, b, 0, 0)
                expert_bias(g, b)
                hidden(g, b, 0, 1)
                for e in range(1, NX):
                    hidden(g, b, e, 0)
                    expert_out(g, b, e - 1)
                    hidden(g, b, e, 1)
                    if ahead and e == 4:
                        transposes(g + 1, 1 - b)
                expert_out(g, b, NX - 1)

            transposes(0, 0)
            for g in range(2):
                node_body(g, g)
            with pe.Fori(1, (NTG - 1) // 2) as trip:
                for b in range(2):
                    node_body(2 * trip + b, b)
            node_body(NTG - 1, 0, ahead=False)


_IN = {'W': 'L0_gnn_W', 'att_src': 'L0_gnn_att_src', 'att_dst': 'L0_gnn_att_dst', 'bias': 'L0_gnn_bias',
       'ln_scale': 'L0_gnn_ln_scale', 'ln_bias': 'L0_gnn_ln_bias', 'rw1': 'L0_ffn_router_w1',
       'rb1': 'L0_ffn_router_b1', 'rw2': 'L0_ffn_router_w2', 'rb2': 'L0_ffn_router_b2',
       'ew1': 'L0_ffn_expert_w1', 'eb1': 'L0_ffn_expert_b1', 'ew2': 'L0_ffn_expert_w2',
       'eb2': 'L0_ffn_expert_b2', 'ew3': 'L0_ffn_expert_w3', 'eb3': 'L0_ffn_expert_b3'}


def kernel(**inputs):
    import numpy as np
    import concourse.bacc as bacc
    from concourse.bass_utils import run_bass_kernel_spmd

    x = np.zeros((NPAD, D), np.float32)
    x[:N] = inputs['x']
    src = np.zeros((LE,), np.int32)
    src[:NE] = inputs['src']
    dst = np.full((LE + 2,), NPAD, np.int32)
    dst[0] = -1
    dst[1:NE + 1] = inputs['dst']
    given = {'x': x, 'src': src, 'dst': dst}
    for name, full in _IN.items():
        given[name] = np.ascontiguousarray(inputs[full])

    nc = bacc.Bacc("TRN2", target_bir_lowering=False, num_devices=1)
    io = {name: nc.dram_tensor(f"in_{name}", a.shape, mybir.dt.from_np(a.dtype), kind="ExternalInput").ap()
          for name, a in given.items()}
    io['out'] = nc.dram_tensor("out_x", (N, D), F32, kind="ExternalOutput").ap()
    build(nc, io)
    r = run_bass_kernel_spmd(nc, [{f"in_{name}": a for name, a in given.items()}], core_ids=[0])
    return r.results[0]["out_x"]
```

```python
from contextlib import ExitStack

import concourse.bass as bass
from concourse import mybir

ALU = mybir.AluOpType
ACT = mybir.ActivationFunctionType
AX = mybir.AxisListType
F32 = mybir.dt.float32
BF16 = mybir.dt.bfloat16
I32 = mybir.dt.int32
U32 = mybir.dt.uint32

P = 128
N = 6250
NE = 206250
D = 256
H = 8
C = D // H
HC = C + 1
ROW = H * HC
NW = -(-N // P)
NPAD = NW * P
EPP = -(-NE // P)
IT = 4
IE = IT * P
GI = 4
GT = GI * IT
HG = GT // 2
NG_MIN = -(-(NE // IE + NW) // GI)
TRIPS = -(-(NG_MIN - 3) // 3)
NG = 3 * TRIPS + 3
NI = NG * GI
LE = NI * IE
NX = 6
RH = 128
BIG = 1e30
SLOPE = 0.2
EPS = 1e-5
TG = 7
NTG = NW // TG
TOK = TG * P
HT = TOK // 2


class Links:

    def __init__(self, engine, sem):
        self.engine, self.sem, self.n, self.trip, self.per_trip = engine, sem, 0, None, 0

    def mark(self, ins):
        ins.then_inc(self.sem, 1)
        self.n += 1
        return self.n if self.trip is None else self.trip * self.per_trip + self.n

    def need(self, mark):
        self.engine.wait_ge(self.sem, mark)

    def link(self, ins):
        self.need(self.mark(ins))

    def enter(self, trip, per_trip):
        self.n -= per_trip
        self.trip, self.per_trip, self.start = trip, per_trip, self.n

    def leave(self, trips):
        assert self.n - self.start == self.per_trip, (self.n - self.start, self.per_trip)
        self.n += self.per_trip * trips
        self.trip = None


def at_least(engine, sem, value):
    if not (isinstance(value, int) and value <= 0):
        engine.wait_ge(sem, value)


def turn(trip, k):
    return 3 * trip + k, trip + k // 3, k % 3


def build(nc, io):
    with ExitStack() as ctx:
        def sb(name, shape, dt=F32):
            return ctx.enter_context(nc.sbuf_tensor(name, shape, dt))

        def ps(name, shape):
            return ctx.enter_context(nc.psum_tensor(name, shape, F32))

        def sem(name):
            return ctx.enter_context(nc.semaphore(name))

        x_d, src_d, dst_d = io["x"], io["src"], io["dst"]
        out_d = io["out"]
        rows_d = nc.dram_tensor("rows_d", (NPAD, ROW), F32).ap()
        adst_d = nc.dram_tensor("adst_d", (NPAD, H), F32).ap()
        xn_d = nc.dram_tensor("xn_d", (NPAD, D), F32).ap()
        sums_d = nc.dram_tensor("sums_d", (NI * P, ROW), F32).ap()

        arena = sb("arena", [P, 3 * GT * ROW])
        X = arena[:, 0:NW * D].rearrange("p (t d) -> p t d", t=NW)
        G = arena[:, :].rearrange("p (b t c) -> p b t c", b=3, t=GT)
        slot = lambda i, k: GI * k + i
        S = sb("S", [P, 3, GT, P])
        S16 = sb("S16", [P, 3, GT, P], BF16)
        ST16 = sb("ST16", [P, GT, P], BF16)
        ident = sb("ident", [P, P])
        ident16 = sb("ident16", [P, P], BF16)
        ones = sb("ones", [P, P])
        lane = sb("lane", [P, P])
        lane16 = sb("lane16", [P, P], BF16)
        lane_p = sb("lane_p", [P, 1])
        item_end = sb("item_end", [P, GT])
        winb = sb("winb", [P, NI])
        reset = sb("reset", [P, NI])
        table = sb("table", [1, NI, 2], I32)
        sums_idx = sb("sums_idx", [P, NW], U32)

        eps = sb("eps", [P, 1])

        last_i = sb("last_i", [P, 1], I32)
        last = sb("last", [P, 1])
        thr = sb("thr", [P, NW + 1])
        thr_p = sb("thr_p", [NW + 1, 1])
        below = sb("below", [P, NW + 1])
        rowno = sb("rowno", [NW + 1, 1])
        rowno_u = sb("rowno_u", [NW + 1, 1], U32)
        found = S[0:NW + 1, 0, :, :].rearrange("p t e -> p (t e)")[:, 0:EPP].bitcast(I32)
        less = S[0:NW + 1, 1, :, :].rearrange("p t e -> p (t e)")[:, 0:EPP]
        cnt = sb("cnt", [NW + 1, 1])
        wst = sb("wst", [NW + 1, 1])
        diffm = sb("diffm", [NW + 1, NW])
        before = sb("before", [NW, NW])
        tailc = sb("tailc", [NW, 1])
        nit_i = sb("nit_i", [NW, 2], I32)
        nit = sb("nit", [NW, 1])
        i0 = sb("i0", [NW, 1])
        i1 = sb("i1", [NW, 1])
        i1t = sb("i1t", [NW, 1])
        dcol = sb("dcol", [NW, 1])
        diagl = sb("diagl", [NW, NW])
        iota_i = sb("iota_i", [NW, NI])
        ge = sb("ge", [NW, NI])
        oneh = sb("oneh", [NW, NI])
        w128 = sb("w128", [NW, P])

        W_s = sb("W_s", [P, 2, D])
        att = sb("att", [P, 2, D])
        prod = sb("prod", [P, D])
        Wcat = sb("Wcat", [P, 2, ROW + H])
        wa = sb("wa", [P, 2, 2, H])
        stat = sb("stat", [P, TG, 6])
        mv = sb("mv", [P, 2, TG, 2])
        sd = sb("sd", [P, 2, TG])
        rs = sb("rs", [P, 2, TG])
        xnT = sb("xnT", [P, 2, 2, P])
        flat_S = S[:, :, :, :].rearrange("p b t e -> p (b t e)")
        flat_S16 = S16[:, :, :, :].rearrange("p b t e -> p (b t e)").bitcast(F32)
        hrow = [flat_S[:, b * TG * (ROW + H):(b + 1) * TG * (ROW + H)].rearrange("p (t c) -> p t c", t=TG)
                for b in range(2)]
        xn_s = [o.rearrange("p (t d) -> p t d", t=TG)
                for o in (flat_S16[:, 0:TG * D], flat_S[:, 3 * GT * P - TG * D:3 * GT * P])]

        erow = sb("erow", [GT, 3, 2 * P + 1], I32)
        erowf = sb("erowf", [GT, 2 * P + 1])
        erend = sb("erend", [GT, P])
        hrep = sb("hrep", [GI * H, 3, IE + 1], I32)
        hrepf = sb("hrepf", [GI * H, 3, IE + 1])
        gap = sb("gap", [GI * H, IE])
        F = sb("F", [GI * H, IE])
        gidx = sb("gidx", [P, 3, GT], U32)
        dloc = sb("dloc", [P, 3, GT], BF16)
        isend = sb("isend", [P, 3, GT])
        Fe = sb("Fe", [P, GT, H])
        Fr = sb("Fr", [P, GT, H])
        Fe16 = sb("Fe16", [P, GT, 3 * H + 1], BF16)
        t1 = sb("t1", [P, GI])
        mi = sb("mi", [P, GI, H])
        M = sb("M", [P, GI + 1, H])
        xm = sb("xm", [P, GI, H])
        R16 = sb("R16", [P, GI, 3, 2 * H], BF16)
        Rr = sb("Rr", [P, GI, 2 * H])
        R = sb("R", [P, 3, GI + 1, 2 * H])
        da = sb("da", [P, GI, H])
        alpha = sb("alpha", [P, 3, GI, H])
        z = sb("z", [P, GT, H])
        lz = sb("lz", [P, GT, H])
        df = sb("df", [P, GT, H])
        scaled = sb("scaled", [P, ROW])
        acc = sb("acc", [P, 3, GI, ROW])

        b0 = ps("b0", [P, 512])
        b1 = ps("b1", [P, 512])
        b2 = ps("b2", [P, 512])
        b3 = ps("b3", [P, 512])
        b4 = ps("b4", [P, 512])
        b5 = ps("b5", [P, 512])
        b6 = ps("b6", [P, 512])
        b7 = ps("b7", [P, 512])

        idx_ps = b7[:, 0:3 * GT].rearrange("p (n t) -> p n t", n=3)
        mt_ps = b7[:, 64:64 + GI * (3 * H + 1)].rearrange("p (i h) -> p i h", i=GI)
        ex_ps = b2[:, 0:GT * 2 * H].rearrange("p (t h) -> p t h", t=GT)
        back_ps = b7[:, 2 * P:2 * P + GT * H]
        st_ps = [b[:, :].bitcast(BF16) for b in (b5, b6)]
        sum_bank = lambda j, b, i: (b1, b3, b4)[(GI * b + i) % 3][:, 0:ROW]

        s_const = sem("s_const")
        s_ld = sem("s_ld")
        s_apart = sem("s_apart")
        s_last = sem("s_last")
        s_w = sem("s_w")
        s_x = sem("s_x")
        s_v = sem("s_v")
        s_below = sem("s_below")
        s_rowcnt = sem("s_rowcnt")
        s_rowno = sem("s_rowno")
        s_row = sem("s_row")
        s_wst = sem("s_wst")
        s_wcnt = sem("s_wcnt")
        s_nit = sem("s_nit")
        s_i0 = sem("s_i0")
        s_diagl = sem("s_diagl")
        s_lists = sem("s_lists")
        s_items = sem("s_items")
        s_wcat = sem("s_wcat")
        s_var = sem("s_var")
        s_sd = sem("s_sd")
        s_xn = sem("s_xn")
        s_xtp = sem("s_xtp")
        s_xt = sem("s_xt")
        s_hp = sem("s_hp")
        s_hrow = sem("s_hrow")
        s_hst = [sem(f"s_hst{b}") for b in range(2)]
        s_eld = [sem(f"s_eld{b}") for b in range(3)]
        s_nld = [sem(f"s_nld{b}") for b in range(3)]
        s_cast = sem("s_cast")
        s_rend = sem("s_rend")
        s_idxp = sem("s_idxp")
        s_gidx = sem("s_gidx")
        s_prep = sem("s_prep")
        s_gath = [sem(f"s_gath{b}") for b in range(3)]
        s_S = sem("s_S")
        s_S32 = sem("s_S32")
        s_stp = sem("s_stp")
        s_st = sem("s_st")
        s_sT = sem("s_sT")
        s_gap = sem("s_gap")
        s_scan = sem("s_scan")
        s_FP = sem("s_FP")
        s_Fe = sem("s_Fe")
        s_mt = sem("s_mt")
        s_R = sem("s_R")
        s_R16 = sem("s_R16")
        s_da = sem("s_da")
        s_alpha = sem("s_alpha")
        s_ex = sem("s_ex")
        s_df = sem("s_df")
        s_wt = sem("s_wt")
        s_msg = sem("s_msg")
        s_pm = sem("s_pm")
        s_acc = sem("s_acc")
        s_sums = [sem(f"s_sums{b}") for b in range(3)]

        def carve(space, at, *shape):
            n = 1
            for q in shape:
                n *= q
            names = " ".join("abcd"[:len(shape)])
            sizes = {"abcd"[i]: q for i, q in enumerate(shape[:-1])}
            return space[:, at:at + n].rearrange(f"p ({names}) -> p {names}", **sizes), at + n

        XT, at = carve(arena, 0, 2, 2, TOK)
        X1, at = carve(arena, at, 2, TG, D)
        XL, at = carve(arena, at, 2, TG, D)
        SM, at = carve(arena, at, TG, ROW)
        S_flat = S[:, :, :, :].rearrange("p b t e -> p (b t e)")
        h1T, at = carve(S_flat, 0, 2, TOK)
        h2T, at = carve(S_flat, at, 2, TOK)
        rhT = S_flat[:, at:at + TOK]
        EW1 = sb("EW1", [P, NX, 2, D])
        EW2 = sb("EW2", [P, NX, 2, D])
        EW3 = sb("EW3", [P, NX, 2, D])
        RW1 = sb("RW1", [P, 2, RH])
        RW2 = sb("RW2", [P, NX])
        EB3 = sb("EB3", [NX, D])
        RB1 = sb("RB1", [P, 1])
        EB = sb("EB", [P, 2, NX, 2])
        RB2 = sb("RB2", [P, NX])
        VEC = sb("VEC", [P, 3, D])
        den = sb("den", [P, TG * H])
        rden = sb("rden", [P, TG * H])
        st_s = sb("st_s", [P, TG, 6])
        st_m = sb("st_m", [P, TG, 2])
        st_d = sb("st_d", [P, TG])
        st_r = sb("st_r", [P, TG])
        lgs = sb("lgs", [P, TG, NX])
        lmx = sb("lmx", [P, TG])
        lsum = sb("lsum", [P, TG])
        lrec = sb("lrec", [P, TG])
        prob = sb("prob", [P, TG, 8])
        top = sb("top", [P, TG, 8])
        topi = sb("topi", [P, TG, 8], U32)
        topf = sb("topf", [P, TG, 2])
        tdif = sb("tdif", [P, TG])
        tex = sb("tex", [P, TG])
        ten = sb("ten", [P, TG])
        tw = sb("tw", [P, 2, TG])
        expert = sb("expert", [P, TG, NX])
        c1 = sb("c1", [P, TG, NX])
        c2 = sb("c2", [P, TG, NX])
        coef = sb("coef", [P, TG, NX])
        coefT = sb("coefT", [NX, TOK])
        s_ew = sem("s_ew")
        s_xl = sem("s_xl")
        s_sm = sem("s_sm")
        s_smfree = sem("s_smfree")
        s_neg = sem("s_neg")
        s_exp = sem("s_exp")
        s_var4 = sem("s_var4")
        s_sd4 = sem("s_sd4")
        s_xn4 = sem("s_xn4")
        s_tp4 = sem("s_tp4")
        s_xt4 = sem("s_xt4")
        s_bank = sem("s_bank")
        s_lay = sem("s_lay")
        s_lg = sem("s_lg")
        s_lsub = sem("s_lsub")
        s_lexp = sem("s_lexp")
        s_tdif = sem("s_tdif")
        s_tex = sem("s_tex")
        s_coef = sem("s_coef")
        s_cT = sem("s_cT")
        s_coefT = sem("s_coefT")
        s_eo = sem("s_eo")
        s_comb = sem("s_comb")
        s_out = [sem(f"s_out{b}") for b in range(2)]
        lg_ps = b6[:, 0:TG * NX].rearrange("p (t e) -> p t e", t=TG)
        lay_bank = lambda b, n: (b0, b1, b2, b3)[(NLAY * b + n) % 4][:, 0:HT]
        eo_bank = lambda b, n: (b4, b5)[(NCOMB * b + n) % 2][:, 0:D]
        NLAY = 2 + NX * 8
        NCOMB = TG * (NX + 1)

        def apart(engine):
            engine.sem_inc(s_apart, 1)

        def rows_stored(engine):
            engine.wait_ge(s_hst[0], 48 * (NTG // 2 + 1))
            engine.wait_ge(s_hst[1], 48 * (NTG // 2))

        x_t = x_d.rearrange("(t p) d -> p t d", p=P)
        block = ctx.enter_context(nc.Block())

        @block.sync
        def _(sp):
            dst_pp = dst_d[0:P * EPP].rearrange("(p e) -> p e", p=P)
            with nc.allow_non_contiguous_dma(reason="one number per partition"):
                sp.dma_start(last_i[:, :], dst_pp[:, EPP - 1:EPP]).then_inc(s_last, 16)
            sp.dma_start(W_s[:, :, :], io["W"].rearrange("(c p) n -> p c n", p=P)).then_inc(s_w, 16)
            for n, a in enumerate((io["att_src"], io["att_dst"])):
                sp.dma_start(att[:, n, :], a.rearrange("h c -> (h c)").partition_broadcast(P)).then_inc(s_w, 16)
            for t in range(0, NW, 7):
                sp.dma_start(X[:, t:t + 7, :], x_t[:, t:t + 7, :]).then_inc(s_x, 16)

            for tile, dram in zip((EW1, EW2, EW3), (io["ew1"], io["ew2"], io["ew3"])):
                sp.dma_start(tile[:, :, :, :], dram.rearrange("e (c p) n -> p e c n", p=P)).then_inc(s_ew, 16)
            sp.dma_start(RW1[:, :, :], io["rw1"].rearrange("(c p) n -> p c n", p=P)).then_inc(s_ew, 16)
            sp.dma_start(RW2[:, :], io["rw2"]).then_inc(s_ew, 16)
            sp.dma_start(EB3[:, :], io["eb3"]).then_inc(s_ew, 16)
            with nc.allow_non_contiguous_dma(reason="small biases, one per partition"):
                sp.dma_start(RB1[:, :], io["rb1"].rearrange("(p a) -> p a", a=1)).then_inc(s_ew, 16)
                for n, dram in enumerate((io["eb1"], io["eb2"])):
                    for e in range(NX):
                        sp.dma_start(EB[:, n, e, :], dram[e].rearrange("(c p) -> p c", p=P)).then_inc(s_ew, 16)
            sp.dma_start(RB2[:, :], io["rb2"].partition_broadcast(P)).then_inc(s_ew, 16)
            for n, dram in enumerate((io["bias"], io["ln_scale"], io["ln_bias"])):
                sp.dma_start(VEC[:, n, :], dram.partition_broadcast(P)).then_inc(s_ew, 16)

            def store_rows(g, b):
                sp.wait_ge(s_hrow, TG * (g + 1))
                tiles = lambda dram: dram[bass.ds(g * TOK, TOK), :].rearrange("(t p) c -> p t c", p=P)
                sp.dma_start(tiles(rows_d), hrow[b][:, :, 0:ROW]).then_inc(s_hst[b], 16)
                sp.dma_start(tiles(adst_d), hrow[b][:, :, ROW:ROW + H]).then_inc(s_hst[b], 16)
                sp.dma_start(tiles(xn_d), xn_s[b][:, :, :]).then_inc(s_hst[b], 16)

            for g in range(3):
                store_rows(g, g % 2)
            with sp.Fori(1, NTG // 2) as trip:
                for k in (1, 2):
                    store_rows(2 * trip + k, k % 2)
            rows_stored(sp)

            sp.wait_ge(s_items, 1)

            def load_edges(j, q, b):
                at_least(sp, s_cast, 2 * (j - 2))
                for i in range(GI):
                    start = sp.value_load(table[0:1, bass.ds(GI * j + i, 1), 0], min_val=0, max_val=LE - IE)
                    sp.dma_start(erow[IT * i:IT * i + IT, b, 0:P],
                                 src_d[bass.ds(start, IE)].rearrange("(k e) -> k e", k=IT)).then_inc(s_eld[b], 16)
                    d = dst_d[bass.ds(start + 1, IE + 1)]
                    sp.dma_start(erow[IT * i:IT * i + IT, b, P:2 * P + 1],
                                 bass.AP(d.tensor, d.offset, [[P, IT], [1, P + 1]])).then_inc(s_eld[b], 16)
                    sp.dma_start(hrep[H * i:H * i + H, b, :],
                                 dst_d[bass.ds(start, IE + 1)].partition_broadcast(H)).then_inc(s_eld[b], 16)

            def load_nodes(j, q, b):
                at_least(sp, s_ex, j - 2)
                for i in range(GI):
                    node = sp.value_load(table[0:1, bass.ds(GI * j + i, 1), 1], min_val=0, max_val=NPAD - P)
                    sp.dma_start(R[:, b, 1 + i, 0:H], adst_d[bass.ds(node, P), :]).then_inc(s_nld[b], 16)

            for k in range(6):
                load_edges(*turn(0, k))
                if k:
                    load_nodes(*turn(0, k - 1))
            with sp.Fori(2, NG // 3) as trip:
                for k in range(3):
                    load_edges(*turn(trip, k))
                    load_nodes(*turn(trip, k - 1))
            load_nodes(*turn(NG // 3, -1))

            sp.wait_ge(s_pm, GI * NG)

            def load_node_group(g):
                at_least(sp, s_tp4, 4 * g)
                nodes = bass.ds(g * TOK, TOK)
                for n, dram in enumerate((x_d, xn_d)):
                    sp.dma_start(XL[:, n, :, :], dram[nodes, :].rearrange("(t p) d -> p t d", p=P)).then_inc(s_xl, 16)

            def store_nodes(g, b):
                sp.wait_ge(s_comb, NCOMB * (g + 1))
                sp.dma_start(out_d[bass.ds(g * TOK, TOK), :].rearrange("(t p) d -> p t d", p=P),
                             X1[:, b, :, :]).then_inc(s_out[b], 16)

            load_node_group(0)
            for g in range(2):
                load_node_group(g + 1)
                store_nodes(g, g)
            with sp.Fori(1, (NTG - 1) // 2) as trip:
                for b in range(2):
                    load_node_group(2 * trip + b + 1)
                    store_nodes(2 * trip + b, b)
            sp.wait_ge(s_comb, NCOMB * NTG)
            first, full = (NTG - 1) * TOK, N // P - (NTG - 1) * TG
            sp.dma_start(out_d[first:first + full * P, :].rearrange("(t p) d -> p t d", p=P),
                         X1[:, 0, 0:full, :]).then_inc(s_out[0], 16)
            sp.dma_start(out_d[first + full * P:N, :], X1[0:N % P, 0, full, :]).then_inc(s_out[0], 16)
            sp.wait_ge(s_out[0], 16 * ((NTG + 1) // 2 + 1))
            sp.wait_ge(s_out[1], 16 * (NTG // 2))

        @block.gpsimd
        def _(pool):
            iota = lambda o, pat, m: pool.iota(o, pattern=pat, base=0, channel_multiplier=m,
                                               allow_small_or_imprecise_dtypes=True)
            pool.memset(ident[:, :], 0.0).then_inc(s_ld, 1)
            pool.memset(diffm[:, :], 0.0).then_inc(s_ld, 1)
            pool.memset(before[:, :], 1.0).then_inc(s_ld, 1)
            pool.memset(tailc[:, :], 0.0).then_inc(s_ld, 1)
            pool.memset(item_end[:, :], 0.0).then_inc(s_ld, 1)
            pool.memset(ones[:, :], 1.0).then_inc(s_const, 1)
            pool.memset(eps[:, :], EPS).then_inc(s_const, 1)
            iota(thr[:, :], [[P, NW + 1]], 0).then_inc(s_const, 1)
            iota(thr_p[:, :], [[0, 1]], P).then_inc(s_const, 1)
            iota(lane[:, :], [[1, P]], 0).then_inc(s_const, 1)
            iota(lane_p[:, :], [[0, 1]], 1).then_inc(s_const, 1)
            iota(iota_i[:, :], [[1, NI]], 0).then_inc(s_const, 1)
            iota(w128[:, :], [[0, P]], P).then_inc(s_const, 1)
            iota(expert[:, :, :], [[0, TG], [1, NX]], 0).then_inc(s_const, 1)
            pool.memset(prob[:, :, :], -1.0).then_inc(s_const, 1)

            def select(m, pat, base, mult, op, fill):
                return pool.affine_select(out=m, in_=m, compare_op=op, fill=fill, base=base,
                                          pattern=pat, channel_multiplier=mult)

            pool.wait_ge(s_ld, 5)
            select(ident[:, :], [[-1, P]], 0, 1, ALU.not_equal, 1.0).then_inc(s_const, 1)
            select(before[:, :], [[1, NW]], 0, -1, ALU.is_gt, 0.0).then_inc(s_const, 1)
            select(tailc[:, :], [[0, 1]], -(NW - 1), 1, ALU.not_equal, 1e6).then_inc(s_const, 1)
            e = item_end[:, :].rearrange("p (i k) -> p i k", k=IT)
            select(e, [[0, GI], [1, IT]], -(IT - 1 + P - 1), 1, ALU.not_equal, 1.0).then_inc(s_const, 1)
            select(diffm[:, :], [[-1, NW]], 0, 1, ALU.not_equal, -1.0).then_inc(s_ld, 1)
            pool.wait_ge(s_ld, 6)
            select(diffm[:, :], [[-1, NW]], -1, 1, ALU.not_equal, 1.0).then_inc(s_const, 1)

            pool.wait_ge(s_rowno, 1)
            dst_pp = dst_d[0:P * EPP].rearrange("(p e) -> p e", p=P)
            pool.indirect_dma_start(found, None, dst_pp,
                                    bass.IndirectOffsetOnAxis(ap=rowno_u[:, 0:1], axis=0)).then_inc(s_row, 16)

            rows_stored(pool)

            def gather(j, q, b):
                pool.wait_ge(s_gidx, j + 1)
                for t in range(GT):
                    if t % IT == 0:
                        at_least(pool, s_pm, GI * (j - 3) + t // IT + 1)
                        apart(pool)
                    pool.indirect_dma_start(G[:, b, slot(t // IT, t % IT), :], None, rows_d,
                                            bass.IndirectOffsetOnAxis(ap=gidx[:, b, t:t + 1], axis=0)
                                            ).then_inc(s_gath[b], 16)

            for k in range(3):
                gather(*turn(0, k))
            with pool.Fori(1, NG // 3) as trip:
                for k in range(3):
                    gather(*turn(trip, k))

            for b in range(3):
                pool.wait_ge(s_sums[b], 16 * (NG // 3))
            for g in range(NTG):
                at_least(pool, s_smfree, g)
                for t in range(TG):
                    pool.indirect_dma_start(SM[:, t, :], None, sums_d,
                                            bass.IndirectOffsetOnAxis(ap=sums_idx[:, TG * g + t:TG * g + t + 1],
                                                                      axis=0)).then_inc(s_sm, 16)

        @block.vector
        def _(dve):
            v = Links(dve, s_v)
            dve.wait_ge(s_last, 16)
            dve.wait_ge(s_const, 15)
            v.link(dve.tensor_copy(last[:, :], last_i[:, :]))
            dve.tensor_scalar(below[:, :], thr[:, :], last[:, 0:1], None, ALU.is_gt).then_inc(s_below, 1)
            dve.wait_ge(s_rowcnt, 1)
            v.link(dve.tensor_scalar(rowno[:, :], b0[0:NW + 1, 0:1], float(P - 1), None, ALU.min))
            dve.tensor_copy(rowno_u[:, :], rowno[:, :]).then_inc(s_rowno, 1)
            dve.wait_ge(s_row, 16)
            v.link(dve.tensor_scalar(less, found, thr_p[:, 0:1], None, ALU.is_lt))
            v.link(dve.tensor_reduce(cnt[:, :], less, AX.X, ALU.add))
            v.link(dve.scalar_tensor_tensor(out=wst[:, :], in0=rowno[:, :], scalar=float(EPP), in1=cnt[:, :],
                                            op0=ALU.mult, op1=ALU.add))
            dve.tensor_scalar(wst[:, :], wst[:, :], -1.0, None, ALU.add).then_inc(s_wst, 1)
            dve.wait_ge(s_wcnt, 1)
            v.link(dve.tensor_scalar(nit_i[:, 0:1], b1[0:NW, 0:1], float(IE - 1), None, ALU.add))
            v.link(dve.tensor_scalar(nit_i[:, 1:2], nit_i[:, 0:1], IE.bit_length() - 1, None,
                                     ALU.arith_shift_right))
            dve.tensor_scalar(nit[:, :], nit_i[:, 1:2], 1.0, None, ALU.max).then_inc(s_nit, 1)
            dve.wait_ge(s_i0, 1)
            v.link(dve.tensor_copy(i0[:, :], b2[0:NW, 0:1]))
            v.link(dve.tensor_tensor(i1t[:, :], i0[:, :], nit[:, :], ALU.add))
            v.link(dve.tensor_tensor(i1[:, :], i1t[:, :], tailc[:, :], ALU.add))
            v.link(dve.tensor_scalar(ge[:, :], iota_i[:, :], i0[:, 0:1], None, ALU.is_ge))
            v.link(dve.scalar_tensor_tensor(out=oneh[:, :], in0=iota_i[:, :], scalar=i1[:, 0:1], in1=ge[:, :],
                                            op0=ALU.is_lt, op1=ALU.mult))
            v.link(dve.scalar_tensor_tensor(out=dcol[:, :], in0=i0[:, :], scalar=-float(IE), in1=wst[0:NW, :],
                                            op0=ALU.mult, op1=ALU.add))
            v.link(dve.tensor_scalar(i1t[:, :], i1[:, :], float(NI), -1.0, ALU.min, ALU.add))
            dve.tensor_scalar(diagl[:, :], ident[0:NW, 0:NW], i1t[:, 0:1], None, ALU.mult).then_inc(s_diagl, 1)
            dve.wait_ge(s_lists, 1)
            v.link(dve.tensor_copy(winb[:, :], b3[:, 0:NI]))
            dve.tensor_copy(table[0:1, :, 1], winb[0:1, :])
            dve.scalar_tensor_tensor(out=table[0:1, :, 0], in0=iota_i[0:1, :], scalar=float(IE),
                                     in1=b4[0:1, 0:NI], op0=ALU.mult, op1=ALU.add).then_inc(s_items, 1)
            v.link(dve.memset(reset[:, 0:1], -BIG))
            v.link(dve.tensor_tensor(reset[:, 1:NI], winb[:, 1:NI], winb[:, 0:NI - 1], ALU.not_equal))
            v.link(dve.tensor_scalar(reset[:, 1:NI], reset[:, 1:NI], -BIG, None, ALU.mult))
            v.link(dve.tensor_scalar(sums_idx[:, :], b5[:, 0:NW], float(P), lane_p[:, 0:1], ALU.mult, ALU.add))

            dve.wait_ge(s_w, 48)
            for c in range(2):
                for n in range(2):
                    v.link(dve.tensor_tensor(prod[:, :], W_s[:, c, :], att[:, n, :], ALU.mult))
                    v.link(dve.tensor_reduce(wa[:, c, n, :], prod[:, :].rearrange("p (h c) -> p h c", h=H),
                                             AX.X, ALU.add))
                heads = Wcat[:, c, 0:ROW].rearrange("p (h c) -> p h c", h=H)
                v.link(dve.tensor_copy(heads[:, :, 0:C], W_s[:, c, :].rearrange("p (h c) -> p h c", h=H)))
                v.link(dve.tensor_copy(heads[:, :, C], wa[:, c, 0, :]))
                dve.tensor_copy(Wcat[:, c, ROW:ROW + H], wa[:, c, 1, :]).then_inc(s_wcat, 1)
            dve.wait_ge(s_x, 16 * NTG)

            def node_group(g, b, used):
                xg = X[:, bass.ds(g * TG, TG), :]
                for t in range(TG):
                    one = dve.bn_stats(stat[:, t, :], xg[:, t, :])
                v.link(one)
                apart(dve)
                for t in range(TG):
                    one = dve.bn_aggr(mv[:, b, t, :], stat[:, t, :])
                one.then_inc(s_var, 1)
                dve.wait_ge(s_sd, g + 1)
                v.link(dve.reciprocal(rs[:, b, :], sd[:, b, :]))
                at_least(dve, s_hst[b], 48 * used)
                for t in range(TG + 1):
                    if t < TG:
                        dve.tensor_scalar(xn_s[b][:, t, :], xg[:, t, :], mv[:, b, t, 0:1], rs[:, b, t:t + 1],
                                          ALU.subtract, ALU.mult).then_inc(s_xn, 1)
                    if t:
                        n = TG * g + t - 1
                        dve.wait_ge(s_xtp, n + 1)
                        at_least(dve, s_hp, n - 1)
                        odd = (b + t - 1) % 2
                        dve.tensor_copy(xnT[:, odd, :, :], (b0, b3)[odd][:, 0:D].rearrange("p (c e) -> p c e", c=2)
                                        ).then_inc(s_xt, 1)

            for g in range(3):
                node_group(g, g % 2, g // 2)
            with dve.Fori(1, NTG // 2) as trip:
                v.enter(trip, 4)
                for k in (1, 2):
                    node_group(2 * trip + k, k % 2, trip + k // 2)
                v.leave(NTG // 2 - 1)

            rows_stored(dve)
            dve.tensor_copy(ident16[:, :], ident[:, :])
            v.link(dve.tensor_copy(lane16[:, :], lane[:, :]))
            v.link(dve.memset(acc[:, 2, GI - 1, :], 0.0))
            v.link(dve.memset(M[:, GI, :], -BIG))
            v.link(dve.memset(R[:, 2, GI, H:2 * H], 0.0))

            def prepare(j, q, b):
                dve.wait_ge(s_cast, 2 * (j + 1) - 1)
                dve.tensor_tensor(erend[:, :], erowf[:, P:2 * P], erowf[:, P + 1:2 * P + 1],
                                  ALU.not_equal).then_inc(s_rend, 1)

            def place(j, q, b):
                dve.wait_ge(s_idxp, j + 1)
                dve.tensor_copy(gidx[:, b, :], idx_ps[:, 0, :]).then_inc(s_gidx, 1)
                items = bass.ds(GI * j, GI)
                dve.tensor_tensor(dloc[:, b, :].rearrange("p (i k) -> p i k", k=IT),
                                         idx_ps[:, 1, :].rearrange("p (i k) -> p i k", k=IT),
                                         winb[:, items].unsqueeze(2).to_broadcast([P, GI, IT]), ALU.subtract)
                dve.tensor_tensor(isend[:, b, :], idx_ps[:, 2, :], item_end[:, :], ALU.max).then_inc(s_prep, 1)

            def one_hot(j, q, b):
                dve.wait_ge(s_prep, j + 1)
                at_least(dve, s_pm, GI * (j - 2))
                dve.tensor_tensor(S16[:, b, :, :], dloc[:, b, :].unsqueeze(2).to_broadcast([P, GT, P]),
                                  lane16[:, :].unsqueeze(1).to_broadcast([P, GT, P]), ALU.is_equal).then_inc(s_S, 1)

            def segment_gaps(j, q, b):
                dve.wait_ge(s_cast, 2 * (j + 1))
                dve.tensor_tensor(gap[:, :], hrepf[:, b, 0:IE], hrepf[:, b, 1:IE + 1], ALU.subtract).then_inc(s_gap, 1)

            def scan(j, q, b):
                dve.wait_ge(s_gap, j + 1)
                dve.wait_ge(s_sT, j + 1)
                dve.tensor_tensor_scan(F[:, :], gap[:, :], b0[0:GI * H, :], -BIG, ALU.add, ALU.max).then_inc(s_scan, 1)

            def ends(j, q, b, between):
                part = lambda n: Fe16[:, :, n * H:(n + 1) * H]
                dve.wait_ge(s_FP, j + 1)
                dve.wait_ge(s_prep, j + 1)
                one = v.mark(dve.tensor_tensor(Fe[:, :, :].rearrange("p (i k) h -> p i k h", k=IT),
                                               back_ps.rearrange("p (k i h) -> p i k h", k=IT, i=GI),
                                               isend[:, b, :].rearrange("p (i k) -> p i k", k=IT).unsqueeze(3)
                                               .to_broadcast([P, GI, IT, H]), ALU.mult))
                dve.tensor_copy(Fe16[:, :, 3 * H], isend[:, b, :])
                v.need(one)
                one = v.mark(dve.tensor_copy(part(0), Fe[:, :, :]))
                between()
                v.need(one)
                v.link(dve.tensor_tensor(Fr[:, :, :], Fe[:, :, :], part(0), ALU.subtract))
                v.link(dve.tensor_copy(part(1), Fr[:, :, :]))
                dve.tensor_tensor(part(2), Fr[:, :, :], part(1), ALU.subtract).then_inc(s_Fe, 1)

            def shifts(j, q, b, between=lambda n: None):
                dve.wait_ge(s_mt, j + 1)
                dve.wait_ge(s_nld[b], GI * 16 * (q + 1))
                dve.tensor_scalar(t1[:, :], mt_ps[:, :, 3 * H], BIG, -BIG, ALU.mult, ALU.add)
                one = v.mark(dve.tensor_reduce(mi[:, :, :], mt_ps[:, :, 0:3 * H].rearrange("p i (n h) -> p i h n", n=3),
                                               AX.X, ALU.add))
                dve.tensor_copy(M[:, 0, :], M[:, GI, :])
                dve.tensor_copy(R[:, b, 0, H:2 * H], R[:, (b + 2) % 3, GI, H:2 * H])
                v.need(one)
                one = v.mark(dve.tensor_tensor(mi[:, :, :], mi[:, :, :],
                                               t1[:, :].unsqueeze(2).to_broadcast([P, GI, H]), ALU.add))
                for i in range(GI):
                    between(i)
                    v.need(one)
                    one = v.mark(dve.scalar_tensor_tensor(out=M[:, i + 1, :], in0=M[:, i, :],
                                                          scalar=reset[:, bass.ds(GI * j + i, 1)],
                                                          in1=mi[:, i, :], op0=ALU.add, op1=ALU.max))
                between(GI)
                v.need(one)
                one = v.mark(dve.tensor_tensor(xm[:, :, :], M[:, 1:GI + 1, :], R[:, b, 1:GI + 1, 0:H], ALU.add))
                between(GI + 1)
                v.need(one)
                dve.scalar_tensor_tensor(out=R[:, b, 1:GI + 1, H:2 * H], in0=xm[:, :, :], scalar=SLOPE,
                                         in1=xm[:, :, :], op0=ALU.mult, op1=ALU.max).then_inc(s_R, 1)
                between(GI + 2)
                dve.wait_ge(s_R, j + 1)
                dve.tensor_tensor(da[:, :, :], R[:, b, 0:GI, H:2 * H], R[:, b, 1:GI + 1, H:2 * H], ALU.subtract)
                one = v.mark(dve.tensor_copy(R16[:, :, 0, :], R[:, b, 1:GI + 1, :]))
                between(GI + 3)
                v.need(one)
                one = v.mark(dve.tensor_tensor(Rr[:, :, :], R[:, b, 1:GI + 1, :], R16[:, :, 0, :], ALU.subtract))
                dve.tensor_tensor(da[:, :, :], da[:, :, :],
                                  reset[:, bass.ds(GI * j, GI)].unsqueeze(2).to_broadcast([P, GI, H]),
                                  ALU.add).then_inc(s_da, 1)
                v.need(one)
                v.link(dve.tensor_copy(R16[:, :, 1, :], Rr[:, :, :]))
                dve.tensor_tensor(R16[:, :, 2, :], Rr[:, :, :], R16[:, :, 1, :], ALU.subtract).then_inc(s_R16, 1)
                between(GI + 4)

            def logits(j, q, b, between=lambda n: None):
                dve.wait_ge(s_ex, j + 1)
                a_src = G[:, b, :, :].rearrange("p t (h c) -> p t h c", h=H)[:, :, :, C]
                one = v.mark(dve.tensor_tensor(z[:, :, :], a_src, ex_ps[:, :, 0:H], ALU.add))
                between(0)
                v.need(one)
                one = v.mark(dve.scalar_tensor_tensor(out=lz[:, :, :], in0=z[:, :, :], scalar=SLOPE,
                                                      in1=z[:, :, :], op0=ALU.mult, op1=ALU.max))
                between(1)
                v.need(one)
                one = v.mark(dve.tensor_tensor(df[:, :, :], lz[:, :, :], ex_ps[:, :, H:2 * H], ALU.subtract))
                between(2)
                v.need(one)
                dve.tensor_scalar(df[:, :, :], df[:, :, :], 0.0, None, ALU.min).then_inc(s_df, 1)

            def message(j, q, b, i):
                dve.wait_ge(s_wt, j + 1)
                g = G[:, b, i:GT:GI, :].rearrange("p t (h c) -> p t h c", h=H)
                dve.tensor_tensor(g[:, :, :, 0:C], g[:, :, :, 0:C], g[:, :, :, C:HC].to_broadcast([P, IT, H, C]),
                                  ALU.mult).then_inc(s_msg, 1)

            def rescale(j, q, b, i):
                dve.wait_ge(s_alpha, j + 1)
                if i == 0:
                    at_least(dve, s_sums[b], 16 * q)
                at_least(dve, s_acc, GI * j + i)
                old = acc[:, (b + 2) % 3, GI - 1, :] if i == 0 else acc[:, b, i - 1, :]
                return v.mark(dve.tensor_tensor(scaled[:, :].rearrange("p (h c) -> p h c", h=H),
                                                old.rearrange("p (h c) -> p h c", h=H),
                                                alpha[:, b, i, :].unsqueeze(2).to_broadcast([P, H, HC]), ALU.mult))

            def add(j, q, b, i, one):
                v.need(one)
                dve.wait_ge(s_pm, GI * j + i + 1)
                dve.tensor_tensor(acc[:, b, i, :], scaled[:, :], sum_bank(j, b, i), ALU.add).then_inc(s_acc, 1)

            def accumulate(j, q, b, i):
                add(j, q, b, i, rescale(j, q, b, i))

            prepare(*turn(0, 0)); place(*turn(0, 0)); one_hot(*turn(0, 0))
            prepare(*turn(0, 1)); place(*turn(0, 1))

            def body(trip, k, back=True, prep=True, ahead=True):
                now, ago, following = turn(trip, k), turn(trip, k - 1), turn(trip, k + 1)
                ends(*now, lambda: prep and prepare(*turn(trip, k + 2)))
                if ahead:
                    one_hot(*following)
                if back:
                    logits(*ago)
                    message(*ago, 0)
                if prep:
                    place(*turn(trip, k + 2))
                if back:
                    for i in range(1, GI):
                        message(*ago, i)
                if ahead:
                    segment_gaps(*following)
                marks = {}

                def old_sums(n):
                    if n == 2 * GI - 1:
                        if ahead:
                            scan(*following)
                    elif back and n == 2 * GI:
                        add(*ago, GI - 1, marks[GI - 1])
                    elif back and n % 2 == 0:
                        marks[n // 2] = rescale(*ago, n // 2)
                    elif back:
                        add(*ago, n // 2, marks[n // 2])

                shifts(*now, old_sums)

            segment_gaps(*turn(0, 0))
            scan(*turn(0, 0))
            body(0, 0, back=False)
            for k in (1, 2, 3):
                body(0, k)
            with dve.Fori(1, TRIPS) as trip:
                v.enter(trip, 3 * (4 + 10 + 3 + 4))
                for k in (1, 2, 3):
                    body(trip, k)
                v.leave(TRIPS - 1)
            body(TRIPS, 1, prep=False)
            body(TRIPS, 2, prep=False, ahead=False)
            logits(*turn(TRIPS, 2))
            for i in range(GI):
                message(*turn(TRIPS, 2), i)
            for i in range(GI):
                accumulate(*turn(TRIPS, 2), i)

            flat = lambda o: o.rearrange("p t d -> p (t d)")
            over_tiles = lambda n: VEC[:, n, :].unsqueeze(1).to_broadcast([P, TG, D])

            def attention_out(g, b):
                dve.wait_ge(s_sm, 16 * TG * (g + 1))
                dve.wait_ge(s_xl, 32 * (g + 1))
                sm = SM[:, :, :].rearrange("p t (h c) -> p (t h) c", h=H)
                v.link(dve.tensor_scalar(den[:, :], sm[:, :, C], 1e-16, None, ALU.add))
                v.link(dve.reciprocal(rden[:, :], den[:, :]))
                at_least(dve, s_out[b], 16 * stored[b])
                dve.tensor_tensor(X1[:, b, :, :].rearrange("p t (h c) -> p (t h) c", h=H), sm[:, :, 0:C],
                                  rden[:, :].unsqueeze(2).to_broadcast([P, TG * H, C]), ALU.mult).then_inc(s_smfree, 1)
                dve.wait_ge(s_smfree, g + 1)
                v.link(dve.tensor_tensor(X1[:, b, :, :], X1[:, b, :, :], over_tiles(0), ALU.add))
                v.link(dve.tensor_tensor(X1[:, b, :, :], X1[:, b, :, :], XL[:, 1, :, :], ALU.add))
                dve.tensor_scalar(XL[:, 1, :, :], X1[:, b, :, :], 0.0, None, ALU.min).then_inc(s_neg, 1)

            def statistics(b):
                for t in range(TG):
                    one = dve.bn_stats(st_s[:, t, :], X1[:, b, t, :])
                v.link(one)
                apart(dve)
                for t in range(TG):
                    one = dve.bn_aggr(st_m[:, t, :], st_s[:, t, :])
                return one

            def elu(g, b):
                dve.wait_ge(s_exp, g + 1)
                v.link(dve.scalar_tensor_tensor(out=flat(X1[:, b, :, :]), in0=flat(XL[:, 1, :, :]), scalar=-1.0,
                                                in1=flat(X1[:, b, :, :]), op0=ALU.add, op1=ALU.max))
                statistics(b).then_inc(s_var4, 1)

            def normalize(out, g, b, done):
                dve.wait_ge(s_sd4, done)
                v.link(dve.reciprocal(st_r[:, :], st_d[:, :]))
                for t in range(TG):
                    one = dve.tensor_scalar(out[:, t, :], X1[:, b, t, :], st_m[:, t, 0:1], st_r[:, t:t + 1],
                                            ALU.subtract, ALU.mult)
                return one

            def first_norm(g, b):
                v.link(normalize(X1[:, b, :, :], g, b, 2 * g + 1))
                v.link(dve.tensor_tensor(X1[:, b, :, :], X1[:, b, :, :], over_tiles(1), ALU.mult))
                v.link(dve.tensor_tensor(X1[:, b, :, :], X1[:, b, :, :], over_tiles(2), ALU.add))
                v.link(dve.tensor_tensor(X1[:, b, :, :], X1[:, b, :, :], XL[:, 0, :, :], ALU.add))
                statistics(b).then_inc(s_var4, 1)

            def second_norm(g, b):
                normalize(XL[:, 1, :, :], g, b, 2 * g + 2).then_inc(s_xn4, 1)

            def route(g, b):
                wide = lambda o, n: o.unsqueeze(2).to_broadcast([P, TG, n])
                dve.wait_ge(s_lg, g + 1)
                v.link(dve.tensor_tensor(lgs[:, :, :], lg_ps, RB2[:, :].unsqueeze(1).to_broadcast([P, TG, NX]), ALU.add))
                v.link(dve.tensor_reduce(lmx[:, :], lgs[:, :, :], AX.X, ALU.max))
                dve.tensor_tensor(lgs[:, :, :], lgs[:, :, :], wide(lmx[:, :], NX), ALU.subtract).then_inc(s_lsub, 1)
                dve.wait_ge(s_lexp, g + 1)
                v.link(dve.tensor_reduce(lsum[:, :], lgs[:, :, :], AX.X, ALU.add))
                v.link(dve.reciprocal(lrec[:, :], lsum[:, :]))
                v.link(dve.tensor_tensor(prob[:, :, 0:NX], lgs[:, :, :], wide(lrec[:, :], NX), ALU.mult))
                apart(dve)
                for t in range(TG):
                    one = dve.max(top[:, t, :], prob[:, t, :])
                v.link(one)
                apart(dve)
                for t in range(TG):
                    one = dve.max_index(topi[:, t, :], top[:, t, :], prob[:, t, :])
                v.link(one)
                dve.tensor_tensor(tdif[:, :], top[:, :, 1], top[:, :, 0], ALU.subtract).then_inc(s_tdif, 1)
                v.link(dve.tensor_copy(topf[:, :, :], topi[:, :, 0:2]))
                v.link(dve.tensor_tensor(c1[:, :, :], expert[:, :, :], wide(topf[:, :, 0], NX), ALU.is_equal))
                v.link(dve.tensor_tensor(c2[:, :, :], expert[:, :, :], wide(topf[:, :, 1], NX), ALU.is_equal))
                dve.wait_ge(s_tex, g + 1)
                v.link(dve.tensor_scalar(ten[:, :], tex[:, :], 1.0, None, ALU.add))
                v.link(dve.reciprocal(tw[:, 0, :], ten[:, :]))
                v.link(dve.tensor_tensor(tw[:, 1, :], tex[:, :], tw[:, 0, :], ALU.mult))
                v.link(dve.tensor_tensor(c1[:, :, :], c1[:, :, :], wide(tw[:, 0, :], NX), ALU.mult))
                v.link(dve.tensor_tensor(c2[:, :, :], c2[:, :, :], wide(tw[:, 1, :], NX), ALU.mult))
                dve.tensor_tensor(coef[:, :, :], c1[:, :, :], c2[:, :, :], ALU.add).then_inc(s_coef, 1)

            def expert_bias(g, b):
                dve.wait_ge(s_cT, g + 1)
                dve.tensor_copy(coefT[:, 0:4 * P], b6[0:NX, :]).then_inc(s_coefT, 1)
                dve.tensor_copy(coefT[:, 4 * P:TOK], b7[0:NX, 0:(TG - 4) * P]).then_inc(s_coefT, 1)
                for t in range(TG):
                    dve.wait_ge(s_eo, NCOMB * g + t + 1)
                    dve.tensor_tensor(X1[:, b, t, :], X1[:, b, t, :], eo_bank(b, t), ALU.add).then_inc(s_comb, 1)

            def combine(g, b, e):
                for t in range(TG):
                    n = TG * (e + 1) + t
                    dve.wait_ge(s_eo, NCOMB * g + n + 1)
                    dve.wait_ge(s_comb, NCOMB * g + n - TG + 1)
                    dve.scalar_tensor_tensor(out=X1[:, b, t, :], in0=eo_bank(b, n), scalar=coef[:, t, e:e + 1],
                                             in1=X1[:, b, t, :], op0=ALU.mult, op1=ALU.add).then_inc(s_comb, 1)

            def node_body(g, b, ahead=True):
                parts = (attention_out, elu, first_norm, second_norm)
                route(g, b)
                for e in range(-1, NX):
                    if e < 0:
                        expert_bias(g, b)
                    else:
                        combine(g, b, e)
                    if ahead and e + 1 < len(parts):
                        parts[e + 1](g + 1, 1 - b)

            stored = [0, 0]
            dve.wait_ge(s_ew, 16 * 23)
            for part in (attention_out, elu, first_norm, second_norm):
                part(0, 0)
            for g in range(2):
                stored = [1, 0]
                node_body(g, g)
            with dve.Fori(1, (NTG - 1) // 2) as trip:
                v.enter(trip, 2 * 28)
                for b in range(2):
                    stored = [trip + 1, trip]
                    node_body(2 * trip + b, b)
                v.leave((NTG - 1) // 2 - 1)
            node_body(NTG - 1, 0, ahead=False)

        @block.scalar
        def _(act):
            def node_group(g, b, used):
                act.wait_ge(s_var, g + 1)
                nc.scalar.activation(sd[:, b, :], mv[:, b, :, 1], ACT.Sqrt, bias=eps[:, 0:1]).then_inc(s_sd, 1)
                at_least(act, s_hst[b], 48 * used)
                for t in range(TG):
                    act.wait_ge(s_hp, TG * g + t + 1)
                    nc.scalar.copy(hrow[b][:, t, :], (b1, b2)[(b + t) % 2][:, 0:ROW + H]).then_inc(s_hrow, 1)

            act.wait_ge(s_const, 15)
            for g in range(3):
                node_group(g, g % 2, g // 2)
            with act.Fori(1, NTG // 2) as trip:
                for k in (1, 2):
                    node_group(2 * trip + k, k % 2, trip + k // 2)
            rows_stored(act)

            def casts(j, q, b):
                act.wait_ge(s_eld[b], 3 * GI * 16 * (q + 1))
                at_least(act, s_idxp, j)
                nc.scalar.copy(erowf[:, 0:2 * P + 1], erow[:, b, :]).then_inc(s_cast, 1)

            def casts_by_head(j, q, b):
                nc.scalar.activation(hrepf[:, b, :], hrep[:, b, :], ACT.Copy, scale=BIG).then_inc(s_cast, 1)

            def st_copies(j, q, b):
                at_least(act, s_ex, j)
                for half in range(2):
                    act.wait_ge(s_stp, 2 * j + half + 1)
                    nc.scalar.copy(ST16[:, HG * half:HG * (half + 1), :].rearrange("p t e -> p (t e)"),
                                   st_ps[half]).then_inc(s_st, 1)

            def one_hot_32(j, q, b):
                act.wait_ge(s_S, j + 1)
                at_least(act, s_pm, GI * (j - 2))
                nc.scalar.copy(S[:, b, :, :], S16[:, b, :, :]).then_inc(s_S32, 1)

            def alphas(j, q, b):
                act.wait_ge(s_da, j + 1)
                nc.scalar.activation(alpha[:, b, :, :], da[:, :, :], ACT.Exp).then_inc(s_alpha, 1)

            def weights(j, q, b):
                act.wait_ge(s_df, j + 1)
                w = G[:, b, :, :].rearrange("p t (h c) -> p (t h) c", h=H)[:, :, C]
                nc.scalar.activation(w, df[:, :, :].rearrange("p t h -> p (t h)"), ACT.Exp).then_inc(s_wt, 1)

            def store_sums(j, q, b):
                act.wait_ge(s_acc, GI * (j + 1))
                act.dma_start(sums_d[bass.ds(GI * P * j, GI * P), :].rearrange("(i p) c -> p i c", p=P),
                              acc[:, b, :, :]).then_inc(s_sums[b], 16)

            for k in range(2):
                casts(*turn(0, k))
                casts_by_head(*turn(0, k))


            def body(trip, k, back=True, prep=True):
                if prep:
                    casts(*turn(trip, k + 2))
                if back:
                    weights(*turn(trip, k - 1))
                if prep:
                    casts_by_head(*turn(trip, k + 2))
                st_copies(*turn(trip, k))
                one_hot_32(*turn(trip, k))
                alphas(*turn(trip, k))
                if back:
                    store_sums(*turn(trip, k - 1))

            body(0, 0, back=False)
            for k in (1, 2, 3):
                body(0, k)
            with act.Fori(1, TRIPS) as trip:
                for k in (1, 2, 3):
                    body(trip, k)
            body(TRIPS, 1, prep=False)
            body(TRIPS, 2, prep=False)
            weights(*turn(TRIPS, 2))
            store_sums(*turn(TRIPS, 2))

            act.sem_inc(s_bank, 4)
            act.wait_ge(s_ew, 16 * 23)

            def negative_exp(g):
                act.wait_ge(s_neg, g + 1)
                nc.scalar.activation(XL[:, 1, :, :], XL[:, 1, :, :], ACT.Exp).then_inc(s_exp, 1)

            def deviation(done):
                act.wait_ge(s_var4, done)
                nc.scalar.activation(st_d[:, :], st_m[:, :, 1], ACT.Sqrt, bias=eps[:, 0:1]).then_inc(s_sd4, 1)

            def transposed(g, b):
                blocks = XT[:, b, :, :].rearrange("p c (t e) -> p (c t) e", e=P)
                for r in range(4):
                    n = min(4, 2 * TG - 4 * r)
                    act.wait_ge(s_tp4, 4 * g + r + 1)
                    nc.scalar.copy(blocks[:, 4 * r:4 * r + n, :], (b6, b7)[r % 2][:, 0:n * P]
                                   .rearrange("p (t e) -> p t e", e=P)).then_inc(s_xt4, 1)

            def layer(g, b, n, out, bias):
                act.wait_ge(s_lay, NLAY * g + n + 1)
                nc.scalar.activation(out, lay_bank(b, n), ACT.Relu, bias=bias).then_inc(s_bank, 1)

            def router(g, b):
                for hf in range(2):
                    layer(g, b, hf, rhT[:, hf * HT:(hf + 1) * HT], RB1[:, 0:1])
                act.wait_ge(s_lsub, g + 1)
                nc.scalar.activation(lgs[:, :, :], lgs[:, :, :], ACT.Exp).then_inc(s_lexp, 1)
                act.wait_ge(s_tdif, g + 1)
                nc.scalar.activation(tex[:, :], tdif[:, :], ACT.Exp).then_inc(s_tex, 1)

            def hidden(g, b, e, lay):
                out = (h1T, h2T)[lay]
                for m in range(2):
                    for hf in range(2):
                        layer(g, b, 2 + 8 * e + 4 * lay + 2 * m + hf, out[:, m, hf * HT:(hf + 1) * HT],
                              EB[:, lay, e, m:m + 1])

            def node_body(g, b, ahead=True):
                router(g, b)
                for e in range(NX):
                    hidden(g, b, e, 0)
                    hidden(g, b, e, 1)
                    if ahead and e == 0:
                        negative_exp(g + 1)
                    if ahead and e in (1, 2):
                        deviation(2 * g + 2 + e)
                    if ahead and e == 4:
                        transposed(g + 1, 1 - b)

            negative_exp(0)
            deviation(1)
            deviation(2)
            transposed(0, 0)
            for g in range(2):
                node_body(g, g)
            with act.Fori(1, (NTG - 1) // 2) as trip:
                for b in range(2):
                    node_body(2 * trip + b, b)
            node_body(NTG - 1, 0, ahead=False)

        @block.tensor
        def _(pe):
            pe.wait_ge(s_const, 15)
            pe.wait_ge(s_below, 1)
            pe.matmul(b0[0:NW + 1, 0:1], below[:, :], ones[:, 0:1], start=True, stop=True).then_inc(s_rowcnt, 1)
            pe.wait_ge(s_wst, 1)
            pe.matmul(b1[0:NW, 0:1], diffm[:, :], wst[:, :], start=True, stop=True).then_inc(s_wcnt, 1)
            pe.wait_ge(s_nit, 1)
            pe.matmul(b2[0:NW, 0:1], before[:, :], nit[:, :], start=True, stop=True).then_inc(s_i0, 1)
            pe.wait_ge(s_diagl, 1)
            pe.matmul(b3[:, 0:NI], w128[:, :], oneh[:, :], start=True, stop=True)
            pe.matmul(b4[0:1, 0:NI], dcol[:, :], oneh[:, :], start=True, stop=True)
            pe.matmul(b5[:, 0:NW], ones[0:NW, :], diagl[:, :], start=True, stop=True).then_inc(s_lists, 1)

            def node_group(g, b):
                for t in range(TG + 1):
                    if t < TG:
                        n, odd = TG * g + t, (b + t) % 2
                        pe.wait_ge(s_xn, n + 1)
                        at_least(pe, s_xt, n - 1)
                        for c in range(2):
                            one = pe.transpose((b0, b3)[odd][:, c * P:(c + 1) * P],
                                               xn_s[b][:, t, c * P:(c + 1) * P], ident[:, :])
                        one.then_inc(s_xtp, 1)
                    if t:
                        n, odd = TG * g + t - 1, (b + t - 1) % 2
                        pe.wait_ge(s_xt, n + 1)
                        at_least(pe, s_hrow, n - 1)
                        for c in range(2):
                            one = pe.matmul((b1, b2)[odd][:, 0:ROW + H], xnT[:, odd, c, :], Wcat[:, c, :],
                                            start=(c == 0), stop=(c == 1))
                        one.then_inc(s_hp, 1)

            pe.wait_ge(s_wcat, 2)
            for g in range(3):
                node_group(g, g % 2)
            with pe.Fori(1, NTG // 2) as trip:
                for k in (1, 2):
                    node_group(2 * trip + k, k % 2)
            pe.wait_ge(s_hrow, NW)

            def prepare(j, q, b):
                pe.wait_ge(s_cast, 2 * (j + 1) - 1)
                at_least(pe, s_prep, j)
                pe.wait_ge(s_rend, j + 1)
                apart(pe)
                for n, o in ((0, erowf[:, 0:P]), (1, erowf[:, P:2 * P]), (2, erend[:, :])):
                    last_ = pe.transpose(idx_ps[:, n, :], o, ident[0:GT, 0:GT])
                last_.then_inc(s_idxp, 1)

            def transpose_one_hot(j, q, b):
                pe.wait_ge(s_S, j + 1)
                at_least(pe, s_st, 2 * j)
                for half in range(2):
                    for t in range(HG):
                        last_ = pe.transpose(st_ps[half][:, t * P:(t + 1) * P], S16[:, b, HG * half + t, :],
                                             ident16[:, :])
                    last_.then_inc(s_stp, 1)

            def a_src_rows(j, q, b):
                pe.wait_ge(s_gath[b], GT * 16 * (q + 1))
                at_least(pe, s_scan, j)
                a_src = G[:, b, :, :].rearrange("p t (h c) -> p (t h) c", h=H)[:, :, C]
                for k in range(IT):
                    last_ = pe.transpose(b0[0:GI * H, k * P:(k + 1) * P], 
                                         a_src[:, k * GI * H:(k + 1) * GI * H], ident[:, :])
                last_.then_inc(s_sT, 1)

            def maxima_back(j, q, b):
                pe.wait_ge(s_scan, j + 1)
                at_least(pe, s_Fe, j)
                apart(pe)
                for k in range(IT):
                    last_ = pe.transpose(back_ps[:, k * GI * H:(k + 1) * GI * H], F[:, k * P:(k + 1) * P],
                                         ident[0:GI * H, 0:GI * H])
                last_.then_inc(s_FP, 1)

            def node_maxima(j, q, b):
                pe.wait_ge(s_S, j + 1)
                pe.wait_ge(s_Fe, j + 1)
                at_least(pe, s_R, j)
                for i in range(GI):
                    for k in range(IT):
                        last_ = pe.matmul(mt_ps[:, i, :], S16[:, b, IT * i + k, :], Fe16[:, IT * i + k, :],
                                          start=(k == 0), stop=(k == IT - 1))
                last_.then_inc(s_mt, 1)

            def expand(j, q, b):
                pe.wait_ge(s_st, 2 * (j + 1))
                pe.wait_ge(s_R16, j + 1)
                at_least(pe, s_df, j)
                for t in range(GT):
                    for n in range(3):
                        last_ = pe.matmul(ex_ps[:, slot(t // IT, t % IT), :], ST16[:, t, :], R16[:, t // IT, n, :],
                                          start=(n == 0), stop=(n == 2))
                last_.then_inc(s_ex, 1)

            def sum_item(j, q, b, i):
                pe.wait_ge(s_S32, j + 1)
                pe.wait_ge(s_msg, GI * j + i + 1)
                at_least(pe, s_acc, GI * j + i - 2)
                for k in range(IT):
                    last_ = pe.matmul(sum_bank(j, b, i), S[:, b, IT * i + k, :], G[:, b, slot(i, k), :],
                                      start=(k == 0), stop=(k == IT - 1))
                last_.then_inc(s_pm, 1)

            prepare(*turn(0, 0))
            prepare(*turn(0, 1))

            a_src_rows(*turn(0, 0))

            def body(trip, k, back=True, prep=True, ahead=True):
                now, ago = turn(trip, k), turn(trip, k - 1)
                maxima_back(*now)
                if back:
                    expand(*ago)
                node_maxima(*now)
                if prep:
                    prepare(*turn(trip, k + 2))
                transpose_one_hot(*now)
                if back:
                    for i in range(GI - 1):
                        sum_item(*ago, i)
                if ahead:
                    a_src_rows(*turn(trip, k + 1))
                if back:
                    sum_item(*ago, GI - 1)

            body(0, 0, back=False)
            for k in (1, 2, 3):
                body(0, k)
            with pe.Fori(1, TRIPS) as trip:
                for k in (1, 2, 3):
                    body(trip, k)
            body(TRIPS, 1, prep=False)
            body(TRIPS, 2, prep=False, ahead=False)
            expand(*turn(TRIPS, 2))
            for i in range(GI):
                sum_item(*turn(TRIPS, 2), i)

            pe.wait_ge(s_ew, 16 * 23)
            pe.wait_ge(s_acc, GI * NG)

            def transposes(g, b):
                pe.wait_ge(s_xn4, g + 1)
                for r in range(4):
                    at_least(pe, s_xt4, 4 * g + r - 1)
                    for n in range(4 * r, min(4 * r + 4, 2 * TG)):
                        c, t = n // TG, n % TG
                        one = pe.transpose((b6, b7)[r % 2][:, (n % 4) * P:(n % 4 + 1) * P],
                                           XL[:, 1, t, c * P:(c + 1) * P], ident[:, :])
                    one.then_inc(s_tp4, 1)

            def layer(g, b, n, weights, x, hf):
                pe.wait_ge(s_bank, NLAY * g + n + 1)
                for c in range(2):
                    one = pe.matmul(lay_bank(b, n), weights(c), x[:, c, hf * HT:(hf + 1) * HT],
                                    start=(c == 0), stop=(c == 1))
                one.then_inc(s_lay, 1)

            def router(g, b):
                pe.wait_ge(s_xt4, 4 * (g + 1))
                for hf in range(2):
                    layer(g, b, hf, lambda c: RW1[:, c, :], XT[:, b, :, :], hf)
                pe.wait_ge(s_bank, NLAY * g + 2 + 4)
                for t in range(TG):
                    one = pe.matmul(lg_ps[:, t, :], rhT[:, t * P:(t + 1) * P], RW2[:, :], start=True, stop=True)
                one.then_inc(s_lg, 1)

            def hidden(g, b, e, lay):
                w, x = ((EW1, XT[:, b, :, :]), (EW2, h1T))[lay]
                if lay:
                    pe.wait_ge(s_bank, NLAY * g + 2 + 8 * e + 4 + 4)
                for m in range(2):
                    for hf in range(2):
                        layer(g, b, 2 + 8 * e + 4 * lay + 2 * m + hf,
                              lambda c: w[:, e, c, m * P:(m + 1) * P], x, hf)

            def to_add(g, b, n, pairs):
                at_least(pe, s_comb, NCOMB * g + max(n - 1, 0))
                for k, (l, r) in enumerate(pairs):
                    one = pe.matmul(eo_bank(b, n), l, r, start=(k == 0), stop=(k == len(pairs) - 1))
                one.then_inc(s_eo, 1)

            def expert_bias(g, b):
                pe.wait_ge(s_coef, g + 1)
                for t in range(TG):
                    one = pe.transpose((b6, b7)[t // 4][0:NX, (t % 4) * P:(t % 4 + 1) * P], coef[:, t, :], ident[:, :])
                one.then_inc(s_cT, 1)
                pe.wait_ge(s_coefT, 2 * (g + 1))
                for t in range(TG):
                    to_add(g, b, t, [(coefT[:, t * P:(t + 1) * P], EB3[:, :])])

            def expert_out(g, b, e):
                pe.wait_ge(s_bank, NLAY * g + 2 + 8 * (e + 1) + 4)
                for t in range(TG):
                    to_add(g, b, TG * (e + 1) + t,
                           [(h2T[:, c, t * P:(t + 1) * P], EW3[:, e, c, :]) for c in range(2)])

            def node_body(g, b, ahead=True):
                router(g, b)
                hidden(g, b, 0, 0)
                expert_bias(g, b)
                hidden(g, b, 0, 1)
                for e in range(1, NX):
                    hidden(g, b, e, 0)
                    expert_out(g, b, e - 1)
                    hidden(g, b, e, 1)
                    if ahead and e == 4:
                        transposes(g + 1, 1 - b)
                expert_out(g, b, NX - 1)

            transposes(0, 0)
            for g in range(2):
                node_body(g, g)
            with pe.Fori(1, (NTG - 1) // 2) as trip:
                for b in range(2):
                    node_body(2 * trip + b, b)
            node_body(NTG - 1, 0, ahead=False)


_IN = {'W': 'L0_gnn_W', 'att_src': 'L0_gnn_att_src', 'att_dst': 'L0_gnn_att_dst', 'bias': 'L0_gnn_bias',
       'ln_scale': 'L0_gnn_ln_scale', 'ln_bias': 'L0_gnn_ln_bias', 'rw1': 'L0_ffn_router_w1',
       'rb1': 'L0_ffn_router_b1', 'rw2': 'L0_ffn_router_w2', 'rb2': 'L0_ffn_router_b2',
       'ew1': 'L0_ffn_expert_w1', 'eb1': 'L0_ffn_expert_b1', 'ew2': 'L0_ffn_expert_w2',
       'eb2': 'L0_ffn_expert_b2', 'ew3': 'L0_ffn_expert_w3', 'eb3': 'L0_ffn_expert_b3'}


def kernel(**inputs):
    import numpy as np
    import concourse.bacc as bacc
    from concourse.bass_utils import run_bass_kernel_spmd

    x = np.zeros((NPAD, D), np.float32)
    x[:N] = inputs['x']
    src = np.zeros((LE,), np.int32)
    src[:NE] = inputs['src']
    dst = np.full((LE + 2,), NPAD, np.int32)
    dst[0] = -1
    dst[1:NE + 1] = inputs['dst']
    given = {'x': x, 'src': src, 'dst': dst}
    for name, full in _IN.items():
        given[name] = np.ascontiguousarray(inputs[full])

    nc = bacc.Bacc("TRN2", target_bir_lowering=False, num_devices=1)
    io = {name: nc.dram_tensor(f"in_{name}", a.shape, mybir.dt.from_np(a.dtype), kind="ExternalInput").ap()
          for name, a in given.items()}
    io['out'] = nc.dram_tensor("out_x", (N, D), F32, kind="ExternalOutput").ap()
    build(nc, io)
    r = run_bass_kernel_spmd(nc, [{f"in_{name}": a for name, a in given.items()}], core_ids=[0])
    return r.results[0]["out_x"]
```

```python
from contextlib import ExitStack

import concourse.bass as bass
from concourse import mybir

ALU = mybir.AluOpType
ACT = mybir.ActivationFunctionType
AX = mybir.AxisListType
F32 = mybir.dt.float32
BF16 = mybir.dt.bfloat16
I32 = mybir.dt.int32
U32 = mybir.dt.uint32

P = 128
N = 6250
NE = 206250
D = 256
H = 8
C = D // H
HC = C + 1
ROW = H * HC
NW = -(-N // P)
NPAD = NW * P
EPP = -(-NE // P)
IT = 4
IE = IT * P
GI = 4
GT = GI * IT
HG = GT // 2
NG = -(-(NE // IE + NW) // GI)
TRIPS = (NG - 3) // 3
LAST_ONES = range(1, NG - 3 * TRIPS)
LAST = LAST_ONES[-1]
NI = NG * GI
LE = NI * IE
NX = 6
RH = 128
BIG = 1e30
SLOPE = 0.2
EPS = 1e-5
TG = 7
NTG = NW // TG
TOK = TG * P
HT = TOK // 2


class Links:

    def __init__(self, engine, sem):
        self.engine, self.sem, self.n, self.trip, self.per_trip = engine, sem, 0, None, 0

    def mark(self, ins):
        ins.then_inc(self.sem, 1)
        self.n += 1
        return self.n if self.trip is None else self.trip * self.per_trip + self.n

    def need(self, mark):
        self.engine.wait_ge(self.sem, mark)

    def link(self, ins):
        self.need(self.mark(ins))

    def enter(self, trip, per_trip):
        self.n -= per_trip
        self.trip, self.per_trip, self.start = trip, per_trip, self.n

    def leave(self, trips):
        assert self.n - self.start == self.per_trip, (self.n - self.start, self.per_trip)
        self.n += self.per_trip * trips
        self.trip = None


def at_least(engine, sem, value):
    if not (isinstance(value, int) and value <= 0):
        engine.wait_ge(sem, value)


def turn(trip, k):
    return 3 * trip + k, trip + k // 3, k % 3


def build(nc, io):
    with ExitStack() as ctx:
        def sb(name, shape, dt=F32):
            return ctx.enter_context(nc.sbuf_tensor(name, shape, dt))

        def ps(name, shape):
            return ctx.enter_context(nc.psum_tensor(name, shape, F32))

        def sem(name):
            return ctx.enter_context(nc.semaphore(name))

        x_d, src_d, dst_d = io["x"], io["src"], io["dst"]
        out_d = io["out"]
        rows_d = nc.dram_tensor("rows_d", (NPAD, ROW), F32).ap()
        adst_d = nc.dram_tensor("adst_d", (NPAD, H), F32).ap()
        xn_d = nc.dram_tensor("xn_d", (NPAD, D), F32).ap()
        sums_d = nc.dram_tensor("sums_d", (NI * P, ROW), F32).ap()

        arena = sb("arena", [P, 3 * GT * ROW])
        X = arena[:, 0:NW * D].rearrange("p (t d) -> p t d", t=NW)
        G = arena[:, :].rearrange("p (b t c) -> p b t c", b=3, t=GT)
        slot = lambda i, k: GI * k + i
        S = sb("S", [P, 3, GT, P])
        S16 = sb("S16", [P, 3, GT, P], BF16)
        ST16 = sb("ST16", [P, GT, P], BF16)
        ident = sb("ident", [P, P])
        ident16 = sb("ident16", [P, P], BF16)
        ones = sb("ones", [P, P])
        lane = sb("lane", [P, P])
        lane16 = sb("lane16", [P, P], BF16)
        lane_p = sb("lane_p", [P, 1])
        item_end = sb("item_end", [P, GT])
        winb = sb("winb", [P, NI])
        reset = sb("reset", [P, NI])
        table = sb("table", [1, NI, 2], I32)
        sums_idx = sb("sums_idx", [P, NW], U32)

        eps = sb("eps", [P, 1])

        last_i = sb("last_i", [P, 1], I32)
        last = sb("last", [P, 1])
        thr = sb("thr", [P, NW + 1])
        thr_p = sb("thr_p", [NW + 1, 1])
        below = sb("below", [P, NW + 1])
        rowno = sb("rowno", [NW + 1, 1])
        rowno_u = sb("rowno_u", [NW + 1, 1], U32)
        cnt = sb("cnt", [NW + 1, 1])
        wst = sb("wst", [NW + 1, 1])
        diffm = sb("diffm", [NW + 1, NW])
        before = sb("before", [NW, NW])
        tailc = sb("tailc", [NW, 1])
        nit_i = sb("nit_i", [NW, 2], I32)
        nit = sb("nit", [NW, 1])
        i0 = sb("i0", [NW, 1])
        i1 = sb("i1", [NW, 1])
        i1t = sb("i1t", [NW, 1])
        dcol = sb("dcol", [NW, 1])
        diagl = sb("diagl", [NW, NW])
        iota_i = sb("iota_i", [NW, NI])
        ge = sb("ge", [NW, NI])
        oneh = sb("oneh", [NW, NI])
        w128 = sb("w128", [NW, P])

        W_s = sb("W_s", [P, 2, D])
        att = sb("att", [P, 2, D])
        prod = sb("prod", [P, D])
        Wcat = sb("Wcat", [P, 2, ROW + H])
        wa = sb("wa", [P, 2, 2, H])
        stat = sb("stat", [P, TG, 6])
        mv = sb("mv", [P, 2, TG, 2])
        sd = sb("sd", [P, 2, TG])
        rs = sb("rs", [P, 2, TG])
        xnT = sb("xnT", [P, 2, 2, P])
        flat_S = S[:, :, :, :].rearrange("p b t e -> p (b t e)")
        flat_S16 = S16[:, :, :, :].rearrange("p b t e -> p (b t e)").bitcast(F32)
        hrow = [flat_S[:, b * TG * (ROW + H):(b + 1) * TG * (ROW + H)].rearrange("p (t c) -> p t c", t=TG)
                for b in range(2)]
        xn_s = [o.rearrange("p (t d) -> p t d", t=TG)
                for o in (flat_S16[:, 0:TG * D], flat_S[:, 3 * GT * P - TG * D:3 * GT * P])]

        erow = sb("erow", [GT, 3, 2 * P + 2], I32)
        erowf = sb("erowf", [GT, 2 * P + 2])
        opens = sb("opens", [GT, P + 1], BF16)
        spread = sb("spread", [GT, IT, GI * H])
        spread16 = sb("spread16", [GT, IT, GI * H], BF16)
        gap = sb("gap", [GI * H, 3, IE])
        F = sb("F", [GI * H, IE])
        gidx = sb("gidx", [P, 3, GT], U32)
        dloc = sb("dloc", [P, 3, GT], BF16)
        isend = sb("isend", [P, 3, GT])
        Fe = sb("Fe", [P, GT, H])
        Fr = sb("Fr", [P, GT, H])
        Fe16 = sb("Fe16", [P, GT, 3 * H + 1], BF16)
        t1 = sb("t1", [P, GI])
        mi = sb("mi", [P, GI, H])
        M = sb("M", [P, GI + 1, H])
        xm = sb("xm", [P, GI, H])
        R16 = sb("R16", [P, GI, 3, 2 * H], BF16)
        Rr = sb("Rr", [P, GI, 2 * H])
        R = sb("R", [P, 3, GI + 1, 2 * H])
        da = sb("da", [P, GI, H])
        alpha = sb("alpha", [P, 3, GI, H])
        z = sb("z", [P, GT, H])
        lz = sb("lz", [P, GT, H])
        df = sb("df", [P, GT, H])
        scaled = sb("scaled", [P, ROW])
        acc = sb("acc", [P, 3, GI, ROW])

        less = acc[0:NW + 1, :, :, :].rearrange("p b i c -> p (b i c)")[:, 0:EPP]
        found = less.bitcast(I32)

        b0 = ps("b0", [P, 512])
        b1 = ps("b1", [P, 512])
        b2 = ps("b2", [P, 512])
        b3 = ps("b3", [P, 512])
        b4 = ps("b4", [P, 512])
        b5 = ps("b5", [P, 512])
        b6 = ps("b6", [P, 512])
        b7 = ps("b7", [P, 512])

        idx_ps = b7[:, 0:2 * GT].rearrange("p (n t) -> p n t", n=2)
        end_ps = b7[:, 2 * GT:3 * GT].bitcast(BF16)[:, 0:GT]
        gap_ps = b1[0:GI * H, :]
        mt_ps = b7[:, 64:64 + GI * (3 * H + 1)].rearrange("p (i h) -> p i h", i=GI)
        ex_ps = b2[:, 0:GT * 2 * H].rearrange("p (t h) -> p t h", t=GT)
        back_ps = b7[:, 2 * P:2 * P + GT * H]
        st_ps = [b[:, :].bitcast(BF16) for b in (b5, b6)]
        sum_bank = lambda i: (b3, b4)[i % 2][:, 0:ROW]

        s_const = sem("s_const")
        s_ld = sem("s_ld")
        s_apart = sem("s_apart")
        s_last = sem("s_last")
        s_w = sem("s_w")
        s_x = [sem(f"s_x{g}") for g in range(4)]
        s_v = sem("s_v")
        s_below = sem("s_below")
        s_rowcnt = sem("s_rowcnt")
        s_rowno = sem("s_rowno")
        s_row = sem("s_row")
        s_wst = sem("s_wst")
        s_wcnt = sem("s_wcnt")
        s_nit = sem("s_nit")
        s_i0 = sem("s_i0")
        s_diagl = sem("s_diagl")
        s_lists = sem("s_lists")
        s_items = sem("s_items")
        s_wcat = sem("s_wcat")
        s_var = sem("s_var")
        s_sd = sem("s_sd")
        s_xn = sem("s_xn")
        s_xtp = sem("s_xtp")
        s_xt = sem("s_xt")
        s_hp = sem("s_hp")
        s_hrow = sem("s_hrow")
        s_hst = [sem(f"s_hst{b}") for b in range(2)]
        s_eld = [sem(f"s_eld{b}") for b in range(3)]
        s_nld = [sem(f"s_nld{b}") for b in range(3)]
        s_cast = sem("s_cast")
        s_rend = sem("s_rend")
        s_idxp = sem("s_idxp")
        s_gidx = sem("s_gidx")
        s_prep = sem("s_prep")
        s_gath = [sem(f"s_gath{b}") for b in range(3)]
        s_S = sem("s_S")
        s_S32 = sem("s_S32")
        s_stp = sem("s_stp")
        s_st = sem("s_st")
        s_gap = sem("s_gap")
        s_sT = sem("s_sT")
        s_scan = sem("s_scan")
        s_FP = sem("s_FP")
        s_Fe = sem("s_Fe")
        s_mt = sem("s_mt")
        s_R = sem("s_R")
        s_R16 = sem("s_R16")
        s_da = sem("s_da")
        s_alpha = sem("s_alpha")
        s_ex = sem("s_ex")
        s_df = sem("s_df")
        s_wt = sem("s_wt")
        s_msg = sem("s_msg")
        s_pm = sem("s_pm")
        s_acc = sem("s_acc")
        s_sums = [sem(f"s_sums{b}") for b in range(3)]

        def carve(space, at, *shape):
            n = 1
            for q in shape:
                n *= q
            names = " ".join("abcd"[:len(shape)])
            sizes = {"abcd"[i]: q for i, q in enumerate(shape[:-1])}
            return space[:, at:at + n].rearrange(f"p ({names}) -> p {names}", **sizes), at + n

        XT, at = carve(arena, 0, 2, 2, TOK)
        X1, at = carve(arena, at, 2, TG, D)
        XL, at = carve(arena, at, 2, TG, D)
        SM, at = carve(arena, at, TG, ROW)
        S_flat = S[:, :, :, :].rearrange("p b t e -> p (b t e)")
        h1T, at = carve(S_flat, 0, 2, TOK)
        h2T, at = carve(S_flat, at, 2, TOK)
        rhT = S_flat[:, at:at + TOK]
        EW1 = sb("EW1", [P, NX, 2, D])
        EW2 = sb("EW2", [P, NX, 2, D])
        EW3 = sb("EW3", [P, NX, 2, D])
        RW1 = sb("RW1", [P, 2, RH])
        RW2 = sb("RW2", [P, NX])
        EB3 = sb("EB3", [NX, D])
        RB1 = sb("RB1", [P, 1])
        EB = sb("EB", [P, 2, NX, 2])
        RB2 = sb("RB2", [P, NX])
        VEC = sb("VEC", [P, 3, D])
        den = sb("den", [P, TG * H])
        rden = sb("rden", [P, TG * H])
        st_s = sb("st_s", [P, TG, 6])
        st_m = sb("st_m", [P, TG, 2])
        st_d = sb("st_d", [P, TG])
        st_r = sb("st_r", [P, TG])
        lgs = sb("lgs", [P, TG, NX])
        lmx = sb("lmx", [P, TG])
        lsum = sb("lsum", [P, TG])
        lrec = sb("lrec", [P, TG])
        prob = sb("prob", [P, TG, 8])
        top = sb("top", [P, TG, 8])
        topi = sb("topi", [P, TG, 8], U32)
        topf = sb("topf", [P, TG, 2])
        tdif = sb("tdif", [P, TG])
        tex = sb("tex", [P, TG])
        ten = sb("ten", [P, TG])
        tw = sb("tw", [P, 2, TG])
        expert = sb("expert", [P, TG, NX])
        c1 = sb("c1", [P, TG, NX])
        c2 = sb("c2", [P, TG, NX])
        coef = sb("coef", [P, TG, NX])
        coefT = sb("coefT", [NX, TOK])
        s_ew = sem("s_ew")
        s_xl = sem("s_xl")
        s_sm = sem("s_sm")
        s_smfree = sem("s_smfree")
        s_neg = sem("s_neg")
        s_exp = sem("s_exp")
        s_var4 = sem("s_var4")
        s_sd4 = sem("s_sd4")
        s_xn4 = sem("s_xn4")
        s_tp4 = sem("s_tp4")
        s_xt4 = sem("s_xt4")
        s_bank = sem("s_bank")
        s_lay = sem("s_lay")
        s_lg = sem("s_lg")
        s_lsub = sem("s_lsub")
        s_lexp = sem("s_lexp")
        s_tdif = sem("s_tdif")
        s_tex = sem("s_tex")
        s_coef = sem("s_coef")
        s_cT = sem("s_cT")
        s_coefT = sem("s_coefT")
        s_eo = sem("s_eo")
        s_comb = sem("s_comb")
        s_out = [sem(f"s_out{b}") for b in range(2)]
        lg_ps = b6[:, 0:TG * NX].rearrange("p (t e) -> p t e", t=TG)
        lay_bank = lambda b, n: (b0, b1, b2, b3)[(NLAY * b + n) % 4][:, 0:HT]
        eo_bank = lambda b, n: (b4, b5)[(NCOMB * b + n) % 2][:, 0:D]
        NLAY = 2 + NX * 8
        NCOMB = TG * (NX + 1)
        first_addend = lambda e: TG * (e + (e > 0))

        def apart(engine):
            engine.sem_inc(s_apart, 1)

        def rows_stored(engine):
            engine.wait_ge(s_hst[0], 48 * (NTG // 2 + 1))
            engine.wait_ge(s_hst[1], 48 * (NTG // 2))

        x_t = x_d.rearrange("(t p) d -> p t d", p=P)
        block = ctx.enter_context(nc.Block())

        @block.sync
        def _(sp):
            dst_pp = dst_d[0:P * EPP].rearrange("(p e) -> p e", p=P)
            with nc.allow_non_contiguous_dma(reason="one number per partition"):
                sp.dma_start(last_i[:, :], dst_pp[:, EPP - 1:EPP]).then_inc(s_last, 16)
            sp.dma_start(W_s[:, :, :], io["W"].rearrange("(c p) n -> p c n", p=P)).then_inc(s_w, 16)
            for n, a in enumerate((io["att_src"], io["att_dst"])):
                sp.dma_start(att[:, n, :], a.rearrange("h c -> (h c)").partition_broadcast(P)).then_inc(s_w, 16)
            for g in range(NTG):
                sp.dma_start(X[:, TG * g:TG * (g + 1), :], x_t[:, TG * g:TG * (g + 1), :]).then_inc(s_x[min(g, 3)], 16)

            for tile, dram in zip((EW1, EW2, EW3), (io["ew1"], io["ew2"], io["ew3"])):
                sp.dma_start(tile[:, :, :, :], dram.rearrange("e (c p) n -> p e c n", p=P)).then_inc(s_ew, 16)
            sp.dma_start(RW1[:, :, :], io["rw1"].rearrange("(c p) n -> p c n", p=P)).then_inc(s_ew, 16)
            sp.dma_start(RW2[:, :], io["rw2"]).then_inc(s_ew, 16)
            sp.dma_start(EB3[:, :], io["eb3"]).then_inc(s_ew, 16)
            with nc.allow_non_contiguous_dma(reason="small biases, one per partition"):
                sp.dma_start(RB1[:, :], io["rb1"].rearrange("(p a) -> p a", a=1)).then_inc(s_ew, 16)
                for n, dram in enumerate((io["eb1"], io["eb2"])):
                    for e in range(NX):
                        sp.dma_start(EB[:, n, e, :], dram[e].rearrange("(c p) -> p c", p=P)).then_inc(s_ew, 16)
            sp.dma_start(RB2[:, :], io["rb2"].partition_broadcast(P)).then_inc(s_ew, 16)
            for n, dram in enumerate((io["bias"], io["ln_scale"], io["ln_bias"])):
                sp.dma_start(VEC[:, n, :], dram.partition_broadcast(P)).then_inc(s_ew, 16)

            def store_rows(g, b):
                sp.wait_ge(s_hrow, TG * (g + 1))
                tiles = lambda dram: dram[bass.ds(g * TOK, TOK), :].rearrange("(t p) c -> p t c", p=P)
                sp.dma_start(tiles(rows_d), hrow[b][:, :, 0:ROW]).then_inc(s_hst[b], 16)
                sp.dma_start(tiles(adst_d), hrow[b][:, :, ROW:ROW + H]).then_inc(s_hst[b], 16)
                sp.dma_start(tiles(xn_d), xn_s[b][:, :, :]).then_inc(s_hst[b], 16)

            for g in range(2):
                store_rows(g, g)
            with sp.Fori(1, NTG // 2) as trip:
                for b in range(2):
                    store_rows(2 * trip + b, b)
            store_rows(NTG - 1, 0)

            sp.wait_ge(s_items, 1)

            def load_edges(j, q, b):
                at_least(sp, s_cast, j - 2)
                for i in range(GI):
                    start = sp.value_load(table[0:1, bass.ds(GI * j + i, 1), 0], min_val=0, max_val=LE - IE)
                    sp.dma_start(erow[IT * i:IT * i + IT, b, 0:P],
                                 src_d[bass.ds(start, IE)].rearrange("(k e) -> k e", k=IT)).then_inc(s_eld[b], 16)
                    d = dst_d[bass.ds(start, IE + 2)]
                    sp.dma_start(erow[IT * i:IT * i + IT, b, P:2 * P + 2],
                                 bass.AP(d.tensor, d.offset, [[P, IT], [1, P + 2]])).then_inc(s_eld[b], 16)

            def load_nodes(j, q, b):
                at_least(sp, s_ex, j - 2)
                for i in range(GI):
                    node = sp.value_load(table[0:1, bass.ds(GI * j + i, 1), 1], min_val=0, max_val=NPAD - P)
                    sp.dma_start(R[:, b, 1 + i, 0:H], adst_d[bass.ds(node, P), :]).then_inc(s_nld[b], 16)

            load_edges(*turn(0, 0))
            load_edges(*turn(0, 1))
            rows_stored(sp)
            load_nodes(*turn(0, 0))
            for k in range(2, 6):
                load_edges(*turn(0, k))
                load_nodes(*turn(0, k - 1))
            with sp.Fori(2, NG // 3) as trip:
                for k in range(3):
                    load_edges(*turn(trip, k))
                    load_nodes(*turn(trip, k - 1))
            for k in range(NG % 3):
                load_edges(*turn(NG // 3, k))
                load_nodes(*turn(NG // 3, k - 1))
            load_nodes(*turn(NG // 3, NG % 3 - 1))

            sp.wait_ge(s_pm, GI * NG)

            def load_node_group(g):
                at_least(sp, s_tp4, 4 * g)
                nodes = bass.ds(g * TOK, TOK)
                for n, dram in enumerate((x_d, xn_d)):
                    sp.dma_start(XL[:, n, :, :], dram[nodes, :].rearrange("(t p) d -> p t d", p=P)).then_inc(s_xl, 16)

            def store_nodes(g, b):
                sp.wait_ge(s_comb, NCOMB * (g + 1))
                sp.dma_start(out_d[bass.ds(g * TOK, TOK), :].rearrange("(t p) d -> p t d", p=P),
                             X1[:, b, :, :]).then_inc(s_out[b], 16)

            load_node_group(0)
            for g in range(2):
                load_node_group(g + 1)
                store_nodes(g, g)
            with sp.Fori(1, (NTG - 1) // 2) as trip:
                for b in range(2):
                    load_node_group(2 * trip + b + 1)
                    store_nodes(2 * trip + b, b)
            sp.wait_ge(s_comb, NCOMB * NTG)
            first, full = (NTG - 1) * TOK, N // P - (NTG - 1) * TG
            sp.dma_start(out_d[first:first + full * P, :].rearrange("(t p) d -> p t d", p=P),
                         X1[:, 0, 0:full, :]).then_inc(s_out[0], 16)
            sp.dma_start(out_d[first + full * P:N, :], X1[0:N % P, 0, full, :]).then_inc(s_out[0], 16)
            sp.wait_ge(s_out[0], 16 * ((NTG + 1) // 2 + 1))
            sp.wait_ge(s_out[1], 16 * (NTG // 2))

        @block.gpsimd
        def _(pool):
            iota = lambda o, pat, m: pool.iota(o, pattern=pat, base=0, channel_multiplier=m,
                                               allow_small_or_imprecise_dtypes=True)
            pool.memset(ident[:, :], 0.0).then_inc(s_ld, 1)
            pool.memset(diffm[:, :], 0.0).then_inc(s_ld, 1)
            pool.memset(before[:, :], 1.0).then_inc(s_ld, 1)
            pool.memset(tailc[:, :], 0.0).then_inc(s_ld, 1)
            pool.memset(item_end[:, :], 0.0).then_inc(s_ld, 1)
            pool.memset(spread[:, :, :], -BIG).then_inc(s_ld, 1)
            pool.memset(ones[:, :], 1.0).then_inc(s_const, 1)
            pool.memset(eps[:, :], EPS).then_inc(s_const, 1)
            iota(thr[:, :], [[P, NW + 1]], 0).then_inc(s_const, 1)
            iota(thr_p[:, :], [[0, 1]], P).then_inc(s_const, 1)
            iota(lane[:, :], [[1, P]], 0).then_inc(s_const, 1)
            iota(lane_p[:, :], [[0, 1]], 1).then_inc(s_const, 1)
            iota(iota_i[:, :], [[1, NI]], 0).then_inc(s_const, 1)
            iota(w128[:, :], [[0, P]], P).then_inc(s_const, 1)
            iota(expert[:, :, :], [[0, TG], [1, NX]], 0).then_inc(s_const, 1)
            pool.memset(prob[:, :, :], -1.0).then_inc(s_const, 1)

            def select(m, pat, base, mult, op, fill):
                return pool.affine_select(out=m, in_=m, compare_op=op, fill=fill, base=base,
                                          pattern=pat, channel_multiplier=mult)

            pool.wait_ge(s_ld, 6)
            select(ident[:, :], [[-1, P]], 0, 1, ALU.not_equal, 1.0).then_inc(s_const, 1)
            select(before[:, :], [[1, NW]], 0, -1, ALU.is_gt, 0.0).then_inc(s_const, 1)
            select(tailc[:, :], [[0, 1]], -(NW - 1), 1, ALU.not_equal, 1e6).then_inc(s_const, 1)
            select(spread[:, :, :].rearrange("p k (i h) -> p k i h", i=GI), [[-1, IT], [-IT, GI], [0, H]], 0, 1,
                   ALU.is_equal, 0.0).then_inc(s_const, 1)
            e = item_end[:, :].rearrange("p (i k) -> p i k", k=IT)
            select(e, [[0, GI], [1, IT]], -(IT - 1 + P - 1), 1, ALU.not_equal, 1.0).then_inc(s_const, 1)
            select(diffm[:, :], [[-1, NW]], 0, 1, ALU.not_equal, -1.0).then_inc(s_ld, 1)
            pool.wait_ge(s_ld, 7)
            select(diffm[:, :], [[-1, NW]], -1, 1, ALU.not_equal, 1.0).then_inc(s_const, 1)

            pool.wait_ge(s_rowno, 1)
            dst_pp = dst_d[0:P * EPP].rearrange("(p e) -> p e", p=P)
            pool.indirect_dma_start(found, None, dst_pp,
                                    bass.IndirectOffsetOnAxis(ap=rowno_u[:, 0:1], axis=0)).then_inc(s_row, 16)

            rows_stored(pool)

            def gather(j, q, b):
                pool.wait_ge(s_gidx, j + 1)
                for t in range(GT):
                    if t % IT == 0:
                        at_least(pool, s_pm, GI * (j - 3) + t // IT + 1)
                        apart(pool)
                    pool.indirect_dma_start(G[:, b, slot(t // IT, t % IT), :], None, rows_d,
                                            bass.IndirectOffsetOnAxis(ap=gidx[:, b, t:t + 1], axis=0)
                                            ).then_inc(s_gath[b], 16)

            for k in range(3):
                gather(*turn(0, k))
            with pool.Fori(1, NG // 3) as trip:
                for k in range(3):
                    gather(*turn(trip, k))
            for k in range(NG % 3):
                gather(*turn(NG // 3, k))

            for b in range(3):
                groups = (NG - b + 2) // 3
                pool.wait_ge(s_sums[b], 16 * (groups + (GI - 1 if b == (NG - 1) % 3 else 0)))
            for g in range(NTG):
                at_least(pool, s_smfree, g)
                for t in range(TG):
                    pool.indirect_dma_start(SM[:, t, :], None, sums_d,
                                            bass.IndirectOffsetOnAxis(ap=sums_idx[:, TG * g + t:TG * g + t + 1],
                                                                      axis=0)).then_inc(s_sm, 16)

        @block.vector
        def _(dve):
            v = Links(dve, s_v)
            dve.wait_ge(s_last, 16)
            dve.wait_ge(s_const, 16)
            v.link(dve.tensor_copy(last[:, :], last_i[:, :]))
            dve.tensor_scalar(below[:, :], thr[:, :], last[:, 0:1], None, ALU.is_gt).then_inc(s_below, 1)
            dve.wait_ge(s_rowcnt, 1)
            v.link(dve.tensor_scalar(rowno[:, :], b4[0:NW + 1, 0:1], float(P - 1), None, ALU.min))
            dve.tensor_copy(rowno_u[:, :], rowno[:, :]).then_inc(s_rowno, 1)
            dve.wait_ge(s_w, 48)
            for c in range(2):
                for n in range(2):
                    v.link(dve.tensor_tensor(prod[:, :], W_s[:, c, :], att[:, n, :], ALU.mult))
                    v.link(dve.tensor_reduce(wa[:, c, n, :], prod[:, :].rearrange("p (h c) -> p h c", h=H),
                                             AX.X, ALU.add))
                heads = Wcat[:, c, 0:ROW].rearrange("p (h c) -> p h c", h=H)
                v.link(dve.tensor_copy(heads[:, :, 0:C], W_s[:, c, :].rearrange("p (h c) -> p h c", h=H)))
                v.link(dve.tensor_copy(heads[:, :, C], wa[:, c, 0, :]))
                dve.tensor_copy(Wcat[:, c, ROW:ROW + H], wa[:, c, 1, :]).then_inc(s_wcat, 1)

            def statistics_of(g, t):
                return dve.bn_stats(stat[:, t, :], X[:, bass.ds(g * TG + t, 1), :].rearrange("p a d -> p (a d)"))

            def moments(b, one):
                v.link(one)
                apart(dve)
                for t in range(TG):
                    one = dve.bn_aggr(mv[:, b, t, :], stat[:, t, :])
                one.then_inc(s_var, 1)

            def node_group(g, b, used, x_loaded):
                dve.wait_ge(s_sd, g + 1)
                v.link(dve.reciprocal(rs[:, b, :], sd[:, b, :]))
                at_least(dve, s_hst[b], 48 * used)
                for t in range(TG + 1):
                    if t < TG:
                        x_tile = X[:, bass.ds(g * TG + t, 1), :].rearrange("p a d -> p (a d)")
                        dve.tensor_scalar(xn_s[b][:, t, :], x_tile, mv[:, b, t, 0:1], rs[:, b, t:t + 1],
                                          ALU.subtract, ALU.mult).then_inc(s_xn, 1)
                    if t:
                        n = TG * g + t - 1
                        dve.wait_ge(s_xtp, n + 1)
                        at_least(dve, s_hp, n - 1)
                        odd = (b + t - 1) % 2
                        dve.tensor_copy(xnT[:, odd, :, :], (b0, b3)[odd][:, 0:D].rearrange("p (c e) -> p c e", c=2)
                                        ).then_inc(s_xt, 1)
                    if t < TG and x_loaded:
                        dve.wait_ge(*x_loaded)
                        one = statistics_of(g + 1, t)
                if x_loaded:
                    moments(1 - b, one)

            dve.wait_ge(s_x[0], 16)
            for t in range(TG):
                one = statistics_of(0, t)
            moments(0, one)
            for g in range(2):
                node_group(g, g, 0, (s_x[g + 1], 16))
            dve.wait_ge(s_row, 16)
            v.link(dve.tensor_scalar(less, found, thr_p[:, 0:1], None, ALU.is_lt))
            v.link(dve.tensor_reduce(cnt[:, :], less, AX.X, ALU.add))
            v.link(dve.scalar_tensor_tensor(out=wst[:, :], in0=rowno[:, :], scalar=float(EPP), in1=cnt[:, :],
                                            op0=ALU.mult, op1=ALU.add))
            dve.tensor_scalar(wst[:, :], wst[:, :], -1.0, None, ALU.add).then_inc(s_wst, 1)
            with dve.Fori(1, NTG // 2) as trip:
                v.enter(trip, 2 * 2)
                for b in range(2):
                    node_group(2 * trip + b, b, trip, (s_x[3], 16 * (NTG - 3)))
                v.leave(NTG // 2 - 1)
            dve.wait_ge(s_wcnt, 1)
            v.link(dve.tensor_scalar(nit_i[:, 0:1], b5[0:NW, 0:1], float(IE - 1), None, ALU.add))
            v.link(dve.tensor_scalar(nit_i[:, 1:2], nit_i[:, 0:1], IE.bit_length() - 1, None,
                                     ALU.arith_shift_right))
            dve.tensor_scalar(nit[:, :], nit_i[:, 1:2], 1.0, None, ALU.max).then_inc(s_nit, 1)
            dve.wait_ge(s_i0, 1)
            v.link(dve.tensor_copy(i0[:, :], b6[0:NW, 0:1]))
            v.link(dve.tensor_tensor(i1t[:, :], i0[:, :], nit[:, :], ALU.add))
            v.link(dve.tensor_tensor(i1[:, :], i1t[:, :], tailc[:, :], ALU.add))
            v.link(dve.tensor_scalar(ge[:, :], iota_i[:, :], i0[:, 0:1], None, ALU.is_ge))
            v.link(dve.scalar_tensor_tensor(out=oneh[:, :], in0=iota_i[:, :], scalar=i1[:, 0:1], in1=ge[:, :],
                                            op0=ALU.is_lt, op1=ALU.mult))
            v.link(dve.scalar_tensor_tensor(out=dcol[:, :], in0=i0[:, :], scalar=-float(IE), in1=wst[0:NW, :],
                                            op0=ALU.mult, op1=ALU.add))
            v.link(dve.tensor_scalar(i1t[:, :], i1[:, :], float(NI), -1.0, ALU.min, ALU.add))
            dve.tensor_scalar(diagl[:, :], ident[0:NW, 0:NW], i1t[:, 0:1], None, ALU.mult).then_inc(s_diagl, 1)
            node_group(NTG - 1, 0, NTG // 2, None)
            dve.wait_ge(s_lists, 1)
            v.link(dve.tensor_copy(winb[:, :], b4[:, 0:NI]))
            dve.tensor_copy(table[0:1, :, 1], winb[0:1, :])
            dve.scalar_tensor_tensor(out=table[0:1, :, 0], in0=iota_i[0:1, :], scalar=float(IE),
                                     in1=b5[0:1, 0:NI], op0=ALU.mult, op1=ALU.add).then_inc(s_items, 1)
            v.link(dve.memset(reset[:, 0:1], -BIG))
            v.link(dve.tensor_tensor(reset[:, 1:NI], winb[:, 1:NI], winb[:, 0:NI - 1], ALU.not_equal))
            v.link(dve.tensor_scalar(reset[:, 1:NI], reset[:, 1:NI], -BIG, None, ALU.mult))
            v.link(dve.tensor_scalar(sums_idx[:, :], b7[:, 0:NW], float(P), lane_p[:, 0:1], ALU.mult, ALU.add))


            def prepare(j, q, b):
                dve.wait_ge(s_cast, j + 1)
                dve.tensor_tensor(opens[:, :], erowf[:, P:2 * P + 1], erowf[:, P + 1:2 * P + 2],
                                  ALU.not_equal).then_inc(s_rend, 1)

            def place(j, q, b):
                dve.wait_ge(s_idxp, j + 1)
                dve.tensor_copy(gidx[:, b, :], idx_ps[:, 0, :]).then_inc(s_gidx, 1)
                items = bass.ds(GI * j, GI)
                dve.tensor_tensor(dloc[:, b, :].rearrange("p (i k) -> p i k", k=IT),
                                         idx_ps[:, 1, :].rearrange("p (i k) -> p i k", k=IT),
                                         winb[:, items].unsqueeze(2).to_broadcast([P, GI, IT]), ALU.subtract)

            def place_ends(j, q, b):
                dve.wait_ge(s_idxp, j + 1)
                dve.tensor_tensor(isend[:, b, :], end_ps, item_end[:, :], ALU.max).then_inc(s_prep, 1)

            def one_hot(j, q, b):
                dve.wait_ge(s_prep, j + 1)
                at_least(dve, s_pm, GI * (j - 2))
                dve.tensor_tensor(S16[:, b, :, :], dloc[:, b, :].unsqueeze(2).to_broadcast([P, GT, P]),
                                  lane16[:, :].unsqueeze(1).to_broadcast([P, GT, P]), ALU.is_equal).then_inc(s_S, 1)

            def scan(j, q, b):
                dve.wait_ge(s_gap, j + 1)
                dve.wait_ge(s_sT, j + 1)
                dve.tensor_tensor_scan(F[:, :], gap[:, b, :], b0[0:GI * H, :], -BIG, ALU.add, ALU.max).then_inc(s_scan, 1)

            def ends(j, q, b, between):
                part = lambda n: Fe16[:, :, n * H:(n + 1) * H]
                dve.wait_ge(s_FP, j + 1)
                dve.wait_ge(s_prep, j + 1)
                one = v.mark(dve.tensor_tensor(Fe[:, :, :].rearrange("p (i k) h -> p i k h", k=IT),
                                               back_ps.rearrange("p (k i h) -> p i k h", k=IT, i=GI),
                                               isend[:, b, :].rearrange("p (i k) -> p i k", k=IT).unsqueeze(3)
                                               .to_broadcast([P, GI, IT, H]), ALU.mult))
                dve.tensor_copy(Fe16[:, :, 3 * H], isend[:, b, :])
                v.need(one)
                one = v.mark(dve.tensor_copy(part(0), Fe[:, :, :]))
                between()
                v.need(one)
                v.link(dve.tensor_tensor(Fr[:, :, :], Fe[:, :, :], part(0), ALU.subtract))
                v.link(dve.tensor_copy(part(1), Fr[:, :, :]))
                dve.tensor_tensor(part(2), Fr[:, :, :], part(1), ALU.subtract).then_inc(s_Fe, 1)

            def shifts(j, q, b, between=lambda n: None):
                dve.wait_ge(s_mt, j + 1)
                dve.wait_ge(s_nld[b], GI * 16 * (q + 1))
                dve.tensor_scalar(t1[:, :], mt_ps[:, :, 3 * H], BIG, -BIG, ALU.mult, ALU.add)
                one = v.mark(dve.tensor_reduce(mi[:, :, :], mt_ps[:, :, 0:3 * H].rearrange("p i (n h) -> p i h n", n=3),
                                               AX.X, ALU.add))
                dve.tensor_copy(M[:, 0, :], M[:, GI, :])
                dve.tensor_copy(R[:, b, 0, H:2 * H], R[:, (b + 2) % 3, GI, H:2 * H])
                v.need(one)
                one = v.mark(dve.tensor_tensor(mi[:, :, :], mi[:, :, :],
                                               t1[:, :].unsqueeze(2).to_broadcast([P, GI, H]), ALU.add))
                for i in range(GI):
                    between(i)
                    v.need(one)
                    one = v.mark(dve.scalar_tensor_tensor(out=M[:, i + 1, :], in0=M[:, i, :],
                                                          scalar=reset[:, bass.ds(GI * j + i, 1)],
                                                          in1=mi[:, i, :], op0=ALU.add, op1=ALU.max))
                between(GI)
                v.need(one)
                one = v.mark(dve.tensor_tensor(xm[:, :, :], M[:, 1:GI + 1, :], R[:, b, 1:GI + 1, 0:H], ALU.add))
                between(GI + 1)
                v.need(one)
                dve.scalar_tensor_tensor(out=R[:, b, 1:GI + 1, H:2 * H], in0=xm[:, :, :], scalar=SLOPE,
                                         in1=xm[:, :, :], op0=ALU.mult, op1=ALU.max).then_inc(s_R, 1)
                between(GI + 2)
                dve.wait_ge(s_R, j + 1)
                dve.tensor_tensor(da[:, :, :], R[:, b, 0:GI, H:2 * H], R[:, b, 1:GI + 1, H:2 * H], ALU.subtract)
                one = v.mark(dve.tensor_copy(R16[:, :, 0, :], R[:, b, 1:GI + 1, :]))
                between(GI + 3)
                v.need(one)
                one = v.mark(dve.tensor_tensor(Rr[:, :, :], R[:, b, 1:GI + 1, :], R16[:, :, 0, :], ALU.subtract))
                dve.tensor_tensor(da[:, :, :], da[:, :, :],
                                  reset[:, bass.ds(GI * j, GI)].unsqueeze(2).to_broadcast([P, GI, H]),
                                  ALU.add).then_inc(s_da, 1)
                v.need(one)
                v.link(dve.tensor_copy(R16[:, :, 1, :], Rr[:, :, :]))
                dve.tensor_tensor(R16[:, :, 2, :], Rr[:, :, :], R16[:, :, 1, :], ALU.subtract).then_inc(s_R16, 1)
                between(GI + 4)

            def logits(j, q, b, between=lambda n: None):
                dve.wait_ge(s_ex, j + 1)
                a_src = G[:, b, :, :].rearrange("p t (h c) -> p t h c", h=H)[:, :, :, C]
                one = v.mark(dve.tensor_tensor(z[:, :, :], a_src, ex_ps[:, :, 0:H], ALU.add))
                between(0)
                v.need(one)
                one = v.mark(dve.scalar_tensor_tensor(out=lz[:, :, :], in0=z[:, :, :], scalar=SLOPE,
                                                      in1=z[:, :, :], op0=ALU.mult, op1=ALU.max))
                between(1)
                v.need(one)
                one = v.mark(dve.tensor_tensor(df[:, :, :], lz[:, :, :], ex_ps[:, :, H:2 * H], ALU.subtract))
                between(2)
                v.need(one)
                dve.tensor_scalar(df[:, :, :], df[:, :, :], 0.0, None, ALU.min).then_inc(s_df, 1)

            def message(j, q, b, i):
                dve.wait_ge(s_wt, j + 1)
                g = G[:, b, i:GT:GI, :].rearrange("p t (h c) -> p t h c", h=H)
                dve.tensor_tensor(g[:, :, :, 0:C], g[:, :, :, 0:C], g[:, :, :, C:HC].to_broadcast([P, IT, H, C]),
                                  ALU.mult).then_inc(s_msg, 1)

            def rescale(j, q, b, i):
                dve.wait_ge(s_alpha, j + 1)
                if i == 0:
                    at_least(dve, s_sums[b], 16 * q)
                at_least(dve, s_acc, GI * j + i)
                old = acc[:, (b + 2) % 3, GI - 1, :] if i == 0 else acc[:, b, i - 1, :]
                return v.mark(dve.tensor_tensor(scaled[:, :].rearrange("p (h c) -> p h c", h=H),
                                                old.rearrange("p (h c) -> p h c", h=H),
                                                alpha[:, b, i, :].unsqueeze(2).to_broadcast([P, H, HC]), ALU.mult))

            def add(j, q, b, i, one):
                v.need(one)
                dve.wait_ge(s_pm, GI * j + i + 1)
                dve.tensor_tensor(acc[:, b, i, :], scaled[:, :], sum_bank(i), ALU.add).then_inc(s_acc, 1)

            def accumulate(j, q, b, i):
                add(j, q, b, i, rescale(j, q, b, i))

            dve.tensor_copy(ident16[:, :], ident[:, :])
            dve.tensor_copy(spread16[:, :, :], spread[:, :, :])
            v.link(dve.tensor_copy(lane16[:, :], lane[:, :]))
            v.link(dve.memset(acc[:, 2, GI - 1, :], 0.0))
            v.link(dve.memset(M[:, GI, :], -BIG))
            v.link(dve.memset(R[:, 2, GI, H:2 * H], 0.0))
            for k in range(2):
                prepare(*turn(0, k))
                place(*turn(0, k))
                place_ends(*turn(0, k))
            rows_stored(dve)
            one_hot(*turn(0, 0))

            def body(trip, k, back=True, prep=True, ahead=True):
                now, ago, following = turn(trip, k), turn(trip, k - 1), turn(trip, k + 1)
                ends(*now, lambda: prep and prepare(*turn(trip, k + 2)))
                if ahead:
                    one_hot(*following)

                def places(n):
                    if prep and n < 2:
                        (place, place_ends)[n](*turn(trip, k + 2))

                if back:
                    logits(*ago, places)
                    message(*ago, 0)
                else:
                    places(0)
                    places(1)
                if back:
                    for i in range(1, GI):
                        message(*ago, i)
                marks = {}

                def old_sums(n):
                    if n == 2 * GI - 1:
                        if ahead:
                            scan(*following)
                    elif back and n == 2 * GI:
                        add(*ago, GI - 1, marks[GI - 1])
                    elif back and n % 2 == 0:
                        marks[n // 2] = rescale(*ago, n // 2)
                    elif back:
                        add(*ago, n // 2, marks[n // 2])

                shifts(*now, old_sums)

            scan(*turn(0, 0))
            body(0, 0, back=False)
            for k in (1, 2, 3):
                body(0, k)
            with dve.Fori(1, TRIPS) as trip:
                v.enter(trip, 3 * (4 + 10 + 3 + 4))
                for k in (1, 2, 3):
                    body(trip, k)
                v.leave(TRIPS - 1)
            for k in LAST_ONES:
                body(TRIPS, k, prep=k < LAST - 1, ahead=k < LAST)
            logits(*turn(TRIPS, LAST))
            for i in range(GI):
                message(*turn(TRIPS, LAST), i)
            for i in range(GI):
                accumulate(*turn(TRIPS, LAST), i)

            flat = lambda o: o.rearrange("p t d -> p (t d)")
            over_tiles = lambda n: VEC[:, n, :].unsqueeze(1).to_broadcast([P, TG, D])

            def attention_out(g, b):
                dve.wait_ge(s_xl, 32 * (g + 1))
                v.link(dve.tensor_tensor(XL[:, 1, :, :], XL[:, 1, :, :], over_tiles(0), ALU.add))
                dve.wait_ge(s_sm, 16 * TG * (g + 1))
                sm = SM[:, :, :].rearrange("p t (h c) -> p (t h) c", h=H)
                v.link(dve.tensor_scalar(den[:, :], sm[:, :, C], 1e-16, None, ALU.add))
                v.link(dve.reciprocal(rden[:, :], den[:, :]))
                at_least(dve, s_out[b], 16 * stored[b])
                dve.tensor_tensor(X1[:, b, :, :].rearrange("p t (h c) -> p (t h) c", h=H), sm[:, :, 0:C],
                                  rden[:, :].unsqueeze(2).to_broadcast([P, TG * H, C]), ALU.mult).then_inc(s_smfree, 1)
                dve.wait_ge(s_smfree, g + 1)
                v.link(dve.tensor_tensor(X1[:, b, :, :], X1[:, b, :, :], XL[:, 1, :, :], ALU.add))
                dve.tensor_scalar(XL[:, 1, :, :], X1[:, b, :, :], 0.0, None, ALU.min).then_inc(s_neg, 1)

            def statistics(b):
                for t in range(TG):
                    one = dve.bn_stats(st_s[:, t, :], X1[:, b, t, :])
                v.link(one)
                apart(dve)
                for t in range(TG):
                    one = dve.bn_aggr(st_m[:, t, :], st_s[:, t, :])
                return one

            def elu(g, b):
                dve.wait_ge(s_exp, g + 1)
                v.link(dve.scalar_tensor_tensor(out=flat(X1[:, b, :, :]), in0=flat(XL[:, 1, :, :]), scalar=-1.0,
                                                in1=flat(X1[:, b, :, :]), op0=ALU.add, op1=ALU.max))
                statistics(b).then_inc(s_var4, 1)

            def normalize(out, g, b, done):
                dve.wait_ge(s_sd4, done)
                v.link(dve.reciprocal(st_r[:, :], st_d[:, :]))
                for t in range(TG):
                    one = dve.tensor_scalar(out[:, t, :], X1[:, b, t, :], st_m[:, t, 0:1], st_r[:, t:t + 1],
                                            ALU.subtract, ALU.mult)
                return one

            def first_norm(g, b):
                v.link(normalize(X1[:, b, :, :], g, b, 2 * g + 1))
                v.link(dve.tensor_tensor(X1[:, b, :, :], X1[:, b, :, :], over_tiles(1), ALU.mult))
                v.link(dve.tensor_tensor(X1[:, b, :, :], X1[:, b, :, :], over_tiles(2), ALU.add))
                v.link(dve.tensor_tensor(X1[:, b, :, :], X1[:, b, :, :], XL[:, 0, :, :], ALU.add))
                statistics(b).then_inc(s_var4, 1)

            def second_norm(g, b):
                normalize(XL[:, 1, :, :], g, b, 2 * g + 2).then_inc(s_xn4, 1)

            def route(g, b):
                wide = lambda o, n: o.unsqueeze(2).to_broadcast([P, TG, n])
                dve.wait_ge(s_lg, g + 1)
                v.link(dve.tensor_tensor(lgs[:, :, :], lg_ps, RB2[:, :].unsqueeze(1).to_broadcast([P, TG, NX]), ALU.add))
                v.link(dve.tensor_reduce(lmx[:, :], lgs[:, :, :], AX.X, ALU.max))
                dve.tensor_tensor(lgs[:, :, :], lgs[:, :, :], wide(lmx[:, :], NX), ALU.subtract).then_inc(s_lsub, 1)
                dve.wait_ge(s_lexp, g + 1)
                v.link(dve.tensor_reduce(lsum[:, :], lgs[:, :, :], AX.X, ALU.add))
                v.link(dve.reciprocal(lrec[:, :], lsum[:, :]))
                v.link(dve.tensor_tensor(prob[:, :, 0:NX], lgs[:, :, :], wide(lrec[:, :], NX), ALU.mult))
                apart(dve)
                for t in range(TG):
                    one = dve.max(top[:, t, :], prob[:, t, :])
                v.link(one)
                apart(dve)
                for t in range(TG):
                    one = dve.max_index(topi[:, t, :], top[:, t, :], prob[:, t, :])
                v.link(one)
                dve.tensor_tensor(tdif[:, :], top[:, :, 1], top[:, :, 0], ALU.subtract).then_inc(s_tdif, 1)
                v.link(dve.tensor_copy(topf[:, :, :], topi[:, :, 0:2]))
                v.link(dve.tensor_tensor(c1[:, :, :], expert[:, :, :], wide(topf[:, :, 0], NX), ALU.is_equal))
                v.link(dve.tensor_tensor(c2[:, :, :], expert[:, :, :], wide(topf[:, :, 1], NX), ALU.is_equal))
                dve.wait_ge(s_tex, g + 1)
                v.link(dve.tensor_scalar(ten[:, :], tex[:, :], 1.0, None, ALU.add))
                v.link(dve.reciprocal(tw[:, 0, :], ten[:, :]))
                v.link(dve.tensor_tensor(tw[:, 1, :], tex[:, :], tw[:, 0, :], ALU.mult))
                v.link(dve.tensor_tensor(c1[:, :, :], c1[:, :, :], wide(tw[:, 0, :], NX), ALU.mult))
                v.link(dve.tensor_tensor(c2[:, :, :], c2[:, :, :], wide(tw[:, 1, :], NX), ALU.mult))
                dve.tensor_tensor(coef[:, :, :], c1[:, :, :], c2[:, :, :], ALU.add).then_inc(s_coef, 1)

            def coefficients_back(g):
                dve.wait_ge(s_cT, g + 1)
                dve.tensor_copy(coefT[:, 0:4 * P], b6[0:NX, :]).then_inc(s_coefT, 1)
                dve.tensor_copy(coefT[:, 4 * P:TOK], b7[0:NX, 0:(TG - 4) * P]).then_inc(s_coefT, 1)

            def expert_bias(g, b):
                for t in range(TG):
                    n = TG + t
                    dve.wait_ge(s_eo, NCOMB * g + n + 1)
                    dve.wait_ge(s_comb, NCOMB * g + t + 1)
                    dve.tensor_tensor(X1[:, b, t, :], X1[:, b, t, :], eo_bank(b, n), ALU.add).then_inc(s_comb, 1)

            def combine(g, b, e):
                for t in range(TG):
                    n = first_addend(e) + t
                    dve.wait_ge(s_eo, NCOMB * g + n + 1)
                    if e:
                        dve.wait_ge(s_comb, NCOMB * g + n - TG + 1)
                    dve.scalar_tensor_tensor(out=X1[:, b, t, :], in0=eo_bank(b, n), scalar=coef[:, t, e:e + 1],
                                             in1=X1[:, b, t, :], op0=ALU.mult, op1=ALU.add).then_inc(s_comb, 1)

            def node_body(g, b, ahead=True):
                parts = (attention_out, elu, first_norm, second_norm)
                route(g, b)
                coefficients_back(g)
                for e in range(NX):
                    combine(g, b, e)
                    if e == 0:
                        expert_bias(g, b)
                    if ahead and e < len(parts):
                        parts[e](g + 1, 1 - b)

            stored = [0, 0]
            dve.wait_ge(s_ew, 16 * 23)
            for part in (attention_out, elu, first_norm, second_norm):
                part(0, 0)
            for g in range(2):
                stored = [1, 0]
                node_body(g, g)
            with dve.Fori(1, (NTG - 1) // 2) as trip:
                v.enter(trip, 2 * 28)
                for b in range(2):
                    stored = [trip + 1, trip]
                    node_body(2 * trip + b, b)
                v.leave((NTG - 1) // 2 - 1)
            node_body(NTG - 1, 0, ahead=False)

        @block.scalar
        def _(act):
            def node_group(g, b, used):
                act.wait_ge(s_var, g + 1)
                nc.scalar.activation(sd[:, b, :], mv[:, b, :, 1], ACT.Sqrt, bias=eps[:, 0:1]).then_inc(s_sd, 1)
                at_least(act, s_hst[b], 48 * used)
                for t in range(TG):
                    act.wait_ge(s_hp, TG * g + t + 1)
                    nc.scalar.copy(hrow[b][:, t, :], (b1, b2)[(b + t) % 2][:, 0:ROW + H]).then_inc(s_hrow, 1)

            act.wait_ge(s_const, 16)
            for g in range(2):
                node_group(g, g, 0)
            with act.Fori(1, NTG // 2) as trip:
                for b in range(2):
                    node_group(2 * trip + b, b, trip)
            node_group(NTG - 1, 0, NTG // 2)

            def casts(j, q, b):
                act.wait_ge(s_eld[b], 2 * GI * 16 * (q + 1))
                at_least(act, s_idxp, j)
                nc.scalar.copy(erowf[:, :], erow[:, b, :]).then_inc(s_cast, 1)

            def gaps(j, q, b):
                act.wait_ge(s_idxp, j + 1)
                nc.scalar.copy(gap[:, b, :], gap_ps).then_inc(s_gap, 1)

            def st_copies(j, q, b):
                at_least(act, s_ex, j)
                for half in range(2):
                    act.wait_ge(s_stp, 2 * j + half + 1)
                    nc.scalar.copy(ST16[:, HG * half:HG * (half + 1), :].rearrange("p t e -> p (t e)"),
                                   st_ps[half]).then_inc(s_st, 1)

            def one_hot_32(j, q, b):
                act.wait_ge(s_S, j + 1)
                at_least(act, s_pm, GI * (j - 2))
                nc.scalar.copy(S[:, b, :, :], S16[:, b, :, :]).then_inc(s_S32, 1)

            def alphas(j, q, b):
                act.wait_ge(s_da, j + 1)
                nc.scalar.activation(alpha[:, b, :, :], da[:, :, :], ACT.Exp).then_inc(s_alpha, 1)

            def weights(j, q, b):
                act.wait_ge(s_df, j + 1)
                w = G[:, b, :, :].rearrange("p t (h c) -> p (t h) c", h=H)[:, :, C]
                nc.scalar.activation(w, df[:, :, :].rearrange("p t h -> p (t h)"), ACT.Exp).then_inc(s_wt, 1)

            def store_sums(j, q, b):
                act.wait_ge(s_acc, GI * (j + 1))
                act.dma_start(sums_d[bass.ds(GI * P * j, GI * P), :].rearrange("(i p) c -> p i c", p=P),
                              acc[:, b, :, :]).then_inc(s_sums[b], 16)

            for k in range(2):
                casts(*turn(0, k))
                gaps(*turn(0, k))
            rows_stored(act)

            def body(trip, k, back=2, prep=True):
                if prep:
                    casts(*turn(trip, k + 2))
                if back:
                    weights(*turn(trip, k - 1))
                if prep:
                    gaps(*turn(trip, k + 2))
                st_copies(*turn(trip, k))
                one_hot_32(*turn(trip, k))
                if back == 2:
                    store_sums(*turn(trip, k - 2))
                alphas(*turn(trip, k))

            for k in range(4):
                body(0, k, back=min(k, 2))
            with act.Fori(1, TRIPS) as trip:
                for k in (1, 2, 3):
                    body(trip, k)
            for k in LAST_ONES:
                body(TRIPS, k, prep=k < LAST - 1)
            weights(*turn(TRIPS, LAST))
            store_sums(*turn(TRIPS, LAST - 1))
            for i in range(GI):
                act.wait_ge(s_acc, GI * (NG - 1) + i + 1)
                act.dma_start(sums_d[P * (GI * (NG - 1) + i):P * (GI * (NG - 1) + i + 1), :],
                              acc[:, LAST % 3, i, :]).then_inc(s_sums[LAST % 3], 16)

            act.sem_inc(s_bank, 4)
            act.wait_ge(s_ew, 16 * 23)

            def negative_exp(g):
                act.wait_ge(s_neg, g + 1)
                nc.scalar.activation(XL[:, 1, :, :], XL[:, 1, :, :], ACT.Exp).then_inc(s_exp, 1)

            def deviation(done):
                act.wait_ge(s_var4, done)
                nc.scalar.activation(st_d[:, :], st_m[:, :, 1], ACT.Sqrt, bias=eps[:, 0:1]).then_inc(s_sd4, 1)

            def transposed(g, b):
                blocks = XT[:, b, :, :].rearrange("p c (t e) -> p (c t) e", e=P)
                for r in range(4):
                    n = min(4, 2 * TG - 4 * r)
                    act.wait_ge(s_tp4, 4 * g + r + 1)
                    nc.scalar.copy(blocks[:, 4 * r:4 * r + n, :], (b6, b7)[r % 2][:, 0:n * P]
                                   .rearrange("p (t e) -> p t e", e=P)).then_inc(s_xt4, 1)

            def layer(g, b, n, out, bias):
                act.wait_ge(s_lay, NLAY * g + n + 1)
                nc.scalar.activation(out, lay_bank(b, n), ACT.Relu, bias=bias).then_inc(s_bank, 1)

            def router(g, b):
                for hf in range(2):
                    layer(g, b, hf, rhT[:, hf * HT:(hf + 1) * HT], RB1[:, 0:1])

            def softmax_exp(g):
                act.wait_ge(s_lsub, g + 1)
                nc.scalar.activation(lgs[:, :, :], lgs[:, :, :], ACT.Exp).then_inc(s_lexp, 1)

            def top_exp(g):
                act.wait_ge(s_tdif, g + 1)
                nc.scalar.activation(tex[:, :], tdif[:, :], ACT.Exp).then_inc(s_tex, 1)

            def hidden(g, b, e, lay):
                out = (h1T, h2T)[lay]
                for m in range(2):
                    for hf in range(2):
                        layer(g, b, 2 + 8 * e + 4 * lay + 2 * m + hf, out[:, m, hf * HT:(hf + 1) * HT],
                              EB[:, lay, e, m:m + 1])

            def node_body(g, b, ahead=True):
                router(g, b)
                for e in range(NX):
                    hidden(g, b, e, 0)
                    if e == 0:
                        softmax_exp(g)
                    if ahead and e == 2:
                        negative_exp(g + 1)
                    if ahead and e in (3, 4):
                        deviation(2 * g + e)
                    if ahead and e == 5:
                        transposed(g + 1, 1 - b)
                    hidden(g, b, e, 1)
                    if e == 0:
                        top_exp(g)

            negative_exp(0)
            deviation(1)
            deviation(2)
            transposed(0, 0)
            for g in range(2):
                node_body(g, g)
            with act.Fori(1, (NTG - 1) // 2) as trip:
                for b in range(2):
                    node_body(2 * trip + b, b)
            node_body(NTG - 1, 0, ahead=False)

        @block.tensor
        def _(pe):
            pe.wait_ge(s_const, 16)
            pe.wait_ge(s_below, 1)
            pe.matmul(b4[0:NW + 1, 0:1], below[:, :], ones[:, 0:1], start=True, stop=True).then_inc(s_rowcnt, 1)
            def node_group(g, b):
                for t in range(TG + 1):
                    if t < TG:
                        n, odd = TG * g + t, (b + t) % 2
                        pe.wait_ge(s_xn, n + 1)
                        at_least(pe, s_xt, n - 1)
                        for c in range(2):
                            one = pe.transpose((b0, b3)[odd][:, c * P:(c + 1) * P],
                                               xn_s[b][:, t, c * P:(c + 1) * P], ident[:, :])
                        one.then_inc(s_xtp, 1)
                    if t:
                        n, odd = TG * g + t - 1, (b + t - 1) % 2
                        pe.wait_ge(s_xt, n + 1)
                        at_least(pe, s_hrow, n - 1)
                        for c in range(2):
                            one = pe.matmul((b1, b2)[odd][:, 0:ROW + H], xnT[:, odd, c, :], Wcat[:, c, :],
                                            start=(c == 0), stop=(c == 1))
                        one.then_inc(s_hp, 1)

            pe.wait_ge(s_wcat, 2)
            for g in range(2):
                node_group(g, g)
            with pe.Fori(1, NTG // 2) as trip:
                for b in range(2):
                    node_group(2 * trip + b, b)
            pe.wait_ge(s_wst, 1)
            pe.matmul(b5[0:NW, 0:1], diffm[:, :], wst[:, :], start=True, stop=True).then_inc(s_wcnt, 1)
            pe.wait_ge(s_nit, 1)
            pe.matmul(b6[0:NW, 0:1], before[:, :], nit[:, :], start=True, stop=True).then_inc(s_i0, 1)
            node_group(NTG - 1, 0)
            pe.wait_ge(s_diagl, 1)
            pe.matmul(b4[:, 0:NI], w128[:, :], oneh[:, :], start=True, stop=True)
            pe.matmul(b5[0:1, 0:NI], dcol[:, :], oneh[:, :], start=True, stop=True)
            pe.matmul(b7[:, 0:NW], ones[0:NW, :], diagl[:, :], start=True, stop=True).then_inc(s_lists, 1)
            pe.wait_ge(s_hrow, NW)

            def prepare(j, q, b):
                pe.wait_ge(s_cast, j + 1)
                at_least(pe, s_prep, j)
                pe.wait_ge(s_rend, j + 1)
                at_least(pe, s_gap, j)
                apart(pe)
                for k in range(IT):
                    pe.matmul(gap_ps[:, k * P:(k + 1) * P], spread16[:, k, :], opens[:, 0:P],
                              start=True, stop=True)
                for n, o in ((0, erowf[:, 0:P]), (1, erowf[:, P + 1:2 * P + 1])):
                    pe.transpose(idx_ps[:, n, :], o, ident[0:GT, 0:GT])
                pe.transpose(end_ps, opens[:, 1:P + 1], ident16[0:GT, 0:GT]).then_inc(s_idxp, 1)

            def transpose_one_hot(j, q, b):
                pe.wait_ge(s_S, j + 1)
                at_least(pe, s_st, 2 * j)
                for half in range(2):
                    for t in range(HG):
                        last_ = pe.transpose(st_ps[half][:, t * P:(t + 1) * P], S16[:, b, HG * half + t, :],
                                             ident16[:, :])
                    last_.then_inc(s_stp, 1)

            def a_src_rows(j, q, b):
                pe.wait_ge(s_gath[b], GT * 16 * (q + 1))
                at_least(pe, s_scan, j)
                a_src = G[:, b, :, :].rearrange("p t (h c) -> p (t h) c", h=H)[:, :, C]
                for k in range(IT):
                    last_ = pe.transpose(b0[0:GI * H, k * P:(k + 1) * P],
                                         a_src[:, k * GI * H:(k + 1) * GI * H], ident[:, :])
                last_.then_inc(s_sT, 1)

            def maxima_back(j, q, b):
                pe.wait_ge(s_scan, j + 1)
                at_least(pe, s_Fe, j)
                apart(pe)
                for k in range(IT):
                    last_ = pe.transpose(back_ps[:, k * GI * H:(k + 1) * GI * H], F[:, k * P:(k + 1) * P],
                                         ident[0:GI * H, 0:GI * H])
                last_.then_inc(s_FP, 1)

            def node_maxima(j, q, b):
                pe.wait_ge(s_S, j + 1)
                pe.wait_ge(s_Fe, j + 1)
                at_least(pe, s_R, j)
                for i in range(GI):
                    for k in range(IT):
                        last_ = pe.matmul(mt_ps[:, i, :], S16[:, b, IT * i + k, :], Fe16[:, IT * i + k, :],
                                          start=(k == 0), stop=(k == IT - 1))
                last_.then_inc(s_mt, 1)

            def expand(j, q, b):
                pe.wait_ge(s_st, 2 * (j + 1))
                pe.wait_ge(s_R16, j + 1)
                at_least(pe, s_df, j)
                for t in range(GT):
                    for n in range(3):
                        last_ = pe.matmul(ex_ps[:, slot(t // IT, t % IT), :], ST16[:, t, :], R16[:, t // IT, n, :],
                                          start=(n == 0), stop=(n == 2))
                last_.then_inc(s_ex, 1)

            def sum_item(j, q, b, i):
                pe.wait_ge(s_S32, j + 1)
                pe.wait_ge(s_msg, GI * j + i + 1)
                at_least(pe, s_acc, GI * j + i - 1)
                for k in range(IT):
                    last_ = pe.matmul(sum_bank(i), S[:, b, IT * i + k, :], G[:, b, slot(i, k), :],
                                      start=(k == 0), stop=(k == IT - 1))
                last_.then_inc(s_pm, 1)

            prepare(*turn(0, 0))
            prepare(*turn(0, 1))

            a_src_rows(*turn(0, 0))

            def body(trip, k, back=True, prep=True, ahead=True):
                now, ago = turn(trip, k), turn(trip, k - 1)
                maxima_back(*now)
                if back:
                    expand(*ago)
                node_maxima(*now)
                if prep:
                    prepare(*turn(trip, k + 2))
                transpose_one_hot(*now)
                if back:
                    for i in range(GI - 1):
                        sum_item(*ago, i)
                if ahead:
                    a_src_rows(*turn(trip, k + 1))
                if back:
                    sum_item(*ago, GI - 1)

            body(0, 0, back=False)
            for k in (1, 2, 3):
                body(0, k)
            with pe.Fori(1, TRIPS) as trip:
                for k in (1, 2, 3):
                    body(trip, k)
            for k in LAST_ONES:
                body(TRIPS, k, prep=k < LAST - 1, ahead=k < LAST)
            expand(*turn(TRIPS, LAST))
            for i in range(GI):
                sum_item(*turn(TRIPS, LAST), i)

            pe.wait_ge(s_ew, 16 * 23)
            pe.wait_ge(s_acc, GI * NG)

            def transposes(g, b):
                pe.wait_ge(s_xn4, g + 1)
                for r in range(4):
                    at_least(pe, s_xt4, 4 * g + r - 1)
                    for n in range(4 * r, min(4 * r + 4, 2 * TG)):
                        c, t = n // TG, n % TG
                        one = pe.transpose((b6, b7)[r % 2][:, (n % 4) * P:(n % 4 + 1) * P],
                                           XL[:, 1, t, c * P:(c + 1) * P], ident[:, :])
                    one.then_inc(s_tp4, 1)

            def layer(g, b, n, weights, x, hf):
                pe.wait_ge(s_bank, NLAY * g + n + 1)
                for c in range(2):
                    one = pe.matmul(lay_bank(b, n), weights(c), x[:, c, hf * HT:(hf + 1) * HT],
                                    start=(c == 0), stop=(c == 1))
                one.then_inc(s_lay, 1)

            def router(g, b):
                pe.wait_ge(s_xt4, 4 * (g + 1))
                for hf in range(2):
                    layer(g, b, hf, lambda c: RW1[:, c, :], XT[:, b, :, :], hf)

            def router_logits(g):
                pe.wait_ge(s_bank, NLAY * g + 2 + 4)
                for t in range(TG):
                    one = pe.matmul(lg_ps[:, t, :], rhT[:, t * P:(t + 1) * P], RW2[:, :], start=True, stop=True)
                one.then_inc(s_lg, 1)

            def hidden(g, b, e, lay):
                w, x = ((EW1, XT[:, b, :, :]), (EW2, h1T))[lay]
                if lay:
                    pe.wait_ge(s_bank, NLAY * g + 2 + 8 * e + 4 + 4)
                for m in range(2):
                    for hf in range(2):
                        layer(g, b, 2 + 8 * e + 4 * lay + 2 * m + hf,
                              lambda c: w[:, e, c, m * P:(m + 1) * P], x, hf)

            def to_add(g, b, n, pairs):
                at_least(pe, s_comb, NCOMB * g + max(n - 1, 0))
                for k, (l, r) in enumerate(pairs):
                    one = pe.matmul(eo_bank(b, n), l, r, start=(k == 0), stop=(k == len(pairs) - 1))
                one.then_inc(s_eo, 1)

            def transpose_coefficients(g):
                pe.wait_ge(s_coef, g + 1)
                for t in range(TG):
                    one = pe.transpose((b6, b7)[t // 4][0:NX, (t % 4) * P:(t % 4 + 1) * P], coef[:, t, :], ident[:, :])
                one.then_inc(s_cT, 1)

            def expert_bias(g, b):
                pe.wait_ge(s_coefT, 2 * (g + 1))
                for t in range(TG):
                    to_add(g, b, TG + t, [(coefT[:, t * P:(t + 1) * P], EB3[:, :])])

            def expert_out(g, b, e):
                pe.wait_ge(s_bank, NLAY * g + 2 + 8 * (e + 1) + 4)
                for t in range(TG):
                    to_add(g, b, first_addend(e) + t,
                           [(h2T[:, c, t * P:(t + 1) * P], EW3[:, e, c, :]) for c in range(2)])

            def node_body(g, b, ahead=True):
                router(g, b)
                hidden(g, b, 0, 0)
                router_logits(g)
                hidden(g, b, 0, 1)
                for e in range(1, NX):
                    hidden(g, b, e, 0)
                    if e == 1:
                        transpose_coefficients(g)
                    expert_out(g, b, e - 1)
                    if e == 1:
                        expert_bias(g, b)
                    if ahead and e == 5:
                        transposes(g + 1, 1 - b)
                    hidden(g, b, e, 1)
                expert_out(g, b, NX - 1)

            transposes(0, 0)
            for g in range(2):
                node_body(g, g)
            with pe.Fori(1, (NTG - 1) // 2) as trip:
                for b in range(2):
                    node_body(2 * trip + b, b)
            node_body(NTG - 1, 0, ahead=False)


_IN = {'W': 'L0_gnn_W', 'att_src': 'L0_gnn_att_src', 'att_dst': 'L0_gnn_att_dst', 'bias': 'L0_gnn_bias',
       'ln_scale': 'L0_gnn_ln_scale', 'ln_bias': 'L0_gnn_ln_bias', 'rw1': 'L0_ffn_router_w1',
       'rb1': 'L0_ffn_router_b1', 'rw2': 'L0_ffn_router_w2', 'rb2': 'L0_ffn_router_b2',
       'ew1': 'L0_ffn_expert_w1', 'eb1': 'L0_ffn_expert_b1', 'ew2': 'L0_ffn_expert_w2',
       'eb2': 'L0_ffn_expert_b2', 'ew3': 'L0_ffn_expert_w3', 'eb3': 'L0_ffn_expert_b3'}


def kernel(**inputs):
    import numpy as np
    import concourse.bacc as bacc
    from concourse.bass_utils import run_bass_kernel_spmd

    x = np.zeros((NPAD, D), np.float32)
    x[:N] = inputs['x']
    src = np.zeros((LE,), np.int32)
    src[:NE] = inputs['src']
    dst = np.full((LE + 2,), NPAD, np.int32)
    dst[0] = -1
    dst[1:NE + 1] = inputs['dst']
    given = {'x': x, 'src': src, 'dst': dst}
    for name, full in _IN.items():
        given[name] = np.ascontiguousarray(inputs[full])

    nc = bacc.Bacc("TRN2", target_bir_lowering=False, num_devices=1)
    io = {name: nc.dram_tensor(f"in_{name}", a.shape, mybir.dt.from_np(a.dtype), kind="ExternalInput").ap()
          for name, a in given.items()}
    io['out'] = nc.dram_tensor("out_x", (N, D), F32, kind="ExternalOutput").ap()
    build(nc, io)
    r = run_bass_kernel_spmd(nc, [{f"in_{name}": a for name, a in given.items()}], core_ids=[0])
    return r.results[0]["out_x"]
```
